# Optimizing a Trainium2 kernel written in Bass

```python
import numpy as np
import jax
import jax.numpy as jnp

def _softmax(x, axis=-1):
    return jax.nn.softmax(x, axis=axis)

def _gelu(x):
    return jax.nn.gelu(x, approximate=True)

def _silu(x):
    return jax.nn.silu(x)

def _sigmoid(x):
    return jax.nn.sigmoid(x)

def _layernorm(x, axis=-1, eps=1e-05):
    m = jnp.mean(x, axis=axis, keepdims=True)
    v = jnp.var(x, axis=axis, keepdims=True)
    return (x - m) / jnp.sqrt(v + eps)

def _scatter_add(tgt, idx, src, axis=0):
    return tgt.at[idx].add(src)

def _segment_sum(src, seg, n):
    return jax.ops.segment_sum(src, seg, n)
kernel_name = 'mk_decoder_postln_d1_seqx_r8_6ca796'

def setup_inputs(seed: int=0):
    np.random.seed(seed)
    _w = jnp.asarray

    def _rec_inputs():
        import jax
        import jax.numpy as jnp
        _rk = jax.random.key(seed)
        x = 0.0003765 + 1 * jax.random.normal(jax.random.fold_in(_rk, 1), (32, 128, 128), jnp.float32)
        _lenS = 128 - jax.random.randint(jax.random.fold_in(_rk, 7), (32,), 0, max(1, 128 // 4) + 1, jnp.int32)
        _lenS2 = 128 - jax.random.randint(jax.random.fold_in(_rk, 8), (32,), 0, max(1, 128 // 4) + 1, jnp.int32)
        _ctx_1024P = jax.random.normal(jax.random.fold_in(_rk, 11), (32, 16, 128), jnp.float32)
        _ctx_1024c = jax.random.dirichlet(jax.random.fold_in(_rk, 511), 0.3 * jnp.ones((16,), jnp.float32), (32, 128))
        _ctx_1024t = jnp.einsum('bsk,bkd->bsd', _ctx_1024c, _ctx_1024P)
        _ctx_1024t = _ctx_1024t * jax.lax.rsqrt(jnp.mean(jnp.square(_ctx_1024t)) + 1e-12) * 0.953939
        ctx_1024 = -0.000292821 + 1.00034 * (_ctx_1024t + 0.3 * jax.random.normal(jax.random.fold_in(_rk, 611), (32, 128, 128), jnp.float32))
        _validS = jnp.arange(128)[None, :] < _lenS[:, None]
        _validS2 = jnp.arange(128)[None, :] < _lenS2[:, None]
        _causal = jnp.tril(jnp.ones((128, 128), dtype=bool))
        mask_BxS2_bf0 = jnp.logical_not(jnp.ones((32, 128), dtype=bool))
        return (x, ctx_1024, mask_BxS2_bf0)
    x, ctx_1024, mask_BxS2_bf0 = _rec_inputs()

    def _L0_attn_setup():
        import jax, jax.numpy as jnp
        import numpy as np
        EPS = 1e-05
        N_HEADS = 16

        def _rmsnorm(x):
            return x * jax.lax.rsqrt(jnp.mean(x * x, axis=-1, keepdims=True) + 1e-06)

        def _act_quant(x):
            s = 127.0 / jnp.clip(jnp.max(jnp.abs(x), axis=-1, keepdims=True), EPS)
            xq = jnp.clip(jnp.round(x * s), -128, 127) / s
            return x + jax.lax.stop_gradient(xq - x)

        def _weight_quant(w):
            s = 1.0 / jnp.clip(jnp.mean(jnp.abs(w)), EPS)
            wq = jnp.clip(jnp.round(w * s), -1, 1) / s
            return w + jax.lax.stop_gradient(wq - w)

        def bitlinear(x, w):
            xq = _act_quant(_rmsnorm(x))
            wq = _weight_quant(w)
            return jnp.einsum('bsd,ed->bse', xq, wq)
        key = jax.random.key(seed)
        kx, kq, kk, kv, ko = jax.random.split(key, 5)
        B, S, D = (2, 512, 128)
        return {'x': jax.random.normal(kx, (B, S, D), dtype=jnp.float32), 'wq': jax.random.normal(kq, (D, D), dtype=jnp.float32) * 0.02, 'wk': jax.random.normal(kk, (D, D), dtype=jnp.float32) * 0.02, 'wv': jax.random.normal(kv, (D, D), dtype=jnp.float32) * 0.02, 'wo': jax.random.normal(ko, (D, D), dtype=jnp.float32) * 0.02}
    _L0_attn_all = _L0_attn_setup()
    _L0_attn_in = {k: v for k, v in _L0_attn_all.items() if k in ('wq', 'wk', 'wv', 'wo')}
    del _L0_attn_all

    def _L0_xattn_setup():
        import jax, jax.numpy as jnp
        import numpy as np
        NUM_HEADS = 16
        key = jax.random.key(seed)
        ks = jax.random.split(key, 8)
        B, S, D = (2, 256, 128)
        scale = 1.0 / np.sqrt(D)
        return {'v': jax.random.normal(ks[0], (B, S, D), jnp.float32), 'k': jax.random.normal(ks[1], (B, S, D), jnp.float32), 'q': jax.random.normal(ks[2], (B, S, D), jnp.float32), 'mask': jnp.zeros((B, S), dtype=bool), 'Wq': jax.random.normal(ks[3], (D, D), jnp.float32) * scale, 'bq': jnp.zeros((D,), jnp.float32), 'Wk': jax.random.normal(ks[4], (D, D), jnp.float32) * scale, 'bk': jnp.zeros((D,), jnp.float32), 'Wv': jax.random.normal(ks[5], (D, D), jnp.float32) * scale, 'bv': jnp.zeros((D,), jnp.float32)}
    _L0_xattn_all = _L0_xattn_setup()
    _L0_xattn_in = {k: v for k, v in _L0_xattn_all.items() if k in ('Wq', 'bq', 'Wk', 'bk', 'Wv', 'bv')}
    del _L0_xattn_all

    def _L0_ffn_setup():
        import jax, jax.numpy as jnp
        import numpy as np
        B, S, D, F, E = (2, 256, 128, 512, 8)
        LN_EPS = 1e-05

        def _layer_norm(x, gamma, beta):
            mu = jnp.mean(x, axis=-1, keepdims=True)
            var = jnp.mean(jnp.square(x - mu), axis=-1, keepdims=True)
            return (x - mu) * jax.lax.rsqrt(var + LN_EPS) * gamma + beta
        key = jax.random.key(seed)
        ks = jax.random.split(key, 8)

        def xavier(k, shape):
            fan_in, fan_out = (shape[-1], shape[-2])
            a = jnp.sqrt(6.0 / (fan_in + fan_out))
            return jax.random.uniform(k, shape, jnp.float32, -a, a)
        return {'tgt': jax.random.normal(ks[0], (B, S, D), jnp.float32), 'Wr': xavier(ks[1], (E, D)), 'br': jnp.zeros((E,), jnp.float32), 'W1': xavier(ks[2], (E, F, D)), 'b1': jnp.zeros((E, F), jnp.float32), 'W2': xavier(ks[3], (E, D, F)), 'b2': jnp.zeros((E, D), jnp.float32), 'gamma': jnp.ones((D,), jnp.float32), 'beta': jnp.zeros((D,), jnp.float32)}
    _L0_ffn_all = _L0_ffn_setup()
    _L0_ffn_in = {k: v for k, v in _L0_ffn_all.items() if k in ('Wr', 'br', 'W1', 'b1', 'W2', 'b2', 'gamma', 'beta')}
    del _L0_ffn_all
    return {'x': x, 'ctx_1024': ctx_1024, 'mask_BxS2_bf0': mask_BxS2_bf0, 'L0_attn_wq': _L0_attn_in['wq'], 'L0_attn_wk': _L0_attn_in['wk'], 'L0_attn_wv': _L0_attn_in['wv'], 'L0_attn_wo': _L0_attn_in['wo'], 'L0_xattn_Wq': _L0_xattn_in['Wq'], 'L0_xattn_bq': _L0_xattn_in['bq'], 'L0_xattn_Wk': _L0_xattn_in['Wk'], 'L0_xattn_bk': _L0_xattn_in['bk'], 'L0_xattn_Wv': _L0_xattn_in['Wv'], 'L0_xattn_bv': _L0_xattn_in['bv'], 'L0_ffn_Wr': _L0_ffn_in['Wr'], 'L0_ffn_br': _L0_ffn_in['br'], 'L0_ffn_W1': _L0_ffn_in['W1'], 'L0_ffn_b1': _L0_ffn_in['b1'], 'L0_ffn_W2': _L0_ffn_in['W2'], 'L0_ffn_b2': _L0_ffn_in['b2'], 'L0_ffn_gamma': _L0_ffn_in['gamma'], 'L0_ffn_beta': _L0_ffn_in['beta']}

def reference(x, ctx_1024, mask_BxS2_bf0, L0_attn_wq, L0_attn_wk, L0_attn_wv, L0_attn_wo, L0_xattn_Wq, L0_xattn_bq, L0_xattn_Wk, L0_xattn_bk, L0_xattn_Wv, L0_xattn_bv, L0_ffn_Wr, L0_ffn_br, L0_ffn_W1, L0_ffn_b1, L0_ffn_W2, L0_ffn_b2, L0_ffn_gamma, L0_ffn_beta):
    import jax
    import jax.numpy as jnp

    def _L0_attn_ref(x, wq, wk, wv, wo):
        import jax, jax.numpy as jnp
        import numpy as np
        EPS = 1e-05
        N_HEADS = 16

        def _rmsnorm(x):
            return x * jax.lax.rsqrt(jnp.mean(x * x, axis=-1, keepdims=True) + 1e-06)

        def _act_quant(x):
            s = 127.0 / jnp.clip(jnp.max(jnp.abs(x), axis=-1, keepdims=True), EPS)
            xq = jnp.clip(jnp.round(x * s), -128, 127) / s
            return x + jax.lax.stop_gradient(xq - x)

        def _weight_quant(w):
            s = 1.0 / jnp.clip(jnp.mean(jnp.abs(w)), EPS)
            wq = jnp.clip(jnp.round(w * s), -1, 1) / s
            return w + jax.lax.stop_gradient(wq - w)

        def bitlinear(x, w):
            xq = _act_quant(_rmsnorm(x))
            wq = _weight_quant(w)
            return jnp.einsum('bsd,ed->bse', xq, wq)
        B, S, D = x.shape
        H = N_HEADS
        Dh = D // H
        q = bitlinear(x, wq).reshape(B, S, H, Dh)
        k = bitlinear(x, wk).reshape(B, S, H, Dh)
        v = bitlinear(x, wv).reshape(B, S, H, Dh)
        scores = jnp.einsum('bshd,bstd->bsht', q, k) / Dh ** 0.5
        attn = jax.nn.softmax(scores, axis=-1)
        ctx = jnp.einsum('bsht,bstd->bshd', attn, v)
        ctx = jnp.swapaxes(ctx, 1, 2).reshape(B, S, D)
        return bitlinear(ctx, wo)

    def _L0_xattn_ref(v, k, q, mask, Wq, bq, Wk, bk, Wv, bv):
        import jax, jax.numpy as jnp
        import numpy as np
        NUM_HEADS = 16
        B, Sq, D = q.shape
        H = NUM_HEADS
        hd = D // H

        def proj(x, W, b):
            y = jnp.einsum('bsd,ed->bse', x, W) + b
            return y.reshape(B, -1, H, hd).transpose(0, 2, 1, 3)
        qh = proj(q, Wq, bq)
        kh = proj(k, Wk, bk)
        vh = proj(v, Wv, bv)
        scores = jnp.einsum('bhqd,bhkd->bhqk', qh, kh) / jnp.sqrt(jnp.asarray(hd, jnp.float32))
        m = mask[:, None, None, :]
        scores = jnp.where(m, -jnp.inf, scores)
        w = jax.nn.softmax(scores, axis=-1)
        w = jnp.where(m, 0.0, w)
        out = jnp.einsum('bhqk,bhkd->bhqd', w, vh)
        return out.transpose(0, 2, 1, 3).reshape(B, Sq, D)

    def _L0_ffn_ref(tgt, Wr, br, W1, b1, W2, b2, gamma, beta):
        import jax, jax.numpy as jnp
        import numpy as np
        B, S, D, F, E = (2, 256, 128, 512, 8)
        LN_EPS = 1e-05

        def _layer_norm(x, gamma, beta):
            mu = jnp.mean(x, axis=-1, keepdims=True)
            var = jnp.mean(jnp.square(x - mu), axis=-1, keepdims=True)
            return (x - mu) * jax.lax.rsqrt(var + LN_EPS) * gamma + beta
        logits = jnp.einsum('bsd,ed->bse', tgt, Wr) + br
        top_v, top_i = jax.lax.top_k(logits, 2)
        top_w = jax.nn.softmax(top_v, axis=-1)
        n_exp = logits.shape[-1]
        router_w = jnp.sum(jax.nn.one_hot(top_i, n_exp, dtype=top_w.dtype) * top_w[..., None], axis=-2)
        h = jnp.einsum('bsd,efd->bsef', tgt, W1) + b1
        h = jax.nn.relu(h)
        o = jnp.einsum('bsef,edf->bsed', h, W2) + b2
        tgt2 = jnp.einsum('bsed,bse->bsd', o, router_w)
        return _layer_norm(tgt + tgt2, gamma, beta)
    x = _layernorm(x + _L0_attn_ref(x, L0_attn_wq, L0_attn_wk, L0_attn_wv, L0_attn_wo), axis=-1)
    x = _layernorm(x + _L0_xattn_ref(ctx_1024, ctx_1024, x, mask_BxS2_bf0, L0_xattn_Wq, L0_xattn_bq, L0_xattn_Wk, L0_xattn_bk, L0_xattn_Wv, L0_xattn_bv), axis=-1)
    x = _layernorm(x + _L0_ffn_ref(x, L0_ffn_Wr, L0_ffn_br, L0_ffn_W1, L0_ffn_b1, L0_ffn_W2, L0_ffn_b2, L0_ffn_gamma, L0_ffn_beta), axis=-1)
    return x

_drawn_inputs = setup_inputs


def setup_inputs(seed=0):
    import zlib

    import numpy as np

    out = dict(_drawn_inputs(seed))
    spreads = {'L0_xattn_bq': (0.0, 0.271),
     'L0_xattn_bk': (0.0, 2.0),
     'L0_xattn_bv': (0.0, 0.1),
     'L0_ffn_br': (0.0, 0.1),
     'L0_ffn_b1': (0.0, 0.1),
     'L0_ffn_b2': (0.0, 0.1),
     'L0_ffn_gamma': (1.0, 0.2),
     'L0_ffn_beta': (0.0, 0.1)}
    factors = {'L0_attn_wq': 6.594, 'L0_attn_wk': 7.563}
    for name, (base, spread) in spreads.items():
        noise = np.random.default_rng([zlib.crc32(name.encode()), seed]).standard_normal(out[name].shape)
        drawn = base * np.exp(spread * noise) if base else spread * noise
        out[name] = jnp.asarray(drawn.astype(out[name].dtype))
    for name, factor in factors.items():
        out[name] = (out[name] * factor).astype(out[name].dtype)
    return out
```

```python
from contextlib import ExitStack

import concourse.bass as bass
from concourse import mybir


def decoder_layer(nc, x, ctx_1024, mask, wq, wk, wv, wo, Wq, bq, Wk, bk, Wv, bv,
                  Wr, br, W1, b1, W2, b2, gamma, beta, out):
    F32, BF16, U8, U32 = mybir.dt.float32, mybir.dt.bfloat16, mybir.dt.uint8, mybir.dt.uint32
    ALU, ACT, AX = mybir.AluOpType, mybir.ActivationFunctionType, mybir.AxisListType

    B, P, D = x.shape
    H, HD = 16, D // 16
    E, F = W1.shape[0], W1.shape[1]
    FC = F // P
    TB = 4
    T = B // TB
    NT = TB * P
    HS = 32
    HG = D // HS
    NEG = -1e30
    ROUND = 1.5 * 2.0 ** 23
    A_STEPS, B_STEPS, C_STEPS = 86, 64, 49
    CREDIT = 8

    ctx = ExitStack()
    with ctx:
        def sb(name, shape, dt=F32):
            return ctx.enter_context(nc.sbuf_tensor(name, shape, dt))

        counters = []

        def sem(name):
            s = ctx.enter_context(nc.semaphore(name))
            counters.append(s)
            return s

        def after(eng, s, n):
            eng.wait_ge(s, n + CREDIT)

        def after_dma(eng, s, n):
            eng.wait_ge(s, 16 * (n + CREDIT))

        class Chain:

            def __init__(self, eng, s):
                self.eng, self.s, self.n, self.turn = eng, s, 0, 0

            def __call__(self, instruction):
                instruction.then_inc(self.s, 1)
                self.n += 1

            def settle(self):
                self.eng.wait_ge(self.s, self.n + self.turn)

        X = sb("X", [P, B, D])
        Y = sb("Y", [P, B, D])
        w_raw = sb("w_raw", [P, 4, D])
        w_abs = sb("w_abs", [P, 4])
        w_mean = sb("w_mean", [P, 4])
        w_inv = sb("w_inv", [P, 4])
        w_t = sb("w_t", [P, 4, D])
        w_int = sb("w_int", [P, 4, D], BF16)
        w_intT = sb("w_intT", [P, 4, D], BF16)
        W_raw = sb("W_raw", [P, 3, D])
        W_T = sb("W_T", [P, 3, D])
        b_qkv = sb("b_qkv", [P, 3, D])
        gam = sb("gam", [P, D])
        bet = sb("bet", [P, D])
        W1_raw = sb("W1_raw", [P, E * FC, D])
        b1_rows = sb("b1_rows", [E * FC, P])
        W1_T = sb("W1_T", [P, E * FC, P])
        W2_raw = sb("W2_raw", [P, E, F])
        W2_T = sb("W2_T", [P, E * FC, D])
        Wr_raw = sb("Wr_raw", [E, D])
        br_col = sb("br_col", [E, 1])
        Wr_T = sb("Wr_T", [P, E])
        b2_rep = sb("b2_rep", [3 * E, D])
        b2_rest = sb("b2_rest", [3 * E, 2, D])
        b2_parts = sb("b2_parts", [3 * E, 3, D], BF16)
        ident = sb("ident", [P, P])
        ident16 = sb("ident16", [P, P], BF16)
        ones = sb("ones", [P, P])
        sel = sb("sel", [3 * E, E, P], BF16)
        diag = sb("diag", [3 * E, 3, E])
        half = sb("half", [P, B])
        mask8 = sb("mask8", [B, P], U8)
        mask_f = sb("mask_f", [B, P])
        mask_neg = sb("mask_neg", [P, B])
        spare = sb("spare", [P, 1])
        eiota = sb("eiota", [P, TB, E])

        PS = ctx.enter_context(nc.psum_tensor("PS", [P, 8, 512], F32))

        x_in = ctx.enter_context(nc.semaphore("x_in"))
        w_in = ctx.enter_context(nc.semaphore("w_in"))
        xw_in = ctx.enter_context(nc.semaphore("xw_in"))
        ffn_in = ctx.enter_context(nc.semaphore("ffn_in"))
        out_done = ctx.enter_context(nc.semaphore("out_done"))
        consts = ctx.enter_context(nc.semaphore("consts"))
        prep_pe = ctx.enter_context(nc.semaphore("prep_pe"))
        prep_dve = ctx.enter_context(nc.semaphore("prep_dve"))
        prep_act = ctx.enter_context(nc.semaphore("prep_act"))
        prep_pool = ctx.enter_context(nc.semaphore("prep_pool"))
        b1_psum = ctx.enter_context(nc.semaphore("b1_psum"))
        dve_chain = ctx.enter_context(nc.semaphore("dve_chain"))
        act_chain = ctx.enter_context(nc.semaphore("act_chain"))
        pool_chain = ctx.enter_context(nc.semaphore("pool_chain"))

        sq_all = Y
        ssq1 = sb("ssq1", [P, B])
        amax1 = sb("amax1", [P, B])
        rms1 = sb("rms1", [P, B])
        clip1 = sb("clip1", [P, B])
        rec1 = sb("rec1", [P, B])
        s1 = sb("s1", [P, B])
        inv1 = sb("inv1", [P, B])
        inv1sq = sb("inv1sq", [P, B])
        w_qk = sb("w_qk", [P, 1])
        c_qk = sb("c_qk", [P, B])
        c_v = sb("c_v", [P, B])
        xq_f = sb("xq_f", [P, TB, D])
        xq_g = sb("xq_g", [P, TB, D])
        xq = sb("xq", [P, TB, D], BF16)
        xqT = sb("xqT", [P, TB, P], BF16)
        qkv = sb("qkv", [P, 2, 3 * D])
        prod1 = W1_raw[:].rearrange("p a b -> p (a b)").rearrange("p (a b) -> p a b", a=2)
        prod2 = W2_raw[:].rearrange("p a b -> p (a b)").rearrange("p (a b) -> p a b", a=2)
        S1 = sb("S1", [P, 2, H * H])
        S1m = sb("S1m", [P, 2, H])
        S1d = sb("S1d", [P, 2, H * H])
        E1 = sb("E1", [P, 2, H * H])
        E1sum = sb("E1sum", [P, 2, H])
        E1inv = sb("E1inv", [P, 4, H])
        hctx_f = sb("hctx_f", [P, 2, D])
        hctx = sb("hctx", [P, 2, D])
        ysq = sb("ysq", [P, TB, D])
        ssq2 = sb("ssq2", [P, TB])
        ms2 = sb("ms2", [P, TB])
        amax2 = sb("amax2", [P, TB])
        rms2 = sb("rms2", [P, TB])
        clip2 = sb("clip2", [P, TB])
        rec2 = sb("rec2", [P, TB])
        s2 = sb("s2", [P, TB])
        f2 = sb("f2", [P, TB])
        yq_f = sb("yq_f", [P, TB, D])
        yq_g = sb("yq_g", [P, TB, D])
        yq = sb("yq", [P, TB, D], BF16)
        yqT = sb("yqT", [P, TB, P], BF16)
        z1 = sb("z1", [P, TB, D])
        z1r = sb("z1r", [P, TB, D])
        bn1 = sb("bn1", [P, TB, 6])
        mv1 = sb("mv1", [P, TB, 2])
        ve1 = sb("ve1", [P, TB])
        rstd1 = sb("rstd1", [P, TB])
        shuffle = nc.dram_tensor("shuffle", [B, H, P, HD], F32, kind="Internal").ap()

        xq_ready = sem("xq_ready")
        xqT_psum = sem("xqT_psum")
        xqT_ready = sem("xqT_ready")
        qkv_psum = sem("qkv_psum")
        qkv_ready = sem("qkv_ready")
        qk_prod = sem("qk_prod")
        s1_ready = sem("s1_ready")
        e1_ready = sem("e1_ready")
        av_prod = sem("av_prod")
        hctx_ready = sem("hctx_ready")
        shuffled = sem("shuffled")
        y_in = sem("y_in")
        ysq_ready = sem("ysq_ready")
        ms2_ready = sem("ms2_ready")
        rms2_ready = sem("rms2_ready")
        yq_ready = sem("yq_ready")
        yqT_psum = sem("yqT_psum")
        yqT_ready = sem("yqT_ready")
        wo_psum = sem("wo_psum")
        z1_ready = sem("z1_ready")
        ve1_ready = sem("ve1_ready")
        rstd1_ready = sem("rstd1_ready")
        x1_ready = sem("x1_ready")

        x1s = sb("x1s", [P, TB, D])
        cs = sb("cs", [P, TB, D])
        x1T = sb("x1T", [P, TB, P])
        cT = sb("cT", [P, TB, P])
        Qa = sb("Qa", [P, 4, H, HS])
        Ka = sb("Ka", [P, 4, H, HS])
        Va = sb("Va", [P, 8, H, HD + 1])
        QT = sb("QT", [P, 2, HG, P])
        KT = sb("KT", [P, 4, HG, P])
        QmT = sb("QmT", [P, 2, HG, P])
        m2 = sb("m2", [P, 4, H])
        PT = W1_raw[:].rearrange("p (a h) q -> p a h q", a=2)
        sum2 = sb("sum2", [P, H])
        rsum2 = sb("rsum2", [P, H])
        att2 = sb("att2", [P, TB, D])
        z2 = sb("z2", [P, TB, D])
        bn2 = sb("bn2", [P, TB, 6])
        mv2 = sb("mv2", [P, TB, 2])
        ve2 = sb("ve2", [P, TB])
        rstd2 = sb("rstd2", [P, TB])

        x1s_ready = sem("x1s_ready")
        ctx_in = sem("ctx_in")
        x1T_psum = sem("x1T_psum")
        cT_psum = sem("cT_psum")
        x1T_ready = sem("x1T_ready")
        cT_ready = sem("cT_ready")
        proj_psum = sem("proj_psum")
        qkva_ready = sem("qkva_ready")
        qT_psum = sem("qT_psum")
        kT_psum = sem("kT_psum")
        qT_ready = sem("qT_ready")
        kT_ready = sem("kT_ready")
        score_psum = sem("score_psum")
        max_done = sem("max_done")
        m_ready = sem("m_ready")
        qmT_psum = sem("qmT_psum")
        qmT_ready = sem("qmT_ready")
        scoreT_psum = sem("scoreT_psum")
        p_ready = sem("p_ready")
        pv_psum = sem("pv_psum")
        att_ready = sem("att_ready")
        ve2_ready = sem("ve2_ready")
        rstd2_ready = sem("rstd2_ready")
        x2_ready = sem("x2_ready")

        xa = sb("xa", [P, TB, D])
        xaT = sb("xaT", [P, NT])
        lg = sb("lg", [P, TB, E])
        top = sb("top", [P, TB, 8])
        topi = sb("topi", [P, TB, 8], U32)
        topf = sb("topf", [P, TB, 8])
        gap = sb("gap", [P, TB])
        eg = sb("eg", [P, TB])
        eg1 = sb("eg1", [P, TB])
        w_top = sb("w_top", [P, 2, TB])
        oh = sb("oh", [P, 2, TB, E])
        rw = sb("rw", [P, TB, E])
        rw_rest = sb("rw_rest", [P, 2, TB, E])
        rw16 = sb("rw16", [P, TB, 3, E], BF16)
        rwT = sb("rwT", [3 * E, NT], BF16)
        
        pool2 = W2_raw[:].rearrange("p a b -> p (a b)").rearrange("p (a b) -> p a b", b=NT)
        hT = pool2[:, 0:4, :]
        xe = pool2[:, 4:6, :]
        oT = pool2[:, 6, :]
        z3, n3, g3, z4, o4 = (Y[:, TB * n:TB * (n + 1), :] for n in range(5))
        bn3 = sb("bn3", [P, TB, 6])
        mv3 = sb("mv3", [P, TB, 2])
        ve3 = sb("ve3", [P, TB])
        rstd3 = sb("rstd3", [P, TB])
        bn4 = sb("bn4", [P, TB, 6])
        mv4 = sb("mv4", [P, TB, 2])
        ve4 = sb("ve4", [P, TB])
        rstd4 = sb("rstd4", [P, TB])

        xa_ready = sem("xa_ready")
        xaT_psum = sem("xaT_psum")
        xaT_ready = sem("xaT_ready")
        lg_psum = sem("lg_psum")
        gap_ready = sem("gap_ready")
        eg_ready = sem("eg_ready")
        rw_ready = sem("rw_ready")
        rwT_psum = sem("rwT_psum")
        rwT_ready = sem("rwT_ready")
        rwb_psum = sem("rwb_psum")
        xe_ready = sem("xe_ready")
        h_psum = sem("h_psum")
        h_act = sem("h_act")
        h_dve = sem("h_dve")
        o_chunk = sem("o_chunk")
        oT_ready = sem("oT_ready")
        y3_psum = sem("y3_psum")
        ve3_ready = sem("ve3_ready")
        rstd3_ready = sem("rstd3_ready")
        ve4_ready = sem("ve4_ready")
        rstd4_ready = sem("rstd4_ready")
        o4_ready = sem("o4_ready")
        stored = sem("stored")

        def bc(ap, n):
            return ap.unsqueeze(2).broadcast_to((ap.shape[0], ap.shape[1], n))

        def batch(t, i):
            return bass.ds(TB * t + i, 1)

        def tile(t):
            return bass.ds(TB * t, TB)

        def turns(eng, lag, body, chain=None, steps=0):
            for u in range(lag):
                body(u, u % 2, lambda l, u=u: 0 <= u - l < T)
            with eng.Fori(0, (T - lag) // 2) as pair:
                if chain:
                    first = chain.n
                    chain.turn = pair * steps
                for v in range(2):
                    body(2 * pair + (lag + v), (lag + v) % 2, lambda l: True)
            if chain:
                made = chain.n - first
                assert made == steps, f"the loop makes {made} steps"
                chain.turn = 0
                chain.n += made * ((T - lag) // 2 - 1)
            for u in range(T, T + lag):
                body(u, u % 2, lambda l, u=u: 0 <= u - l < T)

        block = ctx.enter_context(nc.Block())

        def bcast_dma(eng, dst, src, s):
            eng.dma_start(dst, src.rearrange("(a n) -> a n", a=1).broadcast_to((P, src.shape[0]))).then_inc(s, 16)

        @block.sync
        def _(sp):
            for s in counters:
                sp.sem_inc(s, 16 * CREDIT if s in (shuffled, y_in, ctx_in, stored) else CREDIT)
            for n, w in enumerate((wq, wk, wv, wo)):
                sp.dma_start(w_raw[:, n, :], w).then_inc(w_in, 16)
            sp.dma_start(mask8[:], mask).then_inc(w_in, 16)
            for c in range(4):
                k = B // 4
                sp.dma_start(X[:, c * k:(c + 1) * k, :],
                             x[c * k:(c + 1) * k].rearrange("b s d -> s b d")).then_inc(x_in, 16)
            for n, w in enumerate((Wq, Wk, Wv)):
                sp.dma_start(W_raw[:, n, :], w).then_inc(xw_in, 16)
            for n, v in enumerate((bq, bk, bv)):
                bcast_dma(sp, b_qkv[:, n, :], v, xw_in)
            sp.dma_start(W1_raw[:], W1.rearrange("e (c p) d -> p (e c) d", p=P)).then_inc(ffn_in, 16)
            sp.dma_start(b1_rows[:], b1.rearrange("e (c p) -> (e c) p", p=P)).then_inc(ffn_in, 16)
            sp.dma_start(W2_raw[:], W2.rearrange("e d f -> d e f")).then_inc(ffn_in, 16)
            sp.dma_start(Wr_raw[:], Wr).then_inc(ffn_in, 16)
            sp.dma_start(br_col[:], br.rearrange("(e a) -> e a", a=1)).then_inc(ffn_in, 16)
            for n in range(3):
                sp.dma_start(b2_rep[n * E:(n + 1) * E, :], b2).then_inc(ffn_in, 16)
            bcast_dma(sp, gam[:], gamma, ffn_in)
            bcast_dma(sp, bet[:], beta, ffn_in)

            def a_turn(u, parity, there):
                for j in range(TB):
                    l, i = divmod(j - 2, TB)
                    l = -l
                    if there(l):
                        b = TB * (u - l) + i
                        after(sp, hctx_ready, b + 1)
                        sp.dma_start(shuffle[batch(u - l, i)].rearrange("a h s d -> s (a h) d"),
                                     hctx[:, i % 2, :].rearrange("p (h d) -> p h d", h=H)).then_inc(shuffled, 16)
                        after_dma(sp, shuffled, b + 1)
                        sp.dma_start(Y[:, batch(u - l, i), :],
                                     shuffle[batch(u - l, i)].rearrange("a h (q r) d -> (h q) a (r d)", r=D // HD)
                                     ).then_inc(y_in, 16)

            turns(sp, 2, a_turn)

            with sp.Fori(0, T) as t:
                after(sp, cT_psum, t)
                sp.dma_start(cs[:], ctx_1024[tile(t)].rearrange("b s d -> s b d")).then_inc(ctx_in, 16)

            with sp.Fori(0, T) as t:
                after(sp, o4_ready, t + 1)
                sp.dma_start(out[tile(t)].rearrange("b s d -> s b d"), o4[:]).then_inc(stored, 16)
            after_dma(sp, stored, T)

        @block.gpsimd
        def _(pool):
            ch = Chain(pool, pool_chain)
            ch(pool.memset(ident[:], 0.0))
            ch(pool.memset(ident16[:], 0.0))
            ch(pool.memset(sel[:], 1.0))
            pool.memset(ones[:], 1.0).then_inc(consts, 1)
            pool.memset(half[:], -0.5).then_inc(consts, 1)
            ch.settle()
            for m in (ident, ident16):
                pool.affine_select(out=m[:], in_=m[:], compare_op=ALU.not_equal, fill=1.0, base=0,
                                   pattern=[[-1, P]], channel_multiplier=1).then_inc(consts, 1)
            pool.iota(eiota[:], pattern=[[0, TB], [1, E]], base=0, channel_multiplier=0,
                      allow_small_or_imprecise_dtypes=True).then_inc(consts, 1)
            ch(pool.memset(diag[:], 0.0))
            ch.settle()
            for part in range(3):
                ch(pool.affine_select(out=diag[:, part, :], in_=diag[:, part, :], compare_op=ALU.not_equal,
                                      fill=1.0, base=-E * part, pattern=[[-1, E]], channel_multiplier=1))
            ch.settle()
            ch(pool.tensor_tensor(diag[:, 0, :], diag[:, 0, :], diag[:, 1, :], ALU.add))
            ch.settle()
            ch(pool.tensor_tensor(diag[:, 0, :], diag[:, 0, :], diag[:, 2, :], ALU.add))
            ch.settle()
            pool.tensor_tensor(sel[:], bc(diag[:, 0, :], P), sel[:], ALU.mult).then_inc(consts, 1)
            ch(pool.memset(Qa[:], 0.0))
            ch(pool.memset(Ka[:], 0.0))
            ch.settle()
            pool.memset(Qa[:, :, :, HD + 1], 1.0).then_inc(consts, 1)
            pool.memset(Ka[:, :, :, HD], 1.0).then_inc(consts, 1)
            pool.memset(Va[:, :, :, HD], 1.0).then_inc(consts, 1)
            pool.memset(xa[:, :, D - 1], 1.0).then_inc(consts, 1)
            pool.wait_ge(prep_dve, 3)
            pool.tensor_tensor(rms1[:], ssq1[:], half[:], ALU.pow).then_inc(prep_pool, 1)

            def a_turn(u, parity, there):
                for j in range(TB):
                    k = TB * u + j
                    if there(0):
                        after(pool, qkv_ready, k + 1)
                        after(pool, s1_ready, k - 1)
                        q = qkv[:, j % 2, 0:D].rearrange("p (h a d) -> p h a d", h=H, a=1)
                        kk = qkv[:, j % 2, D:2 * D].rearrange("p (a t d) -> p a t d", a=1, t=H)
                        pool.tensor_tensor(prod1[:, j % 2, :].rearrange("p (h t d) -> p h t d", h=H, t=H),
                                           q.broadcast_to((P, H, H, HD)), kk.broadcast_to((P, H, H, HD)),
                                           ALU.mult).then_inc(qk_prod, 1)
                    l, i = divmod(j - 1, TB)
                    l = -l
                    if there(l):
                        after(pool, e1_ready, TB * (u - l) + i + 1)
                        after(pool, hctx_ready, TB * (u - l) + i - 1)
                        a = E1[:, i % 2, :].rearrange("p (h a t) -> p h a t", h=H, a=1)
                        v = qkv[:, i % 2, 2 * D:].rearrange("p (a t d) -> p a d t", a=1, t=H)
                        pool.tensor_tensor(prod2[:, i % 2, :].rearrange("p (h d t) -> p h d t", h=H, d=HD),
                                           a.broadcast_to((P, H, HD, H)), v.broadcast_to((P, H, HD, H)),
                                           ALU.mult).then_inc(av_prod, 1)
                    if j == 3 and there(1):
                        after(pool, ms2_ready, u)
                        pool.tensor_tensor(rms2[:], ms2[:], half[:, 0:TB], ALU.pow).then_inc(rms2_ready, 1)
                    if j == 2 and there(2):
                        after(pool, ve1_ready, u - 1)
                        pool.tensor_tensor(rstd1[:], ve1[:], half[:, 0:TB], ALU.pow).then_inc(rstd1_ready, 1)

            turns(pool, 2, a_turn)

            def b_turn(u, parity, there):
                if there(0):
                    after(pool, x1_ready, u + 1)
                    after(pool, x1T_psum, u)
                    pool.tensor_copy(x1s[:], X[:, tile(u), :]).then_inc(x1s_ready, 1)
                if there(2):
                    after(pool, ve2_ready, u - 1)
                    pool.tensor_tensor(rstd2[:], ve2[:], half[:, 0:TB], ALU.pow).then_inc(rstd2_ready, 1)

            turns(pool, 2, b_turn)

            with pool.Fori(0, T) as t:
                after(pool, ve3_ready, t + 1)
                pool.tensor_tensor(rstd3[:], ve3[:], half[:, 0:TB], ALU.pow).then_inc(rstd3_ready, 1)
                after(pool, ve4_ready, t + 1)
                pool.tensor_tensor(rstd4[:], ve4[:], half[:, 0:TB], ALU.pow).then_inc(rstd4_ready, 1)

        @block.tensor
        def _(pe):
            pe.wait_ge(consts, 10)
            pe.wait_ge(prep_dve, 1)
            pe.matmul(PS[:, 0, 0:4], ones[:], w_abs[:], start=True, stop=True).then_inc(prep_pe, 1)
            pe.transpose(PS[:, 1, 0:B], mask_f[:], ident[0:B, 0:B]).then_inc(prep_pe, 1)
            pe.wait_ge(prep_dve, 4)
            for n in range(4):
                last = pe.transpose(PS[:, 2, n * 64:n * 64 + 64].bitcast(BF16), w_int[:, n, :], ident16[:])
            last.then_inc(prep_pe, 1)
            pe.wait_ge(xw_in, 16 * 6)
            for n in range(3):
                last = pe.transpose(PS[:, 3, n * D:(n + 1) * D], W_raw[:, n, :], ident[:])
            last.then_inc(prep_pe, 1)
            pe.wait_ge(ffn_in, 16 * 10)
            pe.transpose(PS[:, 7, 0:E * FC], b1_rows[:], ident[0:E * FC, 0:E * FC]).then_inc(b1_psum, 1)
            pe.wait_ge(prep_dve, 7)
            for g in range(E * FC // 4):
                if g >= 1:
                    pe.wait_ge(prep_act, 3 + g)
                for n in range(4):
                    pe.transpose(PS[:, 4, n * P:(n + 1) * P], W1_raw[:, 4 * g + n, :], ident[:])
                    last = pe.transpose(PS[:, 5, n * P:(n + 1) * P], W2_raw[:, g, n * P:(n + 1) * P], ident[:])
                last.then_inc(prep_pe, 1)
            pe.transpose(PS[:, 6, 0:E], Wr_raw[:], ident[0:E, 0:E]).then_inc(prep_pe, 1)

            pe.wait_ge(prep_act, 12)

            def a_turn(u, parity, there):
                if there(0):
                    after(pe, xq_ready, u + 1)
                    after(pe, xqT_ready, u)
                    for i in range(TB):
                        last = pe.transpose(PS[:, 0, i * 64:i * 64 + 64].bitcast(BF16), xq[:, i, :], ident16[:])
                    last.then_inc(xqT_psum, 1)
                    after(pe, xqT_ready, u + 1)


                def project(j):
                    if there(0):
                        after(pe, qkv_ready, TB * u + j - 1)
                        pe.matmul(PS[:, 1 + j % 2, 0:3 * D], xqT[:, j, :],
                                  w_intT[:, 0:3, :].rearrange("p a d -> p (a d)"),
                                  start=True, stop=True).then_inc(qkv_psum, 1)

                project(0)
                project(1)
                if there(2):
                    after(pe, yq_ready, u - 1)
                    after(pe, yqT_ready, u - 2)
                    for i in range(TB):
                        last = pe.transpose(PS[:, 3, i * 64:i * 64 + 64].bitcast(BF16), yq[:, i, :], ident16[:])
                    last.then_inc(yqT_psum, 1)
                    after(pe, yqT_ready, u - 1)
                    after(pe, z1_ready, u - 2)
                    for i in range(TB):
                        last = pe.matmul(PS[:, 4, i * D:(i + 1) * D], yqT[:, i, :], w_intT[:, 3, :],
                                         start=True, stop=True)
                    last.then_inc(wo_psum, 1)
                project(2)
                project(3)

            turns(pe, 2, a_turn)

            after(pe, z1_ready, T)
            after(pe, qkv_ready, B)

            def b_turn(u, parity, there):
                if there(0):
                    after(pe, x1s_ready, u + 1)
                    after(pe, qmT_ready, TB * u - 3)
                    for i in range(TB):
                        last = pe.transpose(PS[:, 4, i * P:(i + 1) * P], x1s[:, i, :], ident[:])
                    last.then_inc(x1T_psum, 1)
                    after_dma(pe, ctx_in, u + 1)
                    after(pe, kT_ready, TB * u - 1)
                    for i in range(TB):
                        last = pe.transpose(PS[:, 5, i * P:(i + 1) * P], cs[:, i, :], ident[:])
                    last.then_inc(cT_psum, 1)
                for j in range(TB):
                    k = TB * u + j
                    l, i = divmod(j - 2, TB)
                    if there(-l):
                        after(pe, qT_ready, k - 1)
                        after(pe, kT_ready, k - 1)
                        for a in range(2):
                            after(pe, p_ready, 2 * (k - 5) + a + 1)
                            after(pe, max_done, 2 * (k - 3) + a + 1)
                            for g in range(HG):
                                for h in (2 * a, 2 * a + 1):
                                    rows = slice(HS * h, HS * h + HS)
                                    last = pe.matmul(PS[:, h, g * P:(g + 1) * P], QT[rows, i % 2, g, :],
                                                     KT[rows, i, g, :], start=True, stop=True)
                            last.then_inc(score_psum, 1)
                    if there(0):
                        if j == 0:
                            after(pe, x1T_ready, u + 1)
                            after(pe, cT_ready, u + 1)
                        after(pe, qkva_ready, k)
                        pe.matmul(PS[:, 6, 0:D], x1T[:, j, :], W_T[:, 0, :], start=True, stop=True)
                        pe.matmul(PS[:, 6, D:3 * D], cT[:, j, :], W_T[:, 1:3, :].rearrange("p a d -> p (a d)"),
                                  start=True, stop=True).then_inc(proj_psum, 1)
                    l, i = divmod(j - 1, TB)
                    if there(-l):
                        after(pe, qkva_ready, k)
                        after(pe, qmT_ready, k - 3)
                        after(pe, kT_ready, k - 1)
                        for g in range(HG):
                            last = pe.transpose(PS[:, 4, g * P:(g + 1) * P],
                                                Qa[:, i, g * HG:(g + 1) * HG, :].rearrange("p h r -> p (h r)"), ident[:])
                        last.then_inc(qT_psum, 1)
                        for g in range(HG):
                            last = pe.transpose(PS[:, 5, g * P:(g + 1) * P],
                                                Ka[:, i, g * HG:(g + 1) * HG, :].rearrange("p h r -> p (h r)"), ident[:])
                        last.then_inc(kT_psum, 1)
                    l, i = divmod(j - 3, TB)
                    if there(-l):
                        after(pe, m_ready, k - 2)
                        after(pe, qT_ready, k if there(-((j - 1) // TB)) else B)
                        after(pe, qmT_ready, k - 3)
                        for g in range(HG):
                            last = pe.transpose(PS[:, 4, g * P:(g + 1) * P],
                                                Qa[:, i, g * HG:(g + 1) * HG, :].rearrange("p h r -> p (h r)"), ident[:])
                        last.then_inc(qmT_psum, 1)
                    l, i = divmod(j - 4, TB)
                    if there(-l):
                        after(pe, qmT_ready, k - 3)
                        for a in range(2):
                            after(pe, max_done, 2 * (k - 2) + a + 1 if there(-((j - 2) // TB)) else 2 * B)
                            after(pe, p_ready, 2 * (k - 5) + a + 1)
                            for g in range(HG):
                                for h in (2 * a, 2 * a + 1):
                                    rows = slice(HS * h, HS * h + HS)
                                    last = pe.matmul(PS[:, h, g * P:(g + 1) * P], KT[rows, i, g, :],
                                                     QmT[rows, i % 2, g, :], start=True, stop=True)
                            last.then_inc(scoreT_psum, 1)
                    l, i = divmod(j - 5, TB)
                    if there(-l):
                        after(pe, p_ready, 2 * (k - 4))
                        after(pe, att_ready, k - 5)
                        for h in range(H):
                            last = pe.matmul(PS[:, 7, h * (HD + 1):(h + 1) * (HD + 1)], PT[:, i % 2, h, :],
                                             Va[:, (TB * parity + j - 5) % 8, h, :], start=True, stop=True)
                        last.then_inc(pv_psum, 1)

            turns(pe, 2, b_turn)

            after(pe, att_ready, B)
            NC = E * FC
            with pe.Fori(0, T) as t:
                after(pe, xa_ready, t + 1)
                for i in range(TB):
                    last = pe.transpose(PS[:, 6, i * P:(i + 1) * P], xa[:, i, :], ident[:])
                last.then_inc(xaT_psum, 1)
                after(pe, xaT_ready, t + 1)
                for i in range(TB):
                    last = pe.matmul(PS[:, 6, i * E:(i + 1) * E], xaT[:, i * P:(i + 1) * P], Wr_T[:],
                                     start=True, stop=True)
                last.then_inc(lg_psum, 1)
                after(pe, rw_ready, t + 1)
                for i in range(TB):
                    last = pe.transpose(PS[0:3 * E, 6, i * 64:(i + 1) * 64].bitcast(BF16),
                                        rw16[:, i, :, :].rearrange("p a e -> p (a e)"), ident16[:])
                last.then_inc(rwT_psum, 1)
                after(pe, rwT_ready, t + 1)

                def weights_of(e):
                    after(pe, xe_ready, E * t + e - 1)
                    pe.matmul(PS[:, 4 + e % 2, :], sel[:, e, :], rwT[:], start=True, stop=True).then_inc(rwb_psum, 1)

                def down(n):
                    after(pe, h_dve if n % 2 else h_act, NC // 2 * t + n // 2 + 1)
                    pe.matmul(PS[:, 3, :], W2_T[:, n, :], hT[:, n % 4, :], start=False,
                              stop=(n == NC - 1)).then_inc(o_chunk, 1)

                weights_of(0)
                weights_of(1)
                after(pe, oT_ready, t)
                for a in range(3):
                    pe.matmul(PS[:, 3, :], b2_parts[:, a, :], rwT[:], start=(a == 0), stop=False)
                for n in range(NC):
                    e = n // FC
                    if n % FC == 0:
                        after(pe, xe_ready, E * t + e + 1)
                    if n % FC == 1 and 1 <= e < E - 1:
                        weights_of(e + 1)
                    if n >= 3:
                        after(pe, h_dve if (n - 3) % 2 else h_act, NC // 2 * t + (n - 3) // 2 + 1)
                    else:
                        m = n - 3 + NC
                        after(pe, h_dve if m % 2 else h_act, NC // 2 * (t - 1) + m // 2 + 1)
                    pe.matmul(PS[:, n % 3, :], W1_T[:, n, :], xe[:, e % 2, :], start=True, stop=True).then_inc(h_psum, 1)
                    if n >= 2:
                        down(n - 2)
                down(NC - 2)
                after(pe, h_dve, NC // 2 * (t + 1))
                pe.matmul(PS[:, 3, :], W2_T[:, NC - 1, :], hT[:, (NC - 1) % 4, :], start=False,
                          stop=True).then_inc(o_chunk, 1)
                after(pe, oT_ready, t + 1)
                after(pe, ve3_ready, t)
                for i in range(TB):
                    last = pe.transpose(PS[:, 7, i * D:(i + 1) * D], oT[:, i * P:(i + 1) * P], ident[:])
                last.then_inc(y3_psum, 1)

        @block.scalar
        def _(act):
            act.wait_ge(x_in, 64)
            act.activation(sq_all[:], X[:], ACT.Square).then_inc(prep_act, 1)
            act.wait_ge(prep_pe, 3)
            act.copy(w_intT[:].rearrange("p a d -> p (a d)"), PS[:, 2, 0:256].bitcast(BF16)).then_inc(prep_act, 1)
            act.wait_ge(prep_pe, 4)
            act.copy(W_T[:].rearrange("p a d -> p (a d)"), PS[:, 3, 0:3 * D]).then_inc(prep_act, 1)
            for g in range(E * FC // 4):
                act.wait_ge(prep_pe, 5 + g)
                act.copy(W1_T[:, 4 * g:4 * g + 4, :].rearrange("p a d -> p (a d)"), PS[:, 4, :])
                act.copy(W2_T[:, 4 * g:4 * g + 4, :].rearrange("p a d -> p (a d)"), PS[:, 5, :]).then_inc(prep_act, 1)
            act.wait_ge(prep_pe, 13)
            act.copy(Wr_T[:], PS[:, 6, 0:E]).then_inc(prep_act, 1)

            act.wait_ge(prep_dve, 6)

            def a_turn(u, parity, there):
                if there(0):
                    after(act, xqT_psum, u + 1)
                    after(act, qkv_psum, TB * u)
                    act.copy(xqT[:].rearrange("p a d -> p (a d)"), PS[:, 0, 0:256].bitcast(BF16)).then_inc(xqT_ready, 1)
                for j in range(TB):
                    if there(0):
                        k = TB * u + j
                        after(act, qkv_psum, k + 1)
                        after(act, av_prod, k - 1)
                        act.copy(qkv[:, j % 2, :], PS[:, 1 + j % 2, 0:3 * D]).then_inc(qkv_ready, 1)
                    l, i = divmod(j - 1, TB)
                    l = -l
                    if there(l):
                        b = TB * (u - l) + i
                        after(act, s1_ready, b + 1)
                        after(act, av_prod, b - 1)
                        act.activation(E1[:, i % 2, :], S1d[:, i % 2, :], ACT.Exp,
                                       scale=c_qk[:, batch(u - l, i)]).then_inc(e1_ready, 1)
                    if j == 3 and there(1):
                        after_dma(act, y_in, TB * u)
                        after(act, ms2_ready, u - 1)
                        act.activation(ysq[:], Y[:, tile(u - 1), :], ACT.Square).then_inc(ysq_ready, 1)
                    if j == 1 and there(2):
                        after(act, yqT_psum, u - 1)
                        after(act, wo_psum, u - 2)
                        act.copy(yqT[:].rearrange("p a d -> p (a d)"), PS[:, 3, 0:256].bitcast(BF16)).then_inc(yqT_ready, 1)

            turns(act, 2, a_turn)

            def b_turn(u, parity, there):
                if there(0):
                    after(act, x1T_psum, u + 1)
                    after(act, proj_psum, TB * u)
                    act.copy(x1T[:].rearrange("p a d -> p (a d)"), PS[:, 4, :]).then_inc(x1T_ready, 1)
                    after(act, cT_psum, u + 1)
                    act.copy(cT[:].rearrange("p a d -> p (a d)"), PS[:, 5, :]).then_inc(cT_ready, 1)
                for j in range(TB):
                    k = TB * u + j
                    l, i = divmod(j - 1, TB)
                    if there(-l):
                        after(act, qT_psum, k)
                        after(act, score_psum, 2 * (k - 2))
                        act.copy(QT[:, i % 2, :, :].rearrange("p a d -> p (a d)"), PS[:, 4, :]).then_inc(qT_ready, 1)
                        after(act, kT_psum, k)
                        after(act, scoreT_psum, 2 * (k - 4))
                        act.copy(KT[:, i, :, :].rearrange("p a d -> p (a d)"), PS[:, 5, :]).then_inc(kT_ready, 1)
                    l, i = divmod(j - 3, TB)
                    if there(-l):
                        after(act, qmT_psum, k - 2)
                        act.copy(QmT[:, i % 2, :, :].rearrange("p a d -> p (a d)"), PS[:, 4, :]).then_inc(qmT_ready, 1)
                    l, i = divmod(j - 4, TB)
                    if there(-l):
                        after(act, pv_psum, k - 5)
                        for a in range(2):
                            after(act, scoreT_psum, 2 * (k - 4) + a + 1)
                            act.activation(PT[:, i % 2].rearrange("p (g h) q -> p h g q", g=HG)[:, 2 * a:2 * a + 2],
                                           PS[:, 2 * a:2 * a + 2, :].rearrange("p h (g q) -> p h g q", g=HG),
                                           ACT.Exp, scale=HD ** -0.5).then_inc(p_ready, 1)

            turns(act, 2, b_turn)

            NC = E * FC
            with act.Fori(0, T) as t:
                after(act, xaT_psum, t + 1)
                after(act, h_psum, NC * t)
                act.copy(xaT[:], PS[:, 6, :]).then_inc(xaT_ready, 1)
                after(act, gap_ready, t + 1)
                act.activation(eg[:], gap[:], ACT.Exp).then_inc(eg_ready, 1)
                after(act, rwT_psum, t + 1)
                act.copy(rwT[:], PS[0:3 * E, 6, 0:256].bitcast(BF16)).then_inc(rwT_ready, 1)
                for n in range(0, NC, 2):
                    after(act, h_psum, NC * t + n + 1)
                    after(act, o_chunk, NC * t + n - 3)
                    act.activation(hT[:, n % 4, :], PS[:, n % 3, :], ACT.Relu).then_inc(h_act, 1)
                after(act, o_chunk, NC * (t + 1))
                after(act, y3_psum, t)
                act.copy(oT, PS[:, 3, :]).then_inc(oT_ready, 1)

        @block.vector
        def _(dve):
            ch = Chain(dve, dve_chain)
            step, settle = ch, ch.settle

            def settle_apart():
                settle()
                dve.memset(spare[:], 0.0)

            dve.wait_ge(w_in, 16 * 5)
            step(dve.tensor_copy(mask_f[:], mask8[:]))
            settle()
            dve.tensor_reduce(w_abs[:], w_raw[:], AX.X, ALU.add, apply_absolute_value=True).then_inc(prep_dve, 1)
            dve.wait_ge(x_in, 64)
            dve.tensor_reduce(amax1[:], X[:], AX.X, ALU.max, apply_absolute_value=True).then_inc(prep_dve, 1)
            dve.wait_ge(prep_act, 1)
            step(dve.tensor_reduce(ssq1[:], sq_all[:], AX.X, ALU.add))
            settle()
            dve.tensor_scalar(ssq1[:], ssq1[:], 1.0 / D, 1e-6, ALU.mult, ALU.add).then_inc(prep_dve, 1)
            dve.wait_ge(prep_pe, 2)
            step(dve.tensor_scalar(w_mean[:], PS[:, 0, 0:4], 1.0 / (D * D), 1e-5, ALU.mult, ALU.max))
            step(dve.tensor_scalar(mask_neg[:], PS[:, 1, 0:B], NEG, None, ALU.mult))
            settle()
            step(dve.reciprocal(w_inv[:], w_mean[:]))
            settle()
            step(dve.tensor_tensor(w_t[:], w_raw[:], bc(w_inv[:], D), ALU.mult))
            settle()
            step(dve.tensor_scalar(w_t[:], w_t[:], ROUND, -ROUND, ALU.add, ALU.add))
            settle()
            dve.tensor_scalar(w_int[:], w_t[:], 1.0, -1.0, ALU.min, ALU.max).then_inc(prep_dve, 1)
            dve.wait_ge(prep_pool, 1)
            step(dve.tensor_tensor(clip1[:], amax1[:], rms1[:], ALU.mult))
            settle()
            step(dve.tensor_scalar(clip1[:], clip1[:], 1e-5, None, ALU.max))
            settle()
            step(dve.reciprocal(rec1[:], clip1[:]))
            step(dve.tensor_scalar(inv1[:], clip1[:], 1.0 / 127, None, ALU.mult))
            step(dve.tensor_tensor(w_qk[:], w_mean[:, 0:1], w_mean[:, 1:2], ALU.mult))
            settle()
            dve.tensor_scalar(s1[:], rec1[:], 127.0, None, ALU.mult).then_inc(prep_dve, 1)
            step(dve.tensor_tensor(inv1sq[:], inv1[:], inv1[:], ALU.mult))
            step(dve.tensor_scalar(c_v[:], inv1[:], w_mean[:, 2:3], None, ALU.mult))
            settle()
            dve.tensor_scalar(c_qk[:], inv1sq[:], w_qk[:], HD ** -0.5, ALU.mult, ALU.mult).then_inc(prep_dve, 1)
            dve.wait_ge(ffn_in, 16 * 10)
            step(dve.tensor_tensor(W1_raw[:, :, 0:D - 1], W1_raw[:, :, 0:D - 1],
                                   W1_raw[:, :, D - 1:D].broadcast_to((P, E * FC, D - 1)), ALU.subtract))
            step(dve.tensor_scalar(Wr_raw[:, 0:D - 1], Wr_raw[:, 0:D - 1], Wr_raw[:, D - 1:D], None, ALU.subtract))
            settle()
            step(dve.tensor_copy(Wr_raw[:, D - 1:D], br_col[:]))
            dve.wait_ge(b1_psum, 1)
            step(dve.tensor_copy(W1_raw[:, :, D - 1], PS[:, 7, 0:E * FC]))
            settle()
            step(dve.tensor_copy(b2_parts[:, 0, :], b2_rep[:]))
            settle()
            step(dve.tensor_tensor(b2_rest[:, 0, :], b2_rep[:], b2_parts[:, 0, :], ALU.subtract))
            settle()
            step(dve.tensor_copy(b2_parts[:, 1, :], b2_rest[:, 0, :]))
            settle()
            step(dve.tensor_tensor(b2_rest[:, 1, :], b2_rest[:, 0, :], b2_parts[:, 1, :], ALU.subtract))
            settle()
            dve.tensor_copy(b2_parts[:, 2, :], b2_rest[:, 1, :]).then_inc(prep_dve, 1)
            dve.wait_ge(prep_dve, 7)

            def norm_stats(z, bn, mv, ve, ready):
                for i in range(TB):
                    step(dve.bn_stats(bn[:, i, :], z[:, i, :]))
                settle_apart()
                for i in range(TB):
                    step(dve.bn_aggr(mv[:, i, :], bn[:, i, :]))
                settle()
                dve.tensor_scalar(ve[:], mv[:, :, 1], 1e-5, None, ALU.add).then_inc(ready, 1)

            def norm_apply(o, z, mv, rstd):
                for i in range(TB):
                    last = dve.tensor_scalar(o(i), z[:, i, :], mv[:, i, 0:1], rstd[:, i:i + 1], ALU.subtract, ALU.mult)
                    if i < TB - 1:
                        step(last)
                return last

            def a_turn(u, parity, there):
                if there(0):
                    after(dve, xqT_psum, u)
                    step(dve.tensor_tensor(xq_f[:], X[:, tile(u), :], bc(rms1[:, tile(u)], D), ALU.mult))
                    settle()
                    step(dve.tensor_tensor(xq_g[:], xq_f[:], bc(s1[:, tile(u)], D), ALU.mult))
                    settle()
                    dve.tensor_scalar(xq[:], xq_g[:], ROUND, -ROUND, ALU.add, ALU.add).then_inc(xq_ready, 1)
                for j in range(TB):
                    k = TB * u + j
                    l1, i1 = divmod(j - 1, TB)
                    if there(-l1):
                        after(dve, qk_prod, k)
                        after(dve, e1_ready, k - 2)
                        step(dve.tensor_reduce(S1[:, i1 % 2, :], prod1[:, i1 % 2, :].rearrange("p (a d) -> p a d", d=HD),
                                               AX.X, ALU.add))
                        settle()
                        s = S1[:, i1 % 2, :].rearrange("p (h t) -> p h t", h=H)
                        step(dve.tensor_reduce(S1m[:, i1 % 2, :], s, AX.X, ALU.max))
                        settle()
                        dve.tensor_tensor(S1d[:, i1 % 2, :].rearrange("p (h t) -> p h t", h=H), s,
                                          bc(S1m[:, i1 % 2, :], H), ALU.subtract).then_inc(s1_ready, 1)
                    l2, i2 = divmod(j - 2, TB)
                    if there(-l2):
                        after(dve, av_prod, k - 1)
                        after_dma(dve, shuffled, k - 3)
                        step(dve.tensor_reduce(hctx_f[:, i2 % 2, :], prod2[:, i2 % 2, :].rearrange("p (a t) -> p a t", t=H),
                                               AX.X, ALU.add))
                        settle()
                        dve.scalar_tensor_tensor(hctx[:, i2 % 2, :].rearrange("p (h d) -> p h d", h=H),
                                                 hctx_f[:, i2 % 2, :].rearrange("p (h d) -> p h d", h=H),
                                                 c_v[:, batch(u + l2, i2)], bc(E1inv[:, i2, :], HD),
                                                 ALU.mult, ALU.mult).then_inc(hctx_ready, 1)
                    if there(-l1):
                        after(dve, e1_ready, k)
                        step(dve.tensor_reduce(E1sum[:, i1 % 2, :], E1[:, i1 % 2, :].rearrange("p (h t) -> p h t", h=H),
                                               AX.X, ALU.add))
                        settle()
                        step(dve.reciprocal(E1inv[:, i1, :], E1sum[:, i1 % 2, :]))
                    if j == 3 and there(1):
                        after_dma(dve, y_in, TB * u)
                        step(dve.tensor_reduce(amax2[:], Y[:, tile(u - 1), :], AX.X, ALU.max, apply_absolute_value=True))
                        after(dve, ysq_ready, u)
                        step(dve.tensor_reduce(ssq2[:], ysq[:], AX.X, ALU.add))
                        settle()
                        dve.tensor_scalar(ms2[:], ssq2[:], 1.0 / D, 1e-6, ALU.mult, ALU.add).then_inc(ms2_ready, 1)
                    if j == 0 and there(2):
                        after(dve, rms2_ready, u - 1)
                        after(dve, yqT_psum, u - 2)
                        step(dve.tensor_tensor(clip2[:], amax2[:], rms2[:], ALU.mult))
                        step(dve.tensor_tensor(yq_f[:], Y[:, tile(u - 2), :], bc(rms2[:], D), ALU.mult))
                        settle()
                        step(dve.tensor_scalar(clip2[:], clip2[:], 1e-5, None, ALU.max))
                        settle()
                        step(dve.reciprocal(rec2[:], clip2[:]))
                        step(dve.tensor_scalar(f2[:], clip2[:], 1.0 / 127, w_mean[:, 3:4], ALU.mult, ALU.mult))
                        settle()
                        step(dve.tensor_scalar(s2[:], rec2[:], 127.0, None, ALU.mult))
                        settle()
                        step(dve.tensor_tensor(yq_g[:], yq_f[:], bc(s2[:], D), ALU.mult))
                        settle()
                        dve.tensor_scalar(yq[:], yq_g[:], ROUND, -ROUND, ALU.add, ALU.add).then_inc(yq_ready, 1)
                    if j == 2 and there(2):
                        after(dve, wo_psum, u - 1)
                        dve.tensor_tensor(z1r[:], PS[:, 4, :].rearrange("p (a d) -> p a d", a=TB),
                                          bc(f2[:], D), ALU.mult).then_inc(z1_ready, 1)
                        after(dve, z1_ready, u - 1)
                        step(dve.tensor_tensor(z1[:], z1r[:], X[:, tile(u - 2), :], ALU.add))
                        settle()
                        norm_stats(z1, bn1, mv1, ve1, ve1_ready)
                    if j == 3 and there(2):
                        after(dve, rstd1_ready, u - 1)
                        norm_apply(lambda i: X[:, batch(u - 2, i), :], z1, mv1, rstd1).then_inc(x1_ready, 1)

            turns(dve, 2, a_turn, ch, A_STEPS)

            def b_turn(u, parity, there):
                for j in range(TB):
                    k = TB * u + j
                    l, i = divmod(j - 2, TB)
                    if there(-l):
                        for a in range(2):
                            after(dve, score_psum, 2 * (k - 2) + a + 1)
                            dve.tensor_reduce(m2[:, i, :].rearrange("p (g h) -> p h g", g=HG)[:, 2 * a:2 * a + 2],
                                              PS[:, 2 * a:2 * a + 2, :].rearrange("p h (g t) -> p h g t", g=HG),
                                              AX.X, ALU.max).then_inc(max_done, 1)
                        after(dve, max_done, 2 * (k - 1))
                        dve.tensor_scalar(Qa[:, i, :, HD], m2[:, i, :], -1.0, -0.1 * NEG, ALU.mult,
                                          ALU.min).then_inc(m_ready, 1)
                    if there(0):
                        after(dve, proj_psum, k + 1)
                        after(dve, qmT_psum, k - 3)
                        after(dve, pv_psum, k - 7)
                        p = PS[:, 6, 0:3 * D].rearrange("p (a h d) -> p a h d", a=3, h=H)
                        bb = b_qkv[:].rearrange("p a (h d) -> p a h d", h=H)
                        step(dve.tensor_tensor(Qa[:, j, :, 0:HD], p[:, 0], bb[:, 0], ALU.add))
                        step(dve.tensor_tensor(Va[:, TB * parity + j, :, 0:HD], p[:, 2], bb[:, 2], ALU.add))
                        step(dve.tensor_scalar(Ka[:, j, :, HD + 1], ones[:, 0:H], mask_neg[:, batch(u, j)], None, ALU.mult))
                        dve.tensor_tensor(Ka[:, j, :, 0:HD], p[:, 1], bb[:, 1], ALU.add).then_inc(qkva_ready, 1)
                    l, i = divmod(j - 6, TB)
                    if there(-l):
                        after(dve, pv_psum, k - 5)
                        o = PS[:, 7, 0:H * (HD + 1)].rearrange("p (h d) -> p h d", h=H)
                        step(dve.tensor_scalar(sum2[:], o[:, :, HD], 1e-30, None, ALU.max))
                        settle()
                        step(dve.reciprocal(rsum2[:], sum2[:]))
                        settle()
                        dve.tensor_tensor(att2[:, i, :].rearrange("p (h d) -> p h d", h=H), o[:, :, 0:HD],
                                          bc(rsum2[:], HD), ALU.mult).then_inc(att_ready, 1)
                    if j == 1 and there(2):
                        after(dve, att_ready, TB * (u - 1))
                        step(dve.tensor_tensor(z2[:], att2[:], X[:, tile(u - 2), :], ALU.add))
                        settle()
                        norm_stats(z2, bn2, mv2, ve2, ve2_ready)
                    if j == 3 and there(2):
                        after(dve, rstd2_ready, u - 1)
                        norm_apply(lambda i: X[:, batch(u - 2, i), :], z2, mv2, rstd2).then_inc(x2_ready, 1)

            turns(dve, 2, b_turn, ch, B_STEPS)

            NC = E * FC
            start = ch.n
            with dve.Fori(0, T) as t:
                ch.turn = C_STEPS * t
                after(dve, xaT_psum, t)
                after(dve, x2_ready, T)
                dve.tensor_copy(xa[:, :, 0:D - 1], X[:, tile(t), 0:D - 1]).then_inc(xa_ready, 1)
                after(dve, lg_psum, t + 1)
                step(dve.tensor_copy(lg[:].rearrange("p a e -> p (a e)"), PS[:, 6, 0:TB * E]))
                settle_apart()
                for i in range(TB):
                    step(dve.max(top[:, i, :], lg[:, i, :]))
                settle_apart()
                for i in range(TB):
                    step(dve.max_index(topi[:, i, :], top[:, i, :], lg[:, i, :]))
                dve.tensor_tensor(gap[:], top[:, :, 1], top[:, :, 0], ALU.subtract).then_inc(gap_ready, 1)
                settle()
                step(dve.tensor_copy(topf[:], topi[:]))
                after(dve, eg_ready, t + 1)
                step(dve.tensor_scalar(eg1[:], eg[:], 1.0, None, ALU.add))
                settle()
                step(dve.reciprocal(w_top[:, 0, :], eg1[:]))
                for n in range(2):
                    step(dve.tensor_tensor(oh[:, n], eiota[:], topf[:, :, n:n + 1].broadcast_to((P, TB, E)), ALU.is_equal))
                settle()
                step(dve.tensor_tensor(w_top[:, 1, :], eg[:], w_top[:, 0, :], ALU.mult))
                step(dve.tensor_tensor(oh[:, 0], oh[:, 0], bc(w_top[:, 0, :], E), ALU.mult))
                settle()
                step(dve.tensor_tensor(oh[:, 1], oh[:, 1], bc(w_top[:, 1, :], E), ALU.mult))
                settle()
                step(dve.tensor_tensor(rw[:], oh[:, 0], oh[:, 1], ALU.add))
                settle()
                after(dve, rwT_psum, t)
                step(dve.tensor_copy(rw16[:, :, 0, :], rw[:]))
                settle()
                step(dve.tensor_tensor(rw_rest[:, 0], rw[:], rw16[:, :, 0, :], ALU.subtract))
                settle()
                step(dve.tensor_copy(rw16[:, :, 1, :], rw_rest[:, 0]))
                settle()
                step(dve.tensor_tensor(rw_rest[:, 1], rw_rest[:, 0], rw16[:, :, 1, :], ALU.subtract))
                settle()
                dve.tensor_copy(rw16[:, :, 2, :], rw_rest[:, 1]).then_inc(rw_ready, 1)

                after(dve, xaT_ready, t + 1)

                def scale_x(e):
                    after(dve, rwb_psum, E * t + e + 1)
                    dve.tensor_tensor(xe[:, e % 2, :], xaT[:], PS[:, 4 + e % 2, :], ALU.mult).then_inc(xe_ready, 1)

                scale_x(0)
                scale_x(1)
                for n in range(1, NC, 2):
                    after(dve, h_psum, NC * t + n + 1)
                    after(dve, o_chunk, NC * t + n - 3)
                    dve.tensor_scalar(hT[:, n % 4, :], PS[:, n % 3, :], 0.0, None, ALU.max).then_inc(h_dve, 1)
                    e = n // FC + 1
                    if n % FC == 1 and 2 <= e < E:
                        after(dve, h_psum, NC * t + FC * (e - 1))
                        scale_x(e)
                after(dve, y3_psum, t + 1)
                step(dve.tensor_tensor(z3[:], PS[:, 7, :].rearrange("p (a d) -> p a d", a=TB), X[:, tile(t), :], ALU.add))
                settle()
                norm_stats(z3, bn3, mv3, ve3, ve3_ready)
                after(dve, rstd3_ready, t + 1)
                step(norm_apply(lambda i: n3[:, i, :], z3, mv3, rstd3))
                settle()
                gb = gam[:].unsqueeze(1).broadcast_to((P, TB, D))
                be = bet[:].unsqueeze(1).broadcast_to((P, TB, D))
                step(dve.tensor_tensor(g3[:], n3[:], gb, ALU.mult))
                settle()
                step(dve.tensor_tensor(n3[:], g3[:], be, ALU.add))
                settle()
                step(dve.tensor_tensor(z4[:], n3[:], X[:, tile(t), :], ALU.add))
                settle()
                norm_stats(z4, bn4, mv4, ve4, ve4_ready)
                after(dve, rstd4_ready, t + 1)
                after_dma(dve, stored, t)
                norm_apply(lambda i: o4[:, i, :], z4, mv4, rstd4).then_inc(o4_ready, 1)
            assert ch.n - start == C_STEPS, f"the loop makes {ch.n - start} steps"


_INS = ["x", "ctx_1024", "mask_BxS2_bf0", "L0_attn_wq", "L0_attn_wk", "L0_attn_wv", "L0_attn_wo",
        "L0_xattn_Wq", "L0_xattn_bq", "L0_xattn_Wk", "L0_xattn_bk", "L0_xattn_Wv", "L0_xattn_bv",
        "L0_ffn_Wr", "L0_ffn_br", "L0_ffn_W1", "L0_ffn_b1", "L0_ffn_W2", "L0_ffn_b2", "L0_ffn_gamma", "L0_ffn_beta"]


def kernel(**inputs):
    import numpy as _np
    import concourse.bacc as _bacc
    from concourse import mybir as _mybir
    from concourse.bass_utils import run_bass_kernel_spmd as _run

    nc = _bacc.Bacc("TRN2", target_bir_lowering=False, num_devices=1)
    arrays, args = {}, []
    for name in _INS:
        a = _np.ascontiguousarray(inputs[name])
        arrays[f"in_{name}_dram"] = a
        args.append(nc.dram_tensor(f"in_{name}_dram", a.shape, _mybir.dt.from_np(a.dtype), kind="ExternalInput").ap())
    args.append(nc.dram_tensor("out_dram", inputs["x"].shape, _mybir.dt.float32, kind="ExternalOutput").ap())
    decoder_layer(nc, *args)
    r = _run(nc, [arrays], core_ids=[0])
    return r.results[0]["out_dram"]
```

```python
from contextlib import ExitStack

import concourse.bass as bass
from concourse import mybir


def decoder_layer(nc, x, ctx_1024, mask, wq, wk, wv, wo, Wq, bq, Wk, bk, Wv, bv,
                  Wr, br, W1, b1, W2, b2, gamma, beta, out):
    F32, BF16, F16 = mybir.dt.float32, mybir.dt.bfloat16, mybir.dt.float16
    U8, U32, I32 = mybir.dt.uint8, mybir.dt.uint32, mybir.dt.int32
    ALU, ACT, AX = mybir.AluOpType, mybir.ActivationFunctionType, mybir.AxisListType

    B, P, D = x.shape
    H, HD = 16, D // 16
    E, F = W1.shape[0], W1.shape[1]
    FC = F // P
    TB = 4
    T = B // TB
    NT = TB * P
    HS = 64
    HR = P // HS
    HG = H // HR
    X_SCALE = 8.0
    NEG = -1e30
    ROUND = 1.5 * 2.0 ** 23
    A_STEPS, B_STEPS, C_STEPS = 86, 80, 96
    CREDIT = 16

    ctx = ExitStack()
    with ctx:
        def sb(name, shape, dt=F32):
            return ctx.enter_context(nc.sbuf_tensor(name, shape, dt))

        counters = []

        def sem(name):
            s = ctx.enter_context(nc.semaphore(name))
            counters.append(s)
            return s

        def after(eng, s, n):
            eng.wait_ge(s, n + CREDIT)

        def after_dma(eng, s, n):
            eng.wait_ge(s, 16 * (n + CREDIT))

        class Chain:

            def __init__(self, eng, s):
                self.eng, self.s, self.n, self.turn = eng, s, 0, 0

            def __call__(self, instruction):
                instruction.then_inc(self.s, 1)
                self.n += 1

            def settle(self):
                self.eng.wait_ge(self.s, self.n + self.turn)

        X = sb("X", [P, B, D])
        Y = sb("Y", [P, B, D])
        w_raw = sb("w_raw", [P, 4, D])
        w_abs = sb("w_abs", [P, 4])
        w_mean = sb("w_mean", [P, 4])
        w_inv = sb("w_inv", [P, 4])
        w_t = sb("w_t", [P, 4, D])
        w_int = sb("w_int", [P, 4, D], BF16)
        w_intT = sb("w_intT", [P, 4, D], BF16)
        W_raw = sb("W_raw", [P, 3, D])
        W_T = sb("W_T", [P, 3, D])
        b_qkv = sb("b_qkv", [P, 3, D])
        gam = sb("gam", [P, D])
        bet = sb("bet", [P, D])
        W1_raw = sb("W1_raw", [P, E * FC, D])
        b1_rows = sb("b1_rows", [E * FC, P])
        W1_hi = sb("W1_hi", [P, E * FC, P], F16)
        W1_lo = sb("W1_lo", [P, E * FC, P], F16)
        W2_raw = sb("W2_raw", [P, E, F])
        W2_hi = sb("W2_hi", [P, E * FC, D], F16)
        W2_lo = sb("W2_lo", [P, E * FC, D], F16)
        w_top_abs = sb("w_top_abs", [P, 2])
        w_scale = sb("w_scale", [P, 2])
        b2_scale = sb("b2_scale", [P, 1])
        o_scale = sb("o_scale", [P, 1])
        Wr_raw = sb("Wr_raw", [E, D])
        br_col = sb("br_col", [E, 1])
        Wr_T = sb("Wr_T", [P, E])
        b2_rep = sb("b2_rep", [3 * E, D])
        b2_rest = sb("b2_rest", [3 * E, 2, D])
        b2_parts = sb("b2_parts", [3 * E, 3, D], BF16)
        ident = sb("ident", [P, P])
        ident16 = sb("ident16", [P, P], BF16)
        ones = sb("ones", [P, P])
        sel = sb("sel", [3 * E, E, P], BF16)
        diag = sb("diag", [3 * E, 3, E])
        half = sb("half", [P, B])
        mask8 = sb("mask8", [B, P], U8)
        mask_f = sb("mask_f", [B, P])
        mask_neg = sb("mask_neg", [P, B])
        spare = sb("spare", [P, 1])
        spare_pool = sb("spare_pool", [P, 1])
        eiota = sb("eiota", [P, TB, E])

        PS = ctx.enter_context(nc.psum_tensor("PS", [P, 8, 512], F32))

        x_in = ctx.enter_context(nc.semaphore("x_in"))
        w_in = ctx.enter_context(nc.semaphore("w_in"))
        xw_in = ctx.enter_context(nc.semaphore("xw_in"))
        ffn_in = ctx.enter_context(nc.semaphore("ffn_in"))
        out_done = ctx.enter_context(nc.semaphore("out_done"))
        consts = ctx.enter_context(nc.semaphore("consts"))
        prep_pe = ctx.enter_context(nc.semaphore("prep_pe"))
        prep_dve = ctx.enter_context(nc.semaphore("prep_dve"))
        prep_act = ctx.enter_context(nc.semaphore("prep_act"))
        prep_pool = ctx.enter_context(nc.semaphore("prep_pool"))
        w_abs_ready = ctx.enter_context(nc.semaphore("w_abs_ready"))
        w_split = ctx.enter_context(nc.semaphore("w_split"))
        b1_psum = ctx.enter_context(nc.semaphore("b1_psum"))
        dve_chain = ctx.enter_context(nc.semaphore("dve_chain"))
        act_chain = ctx.enter_context(nc.semaphore("act_chain"))
        pool_chain = ctx.enter_context(nc.semaphore("pool_chain"))

        sq_all = Y
        ssq1 = sb("ssq1", [P, B])
        amax1 = sb("amax1", [P, B])
        rms1 = sb("rms1", [P, B])
        clip1 = sb("clip1", [P, B])
        rec1 = sb("rec1", [P, B])
        s1 = sb("s1", [P, B])
        inv1 = sb("inv1", [P, B])
        inv1sq = sb("inv1sq", [P, B])
        w_qk = sb("w_qk", [P, 1])
        c_qk = sb("c_qk", [P, B])
        c_v = sb("c_v", [P, B])
        xq_f = sb("xq_f", [P, TB, D])
        xq_g = sb("xq_g", [P, TB, D])
        xq = sb("xq", [P, TB, D], BF16)
        xqT = sb("xqT", [P, TB, P], BF16)
        qkv = sb("qkv", [P, 2, 3 * D])
        prod1 = W1_raw[:].rearrange("p a b -> p (a b)").rearrange("p (a b) -> p a b", a=2)
        prod2 = W2_raw[:].rearrange("p a b -> p (a b)").rearrange("p (a b) -> p a b", a=2)
        S1 = sb("S1", [P, 2, H * H])
        S1m = sb("S1m", [P, 2, H])
        S1d = sb("S1d", [P, 2, H * H])
        E1 = sb("E1", [P, 2, H * H])
        E1sum = sb("E1sum", [P, 2, H])
        E1inv = sb("E1inv", [P, 4, H])
        hctx_f = sb("hctx_f", [P, 2, D])
        hctx = sb("hctx", [P, 2, D])
        ysq = sb("ysq", [P, TB, D])
        ssq2 = sb("ssq2", [P, TB])
        ms2 = sb("ms2", [P, TB])
        amax2 = sb("amax2", [P, TB])
        rms2 = sb("rms2", [P, TB])
        clip2 = sb("clip2", [P, TB])
        rec2 = sb("rec2", [P, TB])
        s2 = sb("s2", [P, TB])
        f2 = sb("f2", [P, TB])
        yq_f = sb("yq_f", [P, TB, D])
        yq_g = sb("yq_g", [P, TB, D])
        yq = sb("yq", [P, TB, D], BF16)
        yqT = sb("yqT", [P, TB, P], BF16)
        z1 = sb("z1", [P, TB, D])
        z1r = sb("z1r", [P, TB, D])
        bn1 = sb("bn1", [P, TB, 6])
        mv1 = sb("mv1", [P, TB, 2])
        ve1 = sb("ve1", [P, TB])
        rstd1 = sb("rstd1", [P, TB])
        shuffle = nc.dram_tensor("shuffle", [B, H, P, HD], F32, kind="Internal").ap()

        xq_ready = sem("xq_ready")
        xqT_psum = sem("xqT_psum")
        xqT_ready = sem("xqT_ready")
        qkv_psum = sem("qkv_psum")
        qkv_ready = sem("qkv_ready")
        qk_prod = sem("qk_prod")
        s1_ready = sem("s1_ready")
        e1_ready = sem("e1_ready")
        av_prod = sem("av_prod")
        hctx_ready = sem("hctx_ready")
        shuffled = sem("shuffled")
        y_in = sem("y_in")
        ysq_ready = sem("ysq_ready")
        ms2_ready = sem("ms2_ready")
        rms2_ready = sem("rms2_ready")
        yq_ready = sem("yq_ready")
        yqT_psum = sem("yqT_psum")
        yqT_ready = sem("yqT_ready")
        wo_psum = sem("wo_psum")
        z1_ready = sem("z1_ready")
        ve1_ready = sem("ve1_ready")
        rstd1_ready = sem("rstd1_ready")
        x1_ready = sem("x1_ready")

        x1s = sb("x1s", [P, TB, D])
        cs = sb("cs", [P, TB, D])
        x1T = sb("x1T", [P, TB, P])
        cT = sb("cT", [P, TB, P])
        qk_f = sb("qk_f", [P, 2, 2, D])
        qk_rest = sb("qk_rest", [P, 2, D])
        QK = sb("QK", [P, 4, 2, H, HS], BF16)
        Va = sb("Va", [P, 8, D])
        HO = 8 * (HD + 1)
        VF = 8 * (HO + HD + 1)
        frames = W2_raw[:].rearrange("p a b -> p (a b)")
        v_frame = frames[:, 0:4 * VF].rearrange("p (b a c) -> p b a c", b=2, a=2)
        outT = frames[0:HO, 4 * VF:4 * VF + 2 * P]
        QT = sb("QT", [P, 2, HG, P], BF16)
        KT = sb("KT", [P, 4, HG, P], BF16)
        QmT = sb("QmT", [P, 2, HG, P], BF16)
        m2 = sb("m2", [P, H])
        m_neg = sb("m_neg", [P, H])
        m_rest = sb("m_rest", [P, 1, H])
        PT = W1_raw[:].rearrange("p (a h) q -> p a h q", a=2)
        sum2 = sb("sum2", [P, H])
        rsum2 = sb("rsum2", [P, H])
        att2 = sb("att2", [P, TB, D])
        z2 = yq_f
        bn2 = sb("bn2", [P, TB, 6])
        mv2 = sb("mv2", [P, TB, 2])
        ve2 = sb("ve2", [P, TB])
        rstd2 = sb("rstd2", [P, TB])

        x1s_ready = sem("x1s_ready")
        ctx_in = sem("ctx_in")
        x1T_psum = sem("x1T_psum")
        cT_psum = sem("cT_psum")
        x1T_ready = sem("x1T_ready")
        cT_ready = sem("cT_ready")
        proj_psum = sem("proj_psum")
        qkv_copied = sem("qkv_copied")
        high_ready = sem("high_ready")
        split_ready = sem("split_ready")
        qT_psum = sem("qT_psum")
        kT_psum = sem("kT_psum")
        qT_ready = sem("qT_ready")
        kT_ready = sem("kT_ready")
        score_psum = sem("score_psum")
        max_done = sem("max_done")
        m_ready = sem("m_ready")
        qmT_psum = sem("qmT_psum")
        qmT_ready = sem("qmT_ready")
        scoreT_psum = sem("scoreT_psum")
        p_ready = sem("p_ready")
        frames_clear = sem("frames_clear")
        v_ready = sem("v_ready")
        pv_psum = sem("pv_psum")
        outT_ready = sem("outT_ready")
        out_psum = sem("out_psum")
        att_ready = sem("att_ready")
        ve2_ready = sem("ve2_ready")
        rstd2_ready = sem("rstd2_ready")
        x2_ready = sem("x2_ready")

        xa = sb("xa", [P, TB, D])
        xaT = sb("xaT", [P, 2, NT])
        lg = sb("lg", [P, TB, E])
        top = sb("top", [P, TB, 8])
        topi = sb("topi", [P, TB, 8], U32)
        topf = sb("topf", [P, TB, 8])
        gap = sb("gap", [P, TB])
        eg = sb("eg", [P, TB])
        eg1 = sb("eg1", [P, TB])
        w_top = sb("w_top", [P, 2, TB])
        oh = sb("oh", [P, 2, TB, E])
        rw = sb("rw", [P, TB, E])
        rw_rest = sb("rw_rest", [P, 2, TB, E])
        rw16 = sb("rw16", [P, TB, 3, E], BF16)
        rwT = sb("rwT", [3 * E, 2, NT], BF16)
        
        pool2 = W2_raw[:].rearrange("p a b -> p (a b)").rearrange("p (a b) -> p a b", b=NT)
        xe = pool2[:, 0:2, :]
        oT = pool2[:, 2, :]
        parts = W1_raw[:].rearrange("p a b -> p (a b)").bitcast(F16).rearrange("p (k a b) -> p k a b", k=4, a=4)
        h_hi, h_lo, x_hi, x_lo = (parts[:, k] for k in range(4))
        z3, n3, g3, z4, o4 = (Y[:, TB * n:TB * (n + 1), :] for n in range(5))
        bn3 = sb("bn3", [P, TB, 6])
        mv3 = sb("mv3", [P, TB, 2])
        ve3 = sb("ve3", [P, TB])
        rstd3 = sb("rstd3", [P, TB])
        bn4 = sb("bn4", [P, TB, 6])
        mv4 = sb("mv4", [P, TB, 2])
        ve4 = sb("ve4", [P, TB])
        rstd4 = sb("rstd4", [P, TB])

        xa_ready = sem("xa_ready")
        xaT_psum = sem("xaT_psum")
        xaT_ready = sem("xaT_ready")
        lg_psum = sem("lg_psum")
        gap_ready = sem("gap_ready")
        eg_ready = sem("eg_ready")
        rw_ready = sem("rw_ready")
        rwT_psum = sem("rwT_psum")
        rwT_ready = sem("rwT_ready")
        rwb_psum = sem("rwb_psum")
        xe_ready = sem("xe_ready")
        xsplit_ready = sem("xsplit_ready")
        h_psum = sem("h_psum")
        h_hi_ready = sem("h_hi_ready")
        h_lo_ready = sem("h_lo_ready")
        down_done = sem("down_done")
        oT_ready = sem("oT_ready")
        y3_psum = sem("y3_psum")
        z3_ready = sem("z3_ready")
        ve3_ready = sem("ve3_ready")
        rstd3_ready = sem("rstd3_ready")
        ve4_ready = sem("ve4_ready")
        rstd4_ready = sem("rstd4_ready")
        o4_ready = sem("o4_ready")
        stored = sem("stored")

        def bc(ap, n):
            return ap.unsqueeze(2).broadcast_to((ap.shape[0], ap.shape[1], n))

        def batch(t, i):
            return bass.ds(TB * t + i, 1)

        def tile(t):
            return bass.ds(TB * t, TB)

        def turns(eng, lag, body, chain=None, steps=0):
            for u in range(lag):
                body(u, u % 2, lambda l, u=u: 0 <= u - l < T)
            with eng.Fori(0, (T - lag) // 2) as pair:
                if chain:
                    first = chain.n
                    chain.turn = pair * steps
                for v in range(2):
                    body(2 * pair + (lag + v), (lag + v) % 2, lambda l: True)
            if chain:
                made = chain.n - first
                assert made == steps, f"the loop makes {made} steps"
                chain.turn = 0
                chain.n += made * ((T - lag) // 2 - 1)
            for u in range(T, T + lag):
                body(u, u % 2, lambda l, u=u: 0 <= u - l < T)

        def slots(j, side, first, end, by=1):
            return QK[:, j, side, :, 0:6 * HD].rearrange("p h (s d) -> p h s d", d=HD)[:, :, first:end:by, :]

        def heads(ap):
            return ap.rearrange("p (h d) -> p h d", h=H)

        def banks(a):
            return PS[:, 2 * a:2 * a + 2, :]

        def half_heads(ap, a):
            pat = "p (g r) q -> p r g q" if len(ap.shape) == 3 else "p (g r) -> p r g"
            return ap[:, 8 * a:8 * a + 8].rearrange(pat, r=HR)

        def diagonal(b):
            return v_frame[:, b].rearrange("p a (n c) -> p a n c", n=8)[:, :, :, 0:HD + 1]

        NC = E * FC

        def prepared(g):
            return (1, g + 2) if g + 2 < E else (0, g + 2 - E)

        block = ctx.enter_context(nc.Block())

        def bcast_dma(eng, dst, src, s):
            eng.dma_start(dst, src.rearrange("(a n) -> a n", a=1).broadcast_to((P, src.shape[0]))).then_inc(s, 16)

        @block.sync
        def _(sp):
            for s in counters:
                sp.sem_inc(s, 16 * CREDIT if s in (shuffled, y_in, ctx_in, stored) else CREDIT)
            for n, w in enumerate((wq, wk, wv, wo)):
                sp.dma_start(w_raw[:, n, :], w).then_inc(w_in, 16)
            sp.dma_start(mask8[:], mask).then_inc(w_in, 16)
            for c in range(4):
                k = B // 4
                sp.dma_start(X[:, c * k:(c + 1) * k, :],
                             x[c * k:(c + 1) * k].rearrange("b s d -> s b d")).then_inc(x_in, 16)
            for n, w in enumerate((Wq, Wk, Wv)):
                sp.dma_start(W_raw[:, n, :], w).then_inc(xw_in, 16)
            for n, v in enumerate((bq, bk, bv)):
                bcast_dma(sp, b_qkv[:, n, :], v, xw_in)
            sp.dma_start(W1_raw[:], W1.rearrange("e (c p) d -> p (e c) d", p=P)).then_inc(ffn_in, 16)
            sp.dma_start(b1_rows[:], b1.rearrange("e (c p) -> (e c) p", p=P)).then_inc(ffn_in, 16)
            sp.dma_start(W2_raw[:], W2.rearrange("e d f -> d e f")).then_inc(ffn_in, 16)
            sp.dma_start(Wr_raw[:], Wr).then_inc(ffn_in, 16)
            sp.dma_start(br_col[:], br.rearrange("(e a) -> e a", a=1)).then_inc(ffn_in, 16)
            for n in range(3):
                sp.dma_start(b2_rep[n * E:(n + 1) * E, :], b2).then_inc(ffn_in, 16)
            bcast_dma(sp, gam[:], gamma, ffn_in)
            bcast_dma(sp, bet[:], beta, ffn_in)

            def a_turn(u, parity, there):
                for j in range(TB):
                    l, i = divmod(j - 2, TB)
                    l = -l
                    if there(l):
                        b = TB * (u - l) + i
                        after(sp, hctx_ready, b + 1)
                        sp.dma_start(shuffle[batch(u - l, i)].rearrange("a h s d -> s (a h) d"),
                                     hctx[:, i % 2, :].rearrange("p (h d) -> p h d", h=H)).then_inc(shuffled, 16)
                        after_dma(sp, shuffled, b + 1)
                        sp.dma_start(Y[:, batch(u - l, i), :],
                                     shuffle[batch(u - l, i)].rearrange("a h (q r) d -> (h q) a (r d)", r=D // HD)
                                     ).then_inc(y_in, 16)

            turns(sp, 2, a_turn)

            with sp.Fori(0, T) as t:
                after(sp, cT_psum, t)
                sp.dma_start(cs[:], ctx_1024[tile(t)].rearrange("b s d -> s b d")).then_inc(ctx_in, 16)

            with sp.Fori(0, T) as t:
                after(sp, o4_ready, t + 1)
                sp.dma_start(out[tile(t)].rearrange("b s d -> s b d"), o4[:]).then_inc(stored, 16)
            after_dma(sp, stored, T)

        @block.gpsimd
        def _(pool):
            ch = Chain(pool, pool_chain)
            ch(pool.memset(ident[:], 0.0))
            ch(pool.memset(ident16[:], 0.0))
            ch(pool.memset(sel[:], 1.0))
            pool.memset(ones[:], 1.0).then_inc(consts, 1)
            pool.memset(half[:], -0.5).then_inc(consts, 1)
            ch.settle()
            for m in (ident, ident16):
                pool.affine_select(out=m[:], in_=m[:], compare_op=ALU.not_equal, fill=1.0, base=0,
                                   pattern=[[-1, P]], channel_multiplier=1).then_inc(consts, 1)
            pool.iota(eiota[:], pattern=[[0, TB], [1, E]], base=0, channel_multiplier=0,
                      allow_small_or_imprecise_dtypes=True).then_inc(consts, 1)
            ch(pool.memset(diag[:], 0.0))
            ch.settle()
            for part in range(3):
                ch(pool.affine_select(out=diag[:, part, :], in_=diag[:, part, :], compare_op=ALU.not_equal,
                                      fill=1.0, base=-E * part, pattern=[[-1, E]], channel_multiplier=1))
            ch.settle()
            ch(pool.tensor_tensor(diag[:, 0, :], diag[:, 0, :], diag[:, 1, :], ALU.add))
            ch.settle()
            ch(pool.tensor_tensor(diag[:, 0, :], diag[:, 0, :], diag[:, 2, :], ALU.add))
            ch.settle()
            pool.tensor_tensor(sel[:], bc(diag[:, 0, :], P), sel[:], ALU.mult).then_inc(consts, 1)
            ch(pool.memset(QK[:], 0.0))
            ch.settle()
            pool.memset(QK[:, :, 0, :, 6 * HD + 3], 1.0).then_inc(consts, 1)
            pool.memset(QK[:, :, 1, :, 6 * HD:6 * HD + 3], 1.0).then_inc(consts, 1)
            pool.memset(xa[:, :, D - 1], 1.0).then_inc(consts, 1)
            pool.wait_ge(prep_dve, 3)
            pool.tensor_tensor(rms1[:], ssq1[:], half[:], ALU.pow).then_inc(prep_pool, 1)
            pool.wait_ge(w_abs_ready, 1)
            pool.partition_all_reduce(w_top_abs[:], w_top_abs[:], P, bass.bass_isa.ReduceOp.max).then_inc(prep_pool, 1)

            def a_turn(u, parity, there):
                for j in range(TB):
                    k = TB * u + j
                    if there(0):
                        after(pool, qkv_ready, k + 1)
                        after(pool, s1_ready, k - 1)
                        q = qkv[:, j % 2, 0:D].rearrange("p (h a d) -> p h a d", h=H, a=1)
                        kk = qkv[:, j % 2, D:2 * D].rearrange("p (a t d) -> p a t d", a=1, t=H)
                        pool.tensor_tensor(prod1[:, j % 2, :].rearrange("p (h t d) -> p h t d", h=H, t=H),
                                           q.broadcast_to((P, H, H, HD)), kk.broadcast_to((P, H, H, HD)),
                                           ALU.mult).then_inc(qk_prod, 1)
                    l, i = divmod(j - 1, TB)
                    l = -l
                    if there(l):
                        after(pool, e1_ready, TB * (u - l) + i + 1)
                        after(pool, hctx_ready, TB * (u - l) + i - 1)
                        a = E1[:, i % 2, :].rearrange("p (h a t) -> p h a t", h=H, a=1)
                        v = qkv[:, i % 2, 2 * D:].rearrange("p (a t d) -> p a d t", a=1, t=H)
                        pool.tensor_tensor(prod2[:, i % 2, :].rearrange("p (h d t) -> p h d t", h=H, d=HD),
                                           a.broadcast_to((P, H, HD, H)), v.broadcast_to((P, H, HD, H)),
                                           ALU.mult).then_inc(av_prod, 1)
                    if j == 3 and there(1):
                        after(pool, ms2_ready, u)
                        pool.tensor_tensor(rms2[:], ms2[:], half[:, 0:TB], ALU.pow).then_inc(rms2_ready, 1)
                    if j == 2 and there(2):
                        after(pool, ve1_ready, u - 1)
                        pool.tensor_tensor(rstd1[:], ve1[:], half[:, 0:TB], ALU.pow).then_inc(rstd1_ready, 1)

            turns(pool, 2, a_turn)

            after(pool, hctx_ready, B)
            ch(pool.memset(v_frame, 0.0))
            ch.settle()
            for b in range(2):
                last = pool.memset(diagonal(b)[:, :, :, HD], 1.0)
                if b == 0:
                    ch(last)
            last.then_inc(frames_clear, 1)

            def b_turn(u, parity, there):
                if there(0):
                    after(pool, x1_ready, u + 1)
                    after(pool, x1T_psum, u)
                    pool.tensor_copy(x1s[:], X[:, tile(u), :]).then_inc(x1s_ready, 1)
                for j in range(TB):
                    k = TB * u + j
                    if there(0):
                        after(pool, split_ready, k)
                        after(pool, high_ready, k + 1)
                        for side in range(2):
                            ch(pool.tensor_tensor(heads(qk_rest[:, side]), heads(qk_f[:, j % 2, side]),
                                                  slots(j, side, 4, 5)[:, :, 0, :], ALU.subtract))
                        ch.settle()
                        pool.tensor_tensor(QK[:, j, 1, :, 6 * HD + 3], ones[:, 0:H],
                                           mask_neg[:, batch(u, j)].broadcast_to((P, H)), ALU.mult)
                        for side, (first, end, by) in enumerate(((1, 4, 2), (0, 2, 1))):
                            for s in range(first, end, by):
                                ch(pool.tensor_scalar(slots(j, side, s, s + 1)[:, :, 0, :],
                                                      heads(qk_rest[:, side]), 1.0, None, ALU.mult))
                        ch.settle()
                        for side, low in enumerate((5, 2)):
                            last = pool.tensor_tensor(slots(j, side, low, low + 1)[:, :, 0, :], heads(qk_rest[:, side]),
                                                      slots(j, side, 1, 2)[:, :, 0, :], ALU.subtract)
                            if side == 0:
                                ch(last)
                        last.then_inc(split_ready, 1)
                    if j == 2 and there(2):
                        after(pool, ve2_ready, u - 1)
                        pool.tensor_tensor(rstd2[:], ve2[:], half[:, 0:TB], ALU.pow).then_inc(rstd2_ready, 1)

            turns(pool, 2, b_turn, ch, 2 * TB * 7)

            def c_turn(u, parity, there):
                for n in range(NC):
                    if n % FC == 2:
                        split_tile, e = prepared(n // FC)
                        if there(split_tile):
                            i = E * (u - split_tile) + e
                            after(pool, xe_ready, i + 1)
                            after(pool, h_psum, FC * (i - 3))
                            pool.tensor_tensor(spare_pool[:], half[:, 0:1], half[:, 0:1], ALU.mult)
                            pch(pool.tensor_scalar(x_hi[:, e % 4, :], xe[:, e % 2, :], 1.0, None, ALU.mult))
                            pch.settle()
                            pool.tensor_tensor(x_lo[:, e % 4, :], xe[:, e % 2, :], x_hi[:, e % 4, :],
                                               ALU.subtract).then_inc(xsplit_ready, 1)
                    if n == 7 and there(2):
                        after(pool, ve3_ready, u - 1)
                        pool.tensor_tensor(rstd3[:], ve3[:], half[:, 0:TB], ALU.pow).then_inc(rstd3_ready, 1)
                    if n == 15 and there(2):
                        after(pool, ve4_ready, u - 1)
                        pool.tensor_tensor(rstd4[:], ve4[:], half[:, 0:TB], ALU.pow).then_inc(rstd4_ready, 1)

            pch = ch
            turns(pool, 2, c_turn, ch, 2 * E)

        @block.tensor
        def _(pe):
            pe.wait_ge(consts, 9)
            pe.wait_ge(prep_dve, 1)
            pe.matmul(PS[:, 0, 0:4], ones[:], w_abs[:], start=True, stop=True).then_inc(prep_pe, 1)
            pe.transpose(PS[:, 1, 0:B], mask_f[:], ident[0:B, 0:B]).then_inc(prep_pe, 1)
            pe.wait_ge(prep_dve, 4)
            for n in range(4):
                last = pe.transpose(PS[:, 2, n * 64:n * 64 + 64].bitcast(BF16), w_int[:, n, :], ident16[:])
            last.then_inc(prep_pe, 1)
            pe.wait_ge(xw_in, 16 * 6)
            for n in range(3):
                last = pe.transpose(PS[:, 3, n * D:(n + 1) * D], W_raw[:, n, :], ident[:])
            last.then_inc(prep_pe, 1)
            pe.wait_ge(ffn_in, 16 * 10)
            pe.transpose(PS[:, 7, 0:E * FC], b1_rows[:], ident[0:E * FC, 0:E * FC]).then_inc(b1_psum, 1)
            pe.wait_ge(prep_dve, 7)
            for g in range(E * FC // 4):
                if g >= 1:
                    pe.wait_ge(w_split, g)
                for n in range(4):
                    pe.transpose(PS[:, 4, n * P:(n + 1) * P], W1_raw[:, 4 * g + n, :], ident[:])
                    last = pe.transpose(PS[:, 5, n * P:(n + 1) * P], W2_raw[:, g, n * P:(n + 1) * P], ident[:])
                last.then_inc(prep_pe, 1)
            pe.transpose(PS[:, 6, 0:E], Wr_raw[:], ident[0:E, 0:E]).then_inc(prep_pe, 1)

            pe.wait_ge(prep_act, 12)
            pe.wait_ge(w_split, E)

            def a_turn(u, parity, there):
                if there(0):
                    after(pe, xq_ready, u + 1)
                    after(pe, xqT_ready, u)
                    for i in range(TB):
                        last = pe.transpose(PS[:, 0, i * 64:i * 64 + 64].bitcast(BF16), xq[:, i, :], ident16[:])
                    last.then_inc(xqT_psum, 1)
                    after(pe, xqT_ready, u + 1)


                def project(j):
                    if there(0):
                        after(pe, qkv_ready, TB * u + j - 1)
                        pe.matmul(PS[:, 1 + j % 2, 0:3 * D], xqT[:, j, :],
                                  w_intT[:, 0:3, :].rearrange("p a d -> p (a d)"),
                                  start=True, stop=True).then_inc(qkv_psum, 1)

                project(0)
                project(1)
                if there(2):
                    after(pe, yq_ready, u - 1)
                    after(pe, yqT_ready, u - 2)
                    for i in range(TB):
                        last = pe.transpose(PS[:, 3, i * 64:i * 64 + 64].bitcast(BF16), yq[:, i, :], ident16[:])
                    last.then_inc(yqT_psum, 1)
                    after(pe, yqT_ready, u - 1)
                    after(pe, z1_ready, u - 2)
                    for i in range(TB):
                        last = pe.matmul(PS[:, 4, i * D:(i + 1) * D], yqT[:, i, :], w_intT[:, 3, :],
                                         start=True, stop=True)
                    last.then_inc(wo_psum, 1)
                project(2)
                project(3)

            turns(pe, 2, a_turn)

            after(pe, z1_ready, T)
            after(pe, qkv_ready, B)

            def b_turn(u, parity, there):
                if there(0):
                    after(pe, x1s_ready, u + 1)
                    after(pe, qT_ready, TB * u - 1)
                    for i in range(TB):
                        last = pe.transpose(PS[:, 4, i * P:(i + 1) * P], x1s[:, i, :], ident[:])
                    last.then_inc(x1T_psum, 1)
                    after_dma(pe, ctx_in, u + 1)
                    after(pe, kT_ready, TB * u - 1)
                    for i in range(TB):
                        last = pe.transpose(PS[:, 5, i * P:(i + 1) * P], cs[:, i, :], ident[:])
                    last.then_inc(cT_psum, 1)

                def spread(bank, j, side, ready):
                    for g in range(HG):
                        last = pe.transpose(PS[:, bank, g * 64:(g + 1) * 64].bitcast(BF16),
                                            QK[:, j, side, HR * g:HR * g + HR, :].rearrange("p h r -> p (h r)"),
                                            ident16[:])
                    last.then_inc(ready, 1)

                def half_scores(a, left, right, ready):
                    for g in range(HG // 2):
                        for r in range(HR):
                            rows = slice(HS * r, HS * r + HS)
                            last = pe.matmul(PS[:, 2 * a + r, g * P:(g + 1) * P], left[rows, HG // 2 * a + g, :],
                                             right[rows, HG // 2 * a + g, :], start=True, stop=True)
                    last.then_inc(ready, 1)

                for j in range(TB):
                    k = TB * u + j
                    l, i = divmod(j - 2, TB)
                    if there(-l):
                        after(pe, qT_ready, k - 1)
                        after(pe, kT_ready, k - 1)
                        for a in range(2):
                            after(pe, p_ready, 2 * (k - 5) + a + 1)
                            after(pe, max_done, 2 * (k - 3) + a + 1)
                            half_scores(a, QT[:, i % 2], KT[:, i], score_psum)
                    if there(0):
                        if j == 0:
                            after(pe, x1T_ready, u + 1)
                            after(pe, cT_ready, u + 1)
                        after(pe, qkv_copied, k)
                        pe.matmul(PS[:, 6, 0:D], x1T[:, j, :], W_T[:, 0, :], start=True, stop=True)
                        pe.matmul(PS[:, 6, D:3 * D], cT[:, j, :], W_T[:, 1:3, :].rearrange("p a d -> p (a d)"),
                                  start=True, stop=True).then_inc(proj_psum, 1)
                    if there(-((j - 6) // TB)):
                        after(pe, outT_ready, k - 5)
                        for a in range(2):
                            last = pe.transpose(PS[:, 7, a * HO:(a + 1) * HO], outT[:, a * P:(a + 1) * P],
                                                ident[0:HO, 0:HO])
                        last.then_inc(out_psum, 1)
                    l, i = divmod(j - 3, TB)
                    if there(-l):
                        after(pe, m_ready, k - 2)
                        after(pe, qT_ready, k - 1 if there(-((j - 2) // TB)) else B)
                        after(pe, qmT_ready, k - 3)
                        spread(4, i, 0, qmT_psum)
                    l, i = divmod(j - 1, TB)
                    if there(-l):
                        after(pe, split_ready, k)
                        after(pe, kT_ready, k - 1)
                        spread(5, i, 1, kT_psum)

                    def half_outputs(a):
                        l, i = divmod(j - 5, TB)
                        if there(-l):
                            after(pe, p_ready, 2 * (k - 5) + a + 1)
                            after(pe, att_ready, k - 5)
                            after(pe, v_ready, k - 4)
                            for n in range(8):
                                last = pe.matmul(PS[0:HO, 7, a * P:(a + 1) * P], v_frame[:, i % 2, a, HO * n:HO * (n + 1)],
                                                 PT[:, i % 2, 8 * a + n, :], start=(n == 0), stop=(n == 7))
                            if a == 1:
                                last.then_inc(pv_psum, 1)

                    def half_shifted(a):
                        l, i = divmod(j - 4, TB)
                        if there(-l):
                            after(pe, qmT_ready, k - 3)
                            after(pe, max_done, 2 * (k - 2) + a + 1 if there(-((j - 2) // TB)) else 2 * B)
                            after(pe, p_ready, 2 * (k - 5) + a + 1)
                            half_scores(a, KT[:, i], QmT[:, i % 2], scoreT_psum)

                    half_outputs(0)
                    half_shifted(0)
                    l, i = divmod(j - 1, TB)
                    if there(-l):
                        after(pe, qmT_ready, k - 2)
                        spread(4, i, 0, qT_psum)
                    half_shifted(1)
                    half_outputs(1)

            turns(pe, 2, b_turn)

            after(pe, att_ready, B)

            def c_turn(u, parity, there):
                def down(n, lag):
                    i = NC * (u - lag) + n
                    after(pe, h_lo_ready, i + 1)
                    o = PS[:, 4 + (parity - lag) % 2, :]
                    pe.matmul(o, W2_hi[:, n, :], h_hi[:, n % 4, :], start=False, stop=False)
                    pe.matmul(o, W2_hi[:, n, :], h_lo[:, n % 4, :], start=False, stop=False)
                    pe.matmul(o, W2_lo[:, n, :], h_hi[:, n % 4, :], start=False,
                              stop=(n == NC - 1)).then_inc(down_done, 1)

                for n in range(NC):
                    if n == 0 and there(1):
                        after(pe, oT_ready, u - 2)
                        for a in range(3):
                            pe.matmul(PS[:, 4 + (parity - 1) % 2, :], b2_parts[:, a, :], rwT[:, (parity - 1) % 2, :],
                                      start=(a == 0), stop=False)
                    if there(1):
                        i = NC * (u - 1) + n
                        e = n // FC
                        if n % FC == 0:
                            after(pe, xsplit_ready, E * (u - 1) + e + 1)
                        after(pe, h_lo_ready, i - 3)
                        pe.matmul(PS[:, n % 4, :], W1_hi[:, n, :], x_hi[:, e % 4, :], start=True, stop=False)
                        pe.matmul(PS[:, n % 4, :], W1_hi[:, n, :], x_lo[:, e % 4, :], start=False, stop=False)
                        pe.matmul(PS[:, n % 4, :], W1_lo[:, n, :], x_hi[:, e % 4, :], start=False,
                                  stop=True).then_inc(h_psum, 1)
                    if n < 2:
                        if there(2):
                            down(NC - 2 + n, 2)
                    elif there(1):
                        down(n - 2, 1)
                    if n % FC == 1:
                        lag, e = prepared(n // FC)
                        if there(lag):
                            i = E * (u - lag) + e
                            if lag == 0 and e == 0:
                                after(pe, rwT_ready, u + 1)
                            after(pe, xe_ready, i)
                            pe.matmul(PS[:, 6, :], sel[:, e, :], rwT[:, (parity - lag) % 2, :],
                                      start=True, stop=True).then_inc(rwb_psum, 1)
                    if n == 4 and there(2):
                        after(pe, oT_ready, u - 1)
                        after(pe, rwT_ready, u if there(1) else T)
                        for i in range(TB):
                            last = pe.transpose(PS[:, 7, i * D:(i + 1) * D], oT[:, i * P:(i + 1) * P], ident[:])
                        last.then_inc(y3_psum, 1)
                    if n == 8 and there(0):
                        after(pe, xa_ready, u + 1)
                        after(pe, z3_ready, u - 1)
                        after(pe, rwT_ready, u)
                        for i in range(TB):
                            last = pe.transpose(PS[:, 7, i * P:(i + 1) * P], xa[:, i, :], ident[:])
                        last.then_inc(xaT_psum, 1)
                    if n == 11 and there(0):
                        after(pe, xaT_ready, u + 1)
                        for i in range(TB):
                            last = pe.matmul(PS[:, 7, i * E:(i + 1) * E], xaT[:, parity, i * P:(i + 1) * P], Wr_T[:],
                                             start=True, stop=True)
                        last.then_inc(lg_psum, 1)
                    if n == 22 and there(0):
                        after(pe, rw_ready, u + 1)
                        for i in range(TB):
                            last = pe.transpose(PS[0:3 * E, 7, i * 64:(i + 1) * 64].bitcast(BF16),
                                                rw16[:, i, :, :].rearrange("p a e -> p (a e)"), ident16[:])
                        last.then_inc(rwT_psum, 1)

            turns(pe, 2, c_turn)

        @block.scalar
        def _(act):
            act.wait_ge(x_in, 64)
            act.activation(sq_all[:], X[:], ACT.Square).then_inc(prep_act, 1)
            act.wait_ge(prep_pe, 3)
            act.copy(w_intT[:].rearrange("p a d -> p (a d)"), PS[:, 2, 0:256].bitcast(BF16)).then_inc(prep_act, 1)
            act.wait_ge(prep_pe, 4)
            act.copy(W_T[:].rearrange("p a d -> p (a d)"), PS[:, 3, 0:3 * D]).then_inc(prep_act, 1)
            for g in range(E):
                act.wait_ge(prep_pe, 5 + g)
                act.activation(W1_hi[:, FC * g:FC * g + FC, :].rearrange("p a d -> p (a d)"), PS[:, 4, :], ACT.Copy,
                               scale=w_scale[:, 0:1])
                act.activation(W2_hi[:, FC * g:FC * g + FC, :].rearrange("p a d -> p (a d)"), PS[:, 5, :], ACT.Copy,
                               scale=w_scale[:, 1:2]).then_inc(prep_act, 1)
            act.wait_ge(prep_pe, 13)
            act.copy(Wr_T[:], PS[:, 6, 0:E]).then_inc(prep_act, 1)

            act.wait_ge(prep_dve, 6)

            def a_turn(u, parity, there):
                if there(0):
                    after(act, xqT_psum, u + 1)
                    after(act, qkv_psum, TB * u)
                    act.copy(xqT[:].rearrange("p a d -> p (a d)"), PS[:, 0, 0:256].bitcast(BF16)).then_inc(xqT_ready, 1)
                for j in range(TB):
                    if there(0):
                        k = TB * u + j
                        after(act, qkv_psum, k + 1)
                        after(act, av_prod, k - 1)
                        act.copy(qkv[:, j % 2, :], PS[:, 1 + j % 2, 0:3 * D]).then_inc(qkv_ready, 1)
                    l, i = divmod(j - 1, TB)
                    l = -l
                    if there(l):
                        b = TB * (u - l) + i
                        after(act, s1_ready, b + 1)
                        after(act, av_prod, b - 1)
                        act.activation(E1[:, i % 2, :], S1d[:, i % 2, :], ACT.Exp,
                                       scale=c_qk[:, batch(u - l, i)]).then_inc(e1_ready, 1)
                    if j == 3 and there(1):
                        after_dma(act, y_in, TB * u)
                        after(act, ms2_ready, u - 1)
                        act.activation(ysq[:], Y[:, tile(u - 1), :], ACT.Square).then_inc(ysq_ready, 1)
                    if j == 1 and there(2):
                        after(act, yqT_psum, u - 1)
                        after(act, wo_psum, u - 2)
                        act.copy(yqT[:].rearrange("p a d -> p (a d)"), PS[:, 3, 0:256].bitcast(BF16)).then_inc(yqT_ready, 1)

            turns(act, 2, a_turn)
            after(act, frames_clear, 1)

            def b_turn(u, parity, there):
                if there(0):
                    after(act, x1T_psum, u + 1)
                    after(act, proj_psum, TB * u)
                    act.copy(x1T[:].rearrange("p a d -> p (a d)"), PS[:, 4, :]).then_inc(x1T_ready, 1)
                    after(act, cT_psum, u + 1)
                    act.copy(cT[:].rearrange("p a d -> p (a d)"), PS[:, 5, :]).then_inc(cT_ready, 1)
                for j in range(TB):
                    k = TB * u + j
                    if there(-((j - 6) // TB)):
                        after(act, pv_psum, k - 5)
                        act.copy(outT, PS[0:HO, 7, 0:2 * P]).then_inc(outT_ready, 1)
                    if there(0):
                        after(act, qkv_copied, k + 1)
                        after(act, qmT_psum, k - 3)
                        act.copy(slots(j, 0, 0, 5, 2), heads(qk_f[:, j % 2, 0]).unsqueeze(2).broadcast_to((P, H, 3, HD)))
                        act.copy(slots(j, 1, 3, 6), heads(qk_f[:, j % 2, 1]).unsqueeze(2).broadcast_to((P, H, 3, HD))
                                 ).then_inc(high_ready, 1)
                    l, i = divmod(j - 3, TB)
                    if there(-l):
                        after(act, qmT_psum, k - 2)
                        act.copy(QmT[:, i % 2].rearrange("p a d -> p (a d)"), PS[:, 4, :].bitcast(BF16)
                                 ).then_inc(qmT_ready, 1)

                    def half_exp(a):
                        l, i = divmod(j - 4, TB)
                        if there(-l):
                            after(act, scoreT_psum, 2 * (k - 4) + a + 1)
                            act.activation(half_heads(PT[:, i % 2], a), banks(a).rearrange("p r (g q) -> p r g q", q=P),
                                           ACT.Exp, scale=HD ** -0.5).then_inc(p_ready, 1)

                    half_exp(0)
                    l, i = divmod(j - 1, TB)
                    if there(-l):
                        after(act, qT_psum, k)
                        after(act, score_psum, 2 * (k - 2))
                        act.copy(QT[:, i % 2].rearrange("p a d -> p (a d)"), PS[:, 4, :].bitcast(BF16)
                                 ).then_inc(qT_ready, 1)
                    half_exp(1)
                    l, i = divmod(j - 4, TB)
                    if there(-l):
                        after(act, qkv_copied, k - 3)
                        act.copy(diagonal(i % 2)[:, :, :, 0:HD],
                                 Va[:, (TB * parity + j - 4) % 8].rearrange("p (a n d) -> p a n d", a=2, n=8)
                                 ).then_inc(v_ready, 1)

            turns(act, 2, b_turn)

            def c_turn(u, parity, there):
                for n in range(NC):
                    if there(1):
                        i = NC * (u - 1) + n
                        after(act, h_psum, i + 1)
                        after(act, down_done, i - 3)
                        act.activation(h_hi[:, n % 4, :], PS[:, n % 4, :], ACT.Relu).then_inc(h_hi_ready, 1)
                    if n == 2 and there(2):
                        after(act, down_done, NC * (u - 1))
                        after(act, y3_psum, u - 2)
                        act.activation(oT, PS[:, 4 + parity, :], ACT.Copy, scale=o_scale[:]).then_inc(oT_ready, 1)
                    if n == 9 and there(0):
                        after(act, xaT_psum, u + 1)
                        after(act, xe_ready, E * (u - 1))
                        act.activation(xaT[:, parity, :], PS[:, 7, :], ACT.Copy, scale=X_SCALE).then_inc(xaT_ready, 1)
                    if n == 17 and there(0):
                        after(act, gap_ready, u + 1)
                        act.activation(eg[:], gap[:], ACT.Exp, scale=1 / X_SCALE).then_inc(eg_ready, 1)
                    if n == 23 and there(0):
                        after(act, rwT_psum, u + 1)
                        act.copy(rwT[:, parity, :], PS[0:3 * E, 7, 0:256].bitcast(BF16)).then_inc(rwT_ready, 1)

            turns(act, 2, c_turn)

        @block.vector
        def _(dve):
            ch = Chain(dve, dve_chain)
            step, settle = ch, ch.settle

            def settle_apart():
                settle()
                dve.memset(spare[:], 0.0)

            dve.wait_ge(w_in, 16 * 5)
            step(dve.tensor_copy(mask_f[:], mask8[:]))
            settle()
            dve.tensor_reduce(w_abs[:], w_raw[:], AX.X, ALU.add, apply_absolute_value=True).then_inc(prep_dve, 1)
            dve.wait_ge(x_in, 64)
            dve.tensor_reduce(amax1[:], X[:], AX.X, ALU.max, apply_absolute_value=True).then_inc(prep_dve, 1)
            dve.wait_ge(prep_act, 1)
            step(dve.tensor_reduce(ssq1[:], sq_all[:], AX.X, ALU.add))
            settle()
            dve.tensor_scalar(ssq1[:], ssq1[:], 1.0 / D, 1e-6, ALU.mult, ALU.add).then_inc(prep_dve, 1)
            dve.wait_ge(prep_pe, 2)
            step(dve.tensor_scalar(w_mean[:], PS[:, 0, 0:4], 1.0 / (D * D), 1e-5, ALU.mult, ALU.max))
            step(dve.tensor_scalar(mask_neg[:], PS[:, 1, 0:B], NEG, None, ALU.mult))
            settle()
            step(dve.reciprocal(w_inv[:], w_mean[:]))
            settle()
            step(dve.tensor_tensor(w_t[:], w_raw[:], bc(w_inv[:], D), ALU.mult))
            settle()
            step(dve.tensor_scalar(w_t[:], w_t[:], ROUND, -ROUND, ALU.add, ALU.add))
            settle()
            dve.tensor_scalar(w_int[:], w_t[:], 1.0, -1.0, ALU.min, ALU.max).then_inc(prep_dve, 1)
            dve.wait_ge(prep_pool, 1)
            step(dve.tensor_tensor(clip1[:], amax1[:], rms1[:], ALU.mult))
            settle()
            step(dve.tensor_scalar(clip1[:], clip1[:], 1e-5, None, ALU.max))
            settle()
            step(dve.reciprocal(rec1[:], clip1[:]))
            step(dve.tensor_scalar(inv1[:], clip1[:], 1.0 / 127, None, ALU.mult))
            step(dve.tensor_tensor(w_qk[:], w_mean[:, 0:1], w_mean[:, 1:2], ALU.mult))
            settle()
            dve.tensor_scalar(s1[:], rec1[:], 127.0, None, ALU.mult).then_inc(prep_dve, 1)
            step(dve.tensor_tensor(inv1sq[:], inv1[:], inv1[:], ALU.mult))
            step(dve.tensor_scalar(c_v[:], inv1[:], w_mean[:, 2:3], None, ALU.mult))
            settle()
            dve.tensor_scalar(c_qk[:], inv1sq[:], w_qk[:], HD ** -0.5, ALU.mult, ALU.mult).then_inc(prep_dve, 1)
            dve.wait_ge(ffn_in, 16 * 10)
            step(dve.tensor_tensor(W1_raw[:, :, 0:D - 1], W1_raw[:, :, 0:D - 1],
                                   W1_raw[:, :, D - 1:D].broadcast_to((P, E * FC, D - 1)), ALU.subtract))
            step(dve.tensor_scalar(Wr_raw[:, 0:D - 1], Wr_raw[:, 0:D - 1], Wr_raw[:, D - 1:D], None, ALU.subtract))
            settle()
            step(dve.tensor_copy(Wr_raw[:, D - 1:D], br_col[:]))
            dve.wait_ge(b1_psum, 1)
            step(dve.tensor_copy(W1_raw[:, :, D - 1], PS[:, 7, 0:E * FC]))
            settle()
            step(dve.tensor_reduce(w_top_abs[:, 0:1], W1_raw[:].rearrange("p a d -> p (a d)"), AX.X, ALU.max,
                                   apply_absolute_value=True))
            step(dve.tensor_reduce(w_top_abs[:, 1:2], W2_raw[:].rearrange("p a d -> p (a d)"), AX.X, ALU.max,
                                   apply_absolute_value=True))
            settle()
            dve.tensor_scalar(w_top_abs[:], w_top_abs[:], 1e-12, None, ALU.max).then_inc(w_abs_ready, 1)
            dve.wait_ge(prep_pool, 2)
            scale_bits, top_bits = w_scale[:].bitcast(I32), w_top_abs[:].bitcast(I32)
            step(dve.tensor_scalar(top_bits, top_bits, 0xFF << 23, None, ALU.bitwise_and))
            settle()
            for n, target in enumerate((4, 9)):
                step(dve.tensor_scalar(scale_bits[:, n:n + 1], top_bits[:, n:n + 1], -1.0,
                                       float((254 + target) << 23), ALU.mult, ALU.add))
            settle()
            step(dve.tensor_scalar(b2_scale[:], w_scale[:, 0:1], w_scale[:, 1:2], X_SCALE, ALU.mult, ALU.mult))
            settle()
            step(dve.reciprocal(o_scale[:], b2_scale[:]))
            step(dve.tensor_scalar(b2_rep[:], b2_rep[:], b2_scale[0:3 * E, :], None, ALU.mult))
            settle()
            step(dve.tensor_copy(b2_parts[:, 0, :], b2_rep[:]))
            settle()
            step(dve.tensor_tensor(b2_rest[:, 0, :], b2_rep[:], b2_parts[:, 0, :], ALU.subtract))
            settle()
            step(dve.tensor_copy(b2_parts[:, 1, :], b2_rest[:, 0, :]))
            settle()
            step(dve.tensor_tensor(b2_rest[:, 1, :], b2_rest[:, 0, :], b2_parts[:, 1, :], ALU.subtract))
            settle()
            dve.tensor_copy(b2_parts[:, 2, :], b2_rest[:, 1, :]).then_inc(prep_dve, 1)
            for g in range(E):
                dve.wait_ge(prep_act, 4 + g)
                for n, (hi, lo) in enumerate(((W1_hi, W1_lo), (W2_hi, W2_lo))):
                    last = dve.scalar_tensor_tensor(lo[:, FC * g:FC * g + FC, :].rearrange("p a d -> p (a d)"),
                                                    PS[:, 4 + n, :], w_scale[:, n:n + 1],
                                                    hi[:, FC * g:FC * g + FC, :].rearrange("p a d -> p (a d)"),
                                                    ALU.mult, ALU.subtract)
                    if n == 0:
                        step(last)
                last.then_inc(w_split, 1)
            dve.wait_ge(prep_dve, 7)

            def norm_stats(z, bn, mv, ve, ready):
                for i in range(TB):
                    step(dve.bn_stats(bn[:, i, :], z[:, i, :]))
                settle_apart()
                for i in range(TB):
                    step(dve.bn_aggr(mv[:, i, :], bn[:, i, :]))
                settle()
                dve.tensor_scalar(ve[:], mv[:, :, 1], 1e-5, None, ALU.add).then_inc(ready, 1)

            def norm_apply(o, z, mv, rstd):
                for i in range(TB):
                    last = dve.tensor_scalar(o(i), z[:, i, :], mv[:, i, 0:1], rstd[:, i:i + 1], ALU.subtract, ALU.mult)
                    if i < TB - 1:
                        step(last)
                return last

            def a_turn(u, parity, there):
                if there(0):
                    after(dve, xqT_psum, u)
                    step(dve.tensor_tensor(xq_f[:], X[:, tile(u), :], bc(rms1[:, tile(u)], D), ALU.mult))
                    settle()
                    step(dve.tensor_tensor(xq_g[:], xq_f[:], bc(s1[:, tile(u)], D), ALU.mult))
                    settle()
                    dve.tensor_scalar(xq[:], xq_g[:], ROUND, -ROUND, ALU.add, ALU.add).then_inc(xq_ready, 1)
                for j in range(TB):
                    k = TB * u + j
                    l1, i1 = divmod(j - 1, TB)
                    if there(-l1):
                        after(dve, qk_prod, k)
                        after(dve, e1_ready, k - 2)
                        step(dve.tensor_reduce(S1[:, i1 % 2, :], prod1[:, i1 % 2, :].rearrange("p (a d) -> p a d", d=HD),
                                               AX.X, ALU.add))
                        settle()
                        s = S1[:, i1 % 2, :].rearrange("p (h t) -> p h t", h=H)
                        step(dve.tensor_reduce(S1m[:, i1 % 2, :], s, AX.X, ALU.max))
                        settle()
                        dve.tensor_tensor(S1d[:, i1 % 2, :].rearrange("p (h t) -> p h t", h=H), s,
                                          bc(S1m[:, i1 % 2, :], H), ALU.subtract).then_inc(s1_ready, 1)
                    l2, i2 = divmod(j - 2, TB)
                    if there(-l2):
                        after(dve, av_prod, k - 1)
                        after_dma(dve, shuffled, k - 3)
                        step(dve.tensor_reduce(hctx_f[:, i2 % 2, :], prod2[:, i2 % 2, :].rearrange("p (a t) -> p a t", t=H),
                                               AX.X, ALU.add))
                        settle()
                        dve.scalar_tensor_tensor(hctx[:, i2 % 2, :].rearrange("p (h d) -> p h d", h=H),
                                                 hctx_f[:, i2 % 2, :].rearrange("p (h d) -> p h d", h=H),
                                                 c_v[:, batch(u + l2, i2)], bc(E1inv[:, i2, :], HD),
                                                 ALU.mult, ALU.mult).then_inc(hctx_ready, 1)
                    if there(-l1):
                        after(dve, e1_ready, k)
                        step(dve.tensor_reduce(E1sum[:, i1 % 2, :], E1[:, i1 % 2, :].rearrange("p (h t) -> p h t", h=H),
                                               AX.X, ALU.add))
                        settle()
                        step(dve.reciprocal(E1inv[:, i1, :], E1sum[:, i1 % 2, :]))
                    if j == 3 and there(1):
                        after_dma(dve, y_in, TB * u)
                        step(dve.tensor_reduce(amax2[:], Y[:, tile(u - 1), :], AX.X, ALU.max, apply_absolute_value=True))
                        after(dve, ysq_ready, u)
                        step(dve.tensor_reduce(ssq2[:], ysq[:], AX.X, ALU.add))
                        settle()
                        dve.tensor_scalar(ms2[:], ssq2[:], 1.0 / D, 1e-6, ALU.mult, ALU.add).then_inc(ms2_ready, 1)
                    if j == 0 and there(2):
                        after(dve, rms2_ready, u - 1)
                        after(dve, yqT_psum, u - 2)
                        step(dve.tensor_tensor(clip2[:], amax2[:], rms2[:], ALU.mult))
                        step(dve.tensor_tensor(yq_f[:], Y[:, tile(u - 2), :], bc(rms2[:], D), ALU.mult))
                        settle()
                        step(dve.tensor_scalar(clip2[:], clip2[:], 1e-5, None, ALU.max))
                        settle()
                        step(dve.reciprocal(rec2[:], clip2[:]))
                        step(dve.tensor_scalar(f2[:], clip2[:], 1.0 / 127, w_mean[:, 3:4], ALU.mult, ALU.mult))
                        settle()
                        step(dve.tensor_scalar(s2[:], rec2[:], 127.0, None, ALU.mult))
                        settle()
                        step(dve.tensor_tensor(yq_g[:], yq_f[:], bc(s2[:], D), ALU.mult))
                        settle()
                        dve.tensor_scalar(yq[:], yq_g[:], ROUND, -ROUND, ALU.add, ALU.add).then_inc(yq_ready, 1)
                    if j == 2 and there(2):
                        after(dve, wo_psum, u - 1)
                        dve.tensor_tensor(z1r[:], PS[:, 4, :].rearrange("p (a d) -> p a d", a=TB),
                                          bc(f2[:], D), ALU.mult).then_inc(z1_ready, 1)
                        after(dve, z1_ready, u - 1)
                        step(dve.tensor_tensor(z1[:], z1r[:], X[:, tile(u - 2), :], ALU.add))
                        settle()
                        norm_stats(z1, bn1, mv1, ve1, ve1_ready)
                    if j == 3 and there(2):
                        after(dve, rstd1_ready, u - 1)
                        norm_apply(lambda i: X[:, batch(u - 2, i), :], z1, mv1, rstd1).then_inc(x1_ready, 1)

            turns(dve, 2, a_turn, ch, A_STEPS)

            def b_turn(u, parity, there):
                for j in range(TB):
                    k = TB * u + j

                    def half_max(a):
                        if there(-((j - 2) // TB)):
                            after(dve, score_psum, 2 * (k - 2) + a + 1)
                            dve.tensor_reduce(half_heads(m2[:], a), banks(a).rearrange("p r (g t) -> p r g t", t=P),
                                              AX.X, ALU.max).then_inc(max_done, 1)

                    half_max(0)
                    if there(0):
                        after(dve, proj_psum, k + 1)
                        after(dve, v_ready, k - 7)
                        after(dve, split_ready, k - 1)
                        p = PS[:, 6, 0:3 * D].rearrange("p (a d) -> p a d", a=3)
                        step(dve.tensor_tensor(Va[:, TB * parity + j], p[:, 2], b_qkv[:, 2], ALU.add))
                        dve.tensor_tensor(qk_f[:, j % 2], p[:, 0:2], b_qkv[:, 0:2], ALU.add).then_inc(qkv_copied, 1)
                    l, i = divmod(j - 6, TB)
                    if there(-l):
                        after(dve, out_psum, k - 5)
                        o = PS[:, 7, 0:H * (HD + 1)].rearrange("p (h d) -> p h d", h=H)
                        step(dve.tensor_scalar(sum2[:], o[:, :, HD], 1e-30, None, ALU.max))
                        settle()
                        step(dve.reciprocal(rsum2[:], sum2[:]))
                        settle()
                        dve.tensor_tensor(att2[:, i, :].rearrange("p (h d) -> p h d", h=H), o[:, :, 0:HD],
                                          bc(rsum2[:], HD), ALU.mult).then_inc(att_ready, 1)
                    half_max(1)
                    l, i = divmod(j - 1, TB)
                    if there(-l):
                        after(dve, kT_psum, k)
                        after(dve, scoreT_psum, 2 * (k - 4))
                        dve.tensor_copy(KT[:, i].rearrange("p a d -> p (a d)"), PS[:, 5, :].bitcast(BF16)
                                        ).then_inc(kT_ready, 1)
                    l, i = divmod(j - 2, TB)
                    if there(-l):
                        after(dve, max_done, 2 * (k - 1))
                        parts3 = QK[:, i, 0, :, 6 * HD:6 * HD + 3]
                        step(dve.tensor_scalar(m_neg[:], m2[:], -1.0, -0.1 * NEG, ALU.mult, ALU.min))
                        settle()
                        step(dve.tensor_copy(parts3[:, :, 0], m_neg[:]))
                        settle()
                        step(dve.tensor_tensor(m_rest[:, 0], m_neg[:], parts3[:, :, 0], ALU.subtract))
                        settle()
                        step(dve.tensor_copy(parts3[:, :, 1], m_rest[:, 0]))
                        settle()
                        dve.tensor_tensor(parts3[:, :, 2], m_rest[:, 0], parts3[:, :, 1], ALU.subtract
                                          ).then_inc(m_ready, 1)
                    if j == 1 and there(2):
                        after(dve, att_ready, TB * (u - 1))
                        step(dve.tensor_tensor(z2[:], att2[:], X[:, tile(u - 2), :], ALU.add))
                        settle()
                        norm_stats(z2, bn2, mv2, ve2, ve2_ready)
                    if j == 3 and there(2):
                        after(dve, rstd2_ready, u - 1)
                        norm_apply(lambda i: X[:, batch(u - 2, i), :], z2, mv2, rstd2).then_inc(x2_ready, 1)

            turns(dve, 2, b_turn, ch, B_STEPS)

            after(dve, x2_ready, T)
            gb = gam[:].unsqueeze(1).broadcast_to((P, TB, D))
            be = bet[:].unsqueeze(1).broadcast_to((P, TB, D))

            def c_turn(u, parity, there):
                for n in range(NC):
                    if there(1):
                        after(dve, h_hi_ready, NC * (u - 1) + n + 1)
                        dve.scalar_tensor_tensor(h_lo[:, n % 4, :], PS[:, n % 4, :], 0.0, h_hi[:, n % 4, :],
                                                 ALU.max, ALU.subtract).then_inc(h_lo_ready, 1)
                    if n % FC == 1:
                        lag, e = prepared(n // FC)
                        if there(lag):
                            i = E * (u - lag) + e
                            after(dve, rwb_psum, i + 1)
                            after(dve, xsplit_ready, i - 1)
                            dve.tensor_tensor(xe[:, e % 2, :], xaT[:, (parity - lag) % 2, :], PS[:, 6, :],
                                              ALU.mult).then_inc(xe_ready, 1)
                    if n == 0 and there(0):
                        after(dve, xaT_psum, u)
                        dve.tensor_copy(xa[:, :, 0:D - 1], X[:, tile(u), 0:D - 1]).then_inc(xa_ready, 1)
                    if n == 14 and there(0):
                        after(dve, lg_psum, u + 1)
                        step(dve.tensor_copy(lg[:].rearrange("p a e -> p (a e)"), PS[:, 7, 0:TB * E]))
                        settle_apart()
                        for i in range(TB):
                            step(dve.max(top[:, i, :], lg[:, i, :]))
                        settle()
                        dve.tensor_tensor(gap[:], top[:, :, 1], top[:, :, 0], ALU.subtract).then_inc(gap_ready, 1)
                    if n == 15 and there(0):
                        for i in range(TB):
                            step(dve.max_index(topi[:, i, :], top[:, i, :], lg[:, i, :]))
                        settle()
                        step(dve.tensor_copy(topf[:], topi[:]))
                        settle()
                        for a in range(2):
                            step(dve.tensor_tensor(oh[:, a], eiota[:], topf[:, :, a:a + 1].broadcast_to((P, TB, E)),
                                                   ALU.is_equal))
                    if n == 18 and there(0):
                        after(dve, eg_ready, u + 1)
                        step(dve.tensor_scalar(eg1[:], eg[:], 1.0, None, ALU.add))
                        settle()
                        step(dve.reciprocal(w_top[:, 0, :], eg1[:]))
                        settle()
                        step(dve.tensor_tensor(w_top[:, 1, :], eg[:], w_top[:, 0, :], ALU.mult))
                        step(dve.tensor_tensor(oh[:, 0], oh[:, 0], bc(w_top[:, 0, :], E), ALU.mult))
                        settle()
                        step(dve.tensor_tensor(oh[:, 1], oh[:, 1], bc(w_top[:, 1, :], E), ALU.mult))
                        settle()
                        step(dve.tensor_tensor(rw[:], oh[:, 0], oh[:, 1], ALU.add))
                        settle()
                    if n == 19 and there(0):
                        step(dve.tensor_copy(rw16[:, :, 0, :], rw[:]))
                        settle()
                        step(dve.tensor_tensor(rw_rest[:, 0], rw[:], rw16[:, :, 0, :], ALU.subtract))
                        settle()
                        step(dve.tensor_copy(rw16[:, :, 1, :], rw_rest[:, 0]))
                        settle()
                        step(dve.tensor_tensor(rw_rest[:, 1], rw_rest[:, 0], rw16[:, :, 1, :], ALU.subtract))
                        settle()
                        dve.tensor_copy(rw16[:, :, 2, :], rw_rest[:, 1]).then_inc(rw_ready, 1)
                    if n == 5 and there(2):
                        after(dve, y3_psum, u - 1)
                        dve.tensor_tensor(z3[:], PS[:, 7, :].rearrange("p (a d) -> p a d", a=TB), X[:, tile(u - 2), :],
                                          ALU.add).then_inc(z3_ready, 1)
                        after(dve, z3_ready, u - 1)
                        norm_stats(z3, bn3, mv3, ve3, ve3_ready)
                    if n == 9 and there(2):
                        after(dve, rstd3_ready, u - 1)
                        step(norm_apply(lambda i: n3[:, i, :], z3, mv3, rstd3))
                        settle()
                    if n == 10 and there(2):
                        step(dve.tensor_tensor(g3[:], n3[:], gb, ALU.mult))
                        settle()
                    if n == 11 and there(2):
                        step(dve.tensor_tensor(n3[:], g3[:], be, ALU.add))
                        settle()
                    if n == 12 and there(2):
                        step(dve.tensor_tensor(z4[:], n3[:], X[:, tile(u - 2), :], ALU.add))
                        settle()
                        norm_stats(z4, bn4, mv4, ve4, ve4_ready)
                    if n == 16 and there(2):
                        after(dve, rstd4_ready, u - 1)
                        after_dma(dve, stored, u - 2)
                        norm_apply(lambda i: o4[:, i, :], z4, mv4, rstd4).then_inc(o4_ready, 1)

            turns(dve, 2, c_turn, ch, C_STEPS)


_INS = ["x", "ctx_1024", "mask_BxS2_bf0", "L0_attn_wq", "L0_attn_wk", "L0_attn_wv", "L0_attn_wo",
        "L0_xattn_Wq", "L0_xattn_bq", "L0_xattn_Wk", "L0_xattn_bk", "L0_xattn_Wv", "L0_xattn_bv",
        "L0_ffn_Wr", "L0_ffn_br", "L0_ffn_W1", "L0_ffn_b1", "L0_ffn_W2", "L0_ffn_b2", "L0_ffn_gamma", "L0_ffn_beta"]


def kernel(**inputs):
    import numpy as _np
    import concourse.bacc as _bacc
    from concourse import mybir as _mybir
    from concourse.bass_utils import run_bass_kernel_spmd as _run

    nc = _bacc.Bacc("TRN2", target_bir_lowering=False, num_devices=1)
    arrays, args = {}, []
    for name in _INS:
        a = _np.ascontiguousarray(inputs[name])
        arrays[f"in_{name}_dram"] = a
        args.append(nc.dram_tensor(f"in_{name}_dram", a.shape, _mybir.dt.from_np(a.dtype), kind="ExternalInput").ap())
    args.append(nc.dram_tensor("out_dram", inputs["x"].shape, _mybir.dt.float32, kind="ExternalOutput").ap())
    decoder_layer(nc, *args)
    r = _run(nc, [arrays], core_ids=[0])
    return r.results[0]["out_dram"]
```

```python
from contextlib import ExitStack

import concourse.bass as bass
from concourse import mybir


def decoder_layer(nc, x, ctx_1024, mask, wq, wk, wv, wo, Wq, bq, Wk, bk, Wv, bv,
                  Wr, br, W1, b1, W2, b2, gamma, beta, out):
    F32, BF16, F16 = mybir.dt.float32, mybir.dt.bfloat16, mybir.dt.float16
    U8, U32, I32 = mybir.dt.uint8, mybir.dt.uint32, mybir.dt.int32
    ALU, ACT, AX = mybir.AluOpType, mybir.ActivationFunctionType, mybir.AxisListType

    B, P, D = x.shape
    H, HD = 16, D // 16
    E, F = W1.shape[0], W1.shape[1]
    FC = F // P
    TB = 4
    T = B // TB
    NT = TB * P
    HS = 64
    HR = P // HS
    HG = H // HR
    X_SCALE = 8.0
    HP = 11
    NEG = -1e30
    ROUND = 1.5 * 2.0 ** 23
    A_STEPS, B_STEPS, C_STEPS = 98, 80, 96
    LATE = 3
    CREDIT = 16

    ctx = ExitStack()
    with ctx:
        def sb(name, shape, dt=F32):
            return ctx.enter_context(nc.sbuf_tensor(name, shape, dt))

        counters = []

        def sem(name):
            s = ctx.enter_context(nc.semaphore(name))
            counters.append(s)
            return s

        def after(eng, s, n):
            eng.wait_ge(s, n + CREDIT)

        def after_dma(eng, s, n):
            eng.wait_ge(s, 16 * (n + CREDIT))

        class Chain:

            def __init__(self, eng, s):
                self.eng, self.s, self.n, self.turn = eng, s, 0, 0

            def __call__(self, instruction):
                instruction.then_inc(self.s, 1)
                self.n += 1

            def settle(self):
                self.eng.wait_ge(self.s, self.n + self.turn)

        X = sb("X", [P, B, D])
        Y = sb("Y", [P, B, D])
        w_raw = sb("w_raw", [P, 4, D])
        w_abs = sb("w_abs", [P, 4])
        w_mean = sb("w_mean", [P, 4])
        w_inv = sb("w_inv", [P, 4])
        w_t = sb("w_t", [P, 4, D])
        w_int = sb("w_int", [P, 4, D], BF16)
        w_intT = sb("w_intT", [P, 4, D], BF16)
        W_raw = sb("W_raw", [P, 3, D])
        W_T = sb("W_T", [P, 3, D])
        b_qkv = sb("b_qkv", [P, 3, D])
        gam = sb("gam", [P, D])
        bet = sb("bet", [P, D])
        W1_raw = sb("W1_raw", [P, E * FC, D])
        b1_rows = sb("b1_rows", [E * FC, P])
        W1_hi = sb("W1_hi", [P, E * FC, P], F16)
        W1_lo = sb("W1_lo", [P, E * FC, P], F16)
        W2_raw = sb("W2_raw", [P, E, F])
        W2_hi = sb("W2_hi", [P, E * FC, D], F16)
        W2_lo = sb("W2_lo", [P, E * FC, D], F16)
        w_top_abs = sb("w_top_abs", [P, 2])
        w_scale = sb("w_scale", [P, 2])
        b2_scale = sb("b2_scale", [P, 1])
        o_scale = sb("o_scale", [P, 1])
        Wr_raw = sb("Wr_raw", [E, D])
        br_col = sb("br_col", [E, 1])
        Wr_T = sb("Wr_T", [P, E])
        b2_rep = sb("b2_rep", [3 * E, D])
        b2_rest = sb("b2_rest", [3 * E, 2, D])
        b2_parts = sb("b2_parts", [3 * E, 3, D], BF16)
        ident = sb("ident", [P, P])
        ident16 = sb("ident16", [P, P], BF16)
        ones = sb("ones", [P, P])
        sel = sb("sel", [3 * E, E, P], BF16)
        diag = sb("diag", [3 * E, 3, E])
        half = sb("half", [P, B])
        mask8 = sb("mask8", [B, P], U8)
        mask_f = sb("mask_f", [B, P])
        mask_neg = sb("mask_neg", [P, B])
        spare = sb("spare", [P, 1])
        spare_pool = sb("spare_pool", [P, 1])
        eiota = sb("eiota", [P, TB, E])

        PS = ctx.enter_context(nc.psum_tensor("PS", [P, 8, 512], F32))

        x_sq = ctx.enter_context(nc.semaphore("x_sq"))
        x_ms = ctx.enter_context(nc.semaphore("x_ms"))
        x_rms = ctx.enter_context(nc.semaphore("x_rms"))
        x_scaled = ctx.enter_context(nc.semaphore("x_scaled"))
        w1_in = ctx.enter_context(nc.semaphore("w1_in"))
        w_int_ready = ctx.enter_context(nc.semaphore("w_int_ready"))
        w_ready = ctx.enter_context(nc.semaphore("w_ready"))
        w_scaled = ctx.enter_context(nc.semaphore("w_scaled"))
        w_top_ready = ctx.enter_context(nc.semaphore("w_top_ready"))
        small_psum = ctx.enter_context(nc.semaphore("small_psum"))
        small_ready = ctx.enter_context(nc.semaphore("small_ready"))
        wT_psum = ctx.enter_context(nc.semaphore("wT_psum"))
        w_high = ctx.enter_context(nc.semaphore("w_high"))
        x0_in = ctx.enter_context(nc.semaphore("x0_in"))
        x_in = ctx.enter_context(nc.semaphore("x_in"))
        w_in = ctx.enter_context(nc.semaphore("w_in"))
        xw_in = ctx.enter_context(nc.semaphore("xw_in"))
        ffn_in = ctx.enter_context(nc.semaphore("ffn_in"))
        consts = ctx.enter_context(nc.semaphore("consts"))
        first_psum = ctx.enter_context(nc.semaphore("first_psum"))
        w_sums_ready = ctx.enter_context(nc.semaphore("w_sums_ready"))
        w_intT_ready = ctx.enter_context(nc.semaphore("w_intT_ready"))
        w_abs_ready = ctx.enter_context(nc.semaphore("w_abs_ready"))
        w_split = ctx.enter_context(nc.semaphore("w_split"))
        b1_psum = ctx.enter_context(nc.semaphore("b1_psum"))
        dve_chain = ctx.enter_context(nc.semaphore("dve_chain"))
        pool_chain = ctx.enter_context(nc.semaphore("pool_chain"))

        ssq1 = sb("ssq1", [P, B])
        amax1 = sb("amax1", [P, B])
        rms1 = sb("rms1", [P, B])
        clip1 = sb("clip1", [P, B])
        rec1 = sb("rec1", [P, B])
        s1 = sb("s1", [P, B])
        inv1 = sb("inv1", [P, B])
        inv1sq = sb("inv1sq", [P, B])
        w_qk = sb("w_qk", [P, 1])
        c_qk = sb("c_qk", [P, B])
        c_v = sb("c_v", [P, B])
        yn = sb("yn", [P, TB, D])
        xq_f = sb("xq_f", [P, TB, D])
        xq = sb("xq", [P, TB, D], BF16)
        xqT = sb("xqT", [P, TB, P], BF16)
        qkv = sb("qkv", [P, 4, 3 * D])
        QK = sb("QK", [P, 4, 2, H, HS], BF16)
        QKT = sb("QKT", [P, 8, HG, P], BF16)
        prod1 = QK[:].rearrange("p a b c d -> p (a b c d)").bitcast(F32).rearrange("p (a b) -> p a b", a=2)
        prod2 = QKT[:].rearrange("p a b c -> p (a b c)").bitcast(F32).rearrange("p (a b) -> p a b", a=2)
        S1 = sb("S1", [P, D])
        S1m = sb("S1m", [P, H])
        S1d = sb("S1d", [P, 2, H * H])
        E1 = sb("E1", [P, 2, H * H])
        E1sum = sb("E1sum", [P, 2, H])
        E1inv = sb("E1inv", [P, 4, H])
        hctx = sb("hctx", [P, 2, D])
        ysq = sb("ysq", [P, TB, D])
        ssq2 = sb("ssq2", [P, TB])
        ms2 = sb("ms2", [P, TB])
        amax2 = sb("amax2", [P, TB])
        rms2 = sb("rms2", [P, TB])
        clip2 = sb("clip2", [P, TB])
        rec2 = sb("rec2", [P, TB])
        s2 = sb("s2", [P, TB])
        f2 = sb("f2", [P, TB])
        yq_f = sb("yq_f", [P, TB, D])
        yq = sb("yq", [P, TB, D], BF16)
        yqT = sb("yqT", [P, TB, P], BF16)
        z1 = sb("z1", [P, TB, D])
        bn1 = sb("bn1", [P, TB, 6])
        mv1 = sb("mv1", [P, TB, 2])
        ve1 = sb("ve1", [P, TB])
        minus_mean1 = sb("minus_mean1", [P, TB])
        z1c = sb("z1c", [P, TB, D])
        rstd1 = sb("rstd1", [P, TB])
        shuffle = nc.dram_tensor("shuffle", [B, H, P, HD], F32, kind="Internal").ap()

        xq_ready = sem("xq_ready")
        xqT_psum = sem("xqT_psum")
        xqT_ready = sem("xqT_ready")
        qkv_psum = sem("qkv_psum")
        qkv_ready = sem("qkv_ready")
        qk_prod = sem("qk_prod")
        s1_ready = sem("s1_ready")
        e1_ready = sem("e1_ready")
        av_prod = sem("av_prod")
        av_share = sem("av_share")
        s_psum = sem("s_psum")
        hctx_psum = sem("hctx_psum")
        hctx_ready = sem("hctx_ready")
        shuffled = sem("shuffled")
        y_in = sem("y_in")
        ysq_ready = sem("ysq_ready")
        ms2_ready = sem("ms2_ready")
        rms2_ready = sem("rms2_ready")
        s2_ready = sem("s2_ready")
        y_normal = sem("y_normal")
        yq_f_ready = sem("yq_f_ready")
        yq_ready = sem("yq_ready")
        yqT_psum = sem("yqT_psum")
        yqT_ready = sem("yqT_ready")
        wo_psum = sem("wo_psum")
        z1_ready = sem("z1_ready")
        ve1_ready = sem("ve1_ready")
        rstd1_ready = sem("rstd1_ready")
        z1_centered = sem("z1_centered")
        x1_ready = sem("x1_ready")

        x1s = sb("x1s", [P, TB, D])
        cs = sb("cs", [P, TB, D])
        x1T = sb("x1T", [P, TB, P])
        cT = sb("cT", [P, TB, P])
        qk_f = sb("qk_f", [P, 2, 2, D])
        qk_rest = sb("qk_rest", [P, 2, D])
        Va = sb("Va", [P, 8, D])
        HO = 8 * (HD + 1)
        VF = 8 * (HO + HD + 1)
        frames = W2_raw[:].rearrange("p a b -> p (a b)")
        v_frame = frames[:, 0:4 * VF].rearrange("p (b a c) -> p b a c", b=2, a=2)
        outT = frames[0:HO, 4 * VF:4 * VF + 2 * P]
        QT, QmT, KT = QKT[:, 0:2], QKT[:, 2:4], QKT[:, 4:8]
        m2 = sb("m2", [P, H])
        m_neg = sb("m_neg", [P, H])
        m_rest = sb("m_rest", [P, 1, H])
        PT = W1_raw[:].rearrange("p (a h) q -> p a h q", a=2)
        sum2 = sb("sum2", [P, H])
        rsum2 = sb("rsum2", [P, H])
        att2 = sb("att2", [P, TB, D])
        z2 = yq_f
        bn2 = sb("bn2", [P, TB, 6])
        mv2 = sb("mv2", [P, TB, 2])
        ve2 = sb("ve2", [P, TB])
        rstd2 = sb("rstd2", [P, TB])

        x1s_ready = sem("x1s_ready")
        ctx_in = sem("ctx_in")
        x1T_psum = sem("x1T_psum")
        cT_psum = sem("cT_psum")
        x1T_ready = sem("x1T_ready")
        cT_ready = sem("cT_ready")
        proj_psum = sem("proj_psum")
        qkv_copied = sem("qkv_copied")
        high_ready = sem("high_ready")
        split_ready = sem("split_ready")
        qT_psum = sem("qT_psum")
        kT_psum = sem("kT_psum")
        qT_ready = sem("qT_ready")
        kT_ready = sem("kT_ready")
        score_psum = sem("score_psum")
        max_done = sem("max_done")
        m_ready = sem("m_ready")
        qmT_psum = sem("qmT_psum")
        qmT_ready = sem("qmT_ready")
        scoreT_psum = sem("scoreT_psum")
        p_ready = sem("p_ready")
        frames_clear = sem("frames_clear")
        v_ready = sem("v_ready")
        pv_psum = sem("pv_psum")
        outT_ready = sem("outT_ready")
        out_psum = sem("out_psum")
        att_ready = sem("att_ready")
        ve2_ready = sem("ve2_ready")
        rstd2_ready = sem("rstd2_ready")
        x2_ready = sem("x2_ready")

        xa = sb("xa", [P, TB, D])
        xaT = sb("xaT", [P, 2, NT])
        lg = sb("lg", [P, TB, E])
        top = sb("top", [P, TB, 8])
        topi = sb("topi", [P, TB, 8], U32)
        topf = sb("topf", [P, TB, 8])
        gap = sb("gap", [P, TB])
        eg = sb("eg", [P, TB])
        eg1 = sb("eg1", [P, TB])
        w_top = sb("w_top", [P, 2, TB])
        oh = sb("oh", [P, 2, TB, E])
        rw = sb("rw", [P, TB, E])
        rw_rest = sb("rw_rest", [P, 2, TB, E])
        rw16 = sb("rw16", [P, TB, 3, E], BF16)
        rwT = sb("rwT", [3 * E, 2, NT], BF16)
        tile_rows = W2_raw[:].rearrange("p a b -> p (a b)").rearrange("p (a b) -> p a b", b=NT)
        xe = tile_rows[:, 0:2, :]
        oT = tile_rows[:, 2, :]
        parts = W1_raw[:].rearrange("p a b -> p (a b)").bitcast(F16).rearrange("p (k a b) -> p k a b", k=4, a=4)
        h_hi, h_lo, x_hi, x_lo = (parts[:, k] for k in range(4))
        z3, n3, g3, z4, o4 = (Y[:, TB * n:TB * (n + 1), :] for n in range(5))
        bn3 = sb("bn3", [P, TB, 6])
        mv3 = sb("mv3", [P, TB, 2])
        ve3 = sb("ve3", [P, TB])
        rstd3 = sb("rstd3", [P, TB])
        bn4 = sb("bn4", [P, TB, 6])
        mv4 = sb("mv4", [P, TB, 2])
        ve4 = sb("ve4", [P, TB])
        rstd4 = sb("rstd4", [P, TB])

        xa_ready = sem("xa_ready")
        xaT_psum = sem("xaT_psum")
        xaT_ready = sem("xaT_ready")
        lg_psum = sem("lg_psum")
        gap_ready = sem("gap_ready")
        eg_ready = sem("eg_ready")
        rw_ready = sem("rw_ready")
        rwT_psum = sem("rwT_psum")
        rwT_ready = sem("rwT_ready")
        rwb_psum = sem("rwb_psum")
        xe_ready = sem("xe_ready")
        xsplit_ready = sem("xsplit_ready")
        h_psum = sem("h_psum")
        h_hi_ready = sem("h_hi_ready")
        h_lo_ready = sem("h_lo_ready")
        down_done = sem("down_done")
        oT_ready = sem("oT_ready")
        y3_psum = sem("y3_psum")
        z3_ready = sem("z3_ready")
        ve3_ready = sem("ve3_ready")
        rstd3_ready = sem("rstd3_ready")
        ve4_ready = sem("ve4_ready")
        rstd4_ready = sem("rstd4_ready")
        o4_ready = sem("o4_ready")
        stored = sem("stored")

        def bc(ap, n):
            return ap.unsqueeze(2).broadcast_to((ap.shape[0], ap.shape[1], n))

        def batch(t, i):
            return bass.ds(TB * t + i, 1)

        def tile(t):
            return bass.ds(TB * t, TB)

        def turns(eng, lag, body, chain=None, steps=0):
            for u in range(lag):
                body(u, u % 2, lambda l, u=u: 0 <= u - l < T)
            with eng.Fori(0, (T - lag) // 2) as pair:
                if chain:
                    first = chain.n
                    chain.turn = pair * steps
                for v in range(2):
                    body(2 * pair + (lag + v), (lag + v) % 2, lambda l: True)
            if chain:
                made = chain.n - first
                assert made == steps, f"the loop makes {made} steps"
                chain.turn = 0
                chain.n += made * ((T - lag) // 2 - 1)
            for u in range(T, T + lag):
                body(u, u % 2, lambda l, u=u: 0 <= u - l < T)

        def slots(j, side, first, end, by=1):
            return QK[:, j, side, :, 0:6 * HD].rearrange("p h (s d) -> p h s d", d=HD)[:, :, first:end:by, :]

        def heads(ap):
            return ap.rearrange("p (h d) -> p h d", h=H)

        def banks(a):
            return PS[:, 2 * a:2 * a + 2, :]

        def half_heads(ap, a):
            pat = "p (g r) q -> p r g q" if len(ap.shape) == 3 else "p (g r) -> p r g"
            return ap[:, 8 * a:8 * a + 8].rearrange(pat, r=HR)

        def qk_products(eng, i, first, end):
            n = end - first
            q = qkv[:, i, 0:D].rearrange("p (d h a) -> p d h a", a=1, d=HD)[:, :, first:end, :]
            k = qkv[:, i, D:2 * D].rearrange("p (d a t) -> p d a t", a=1, t=H)
            return eng.tensor_tensor(prod1[:, i % 2, :].rearrange("p (d h t) -> p d h t", d=HD, h=H)[:, :, first:end, :],
                                     q.broadcast_to((P, HD, n, H)), k.broadcast_to((P, HD, n, H)), ALU.mult)

        def av_products(eng, i, first, end):
            n = end - first
            a = E1[:, i % 2, H * first:H * end].rearrange("p (h t a) -> p t h a", a=1, t=H)
            v = qkv[:, i, 2 * D:].rearrange("p (t a d) -> p t a d", a=1, t=H)
            return eng.tensor_tensor(prod2[:, i % 2, :].rearrange("p (t h d) -> p t h d", t=H, h=H)[:, :, first:end, :],
                                     a.broadcast_to((P, H, n, HD)), v.broadcast_to((P, H, n, HD)), ALU.mult)

        expert_slots = {(0, 3): (0, 1), (1, 0): (2,), (1, 1): (3, 4), (1, 2): (5, 6), (1, 3): (7,)}
        W_BANKS = ((5, 4), (3, 0))

        def experts_at(u, j):
            return zip(expert_slots.get((u, j), ()), W_BANKS) if isinstance(u, int) else ()

        def diagonal(b):
            return v_frame[:, b].rearrange("p a (n c) -> p a n c", n=8)[:, :, :, 0:HD + 1]

        NC = E * FC

        def prepared(g):
            return (1, g + 2) if g + 2 < E else (0, g + 2 - E)

        block = ctx.enter_context(nc.Block())

        def bcast_dma(eng, dst, src, s):
            eng.dma_start(dst, src.rearrange("(a n) -> a n", a=1).broadcast_to((P, src.shape[0]))).then_inc(s, 16)

        @block.sync
        def _(sp):
            for s in counters:
                sp.sem_inc(s, 16 * CREDIT if s in (shuffled, y_in, ctx_in, stored) else CREDIT)
            for n, w in enumerate((wq, wk, wv, wo)):
                sp.dma_start(w_raw[:, n, :], w).then_inc(w_in, 16)
            sp.dma_start(mask8[:], mask).then_inc(w_in, 16)
            sp.dma_start(X[:, 0:TB, :], x[0:TB].rearrange("b s d -> s b d")).then_inc(x0_in, 16)
            sp.dma_start(W1_raw[:], W1.rearrange("e (c p) d -> p (e c) d", p=P)).then_inc(w1_in, 16)
            sp.dma_start(b1_rows[:], b1.rearrange("e (c p) -> (e c) p", p=P)).then_inc(w1_in, 16)
            sp.dma_start(Wr_raw[:], Wr).then_inc(w1_in, 16)
            sp.dma_start(br_col[:], br.rearrange("(e a) -> e a", a=1)).then_inc(w1_in, 16)
            sp.dma_start(W2_raw[:], W2.rearrange("e d f -> d e f")).then_inc(ffn_in, 16)
            for n in range(3):
                sp.dma_start(b2_rep[n * E:(n + 1) * E, :], b2).then_inc(ffn_in, 16)
            sp.dma_start(X[:, TB:B, :], x[TB:B].rearrange("b s d -> s b d")).then_inc(x_in, 16)
            for n, w in enumerate((Wq, Wk, Wv)):
                sp.dma_start(W_raw[:, n, :], w).then_inc(xw_in, 16)
            for n, v in enumerate((bq, bk, bv)):
                bcast_dma(sp, b_qkv[:, n, :], v, xw_in)
            bcast_dma(sp, gam[:], gamma, xw_in)
            bcast_dma(sp, bet[:], beta, xw_in)

            def a_turn(u, parity, there):
                for j in range(TB):
                    l, i = divmod(j - 3, TB)
                    l = -l
                    if there(l):
                        b = TB * (u - l) + i
                        after(sp, hctx_ready, b + 1)
                        sp.dma_start(shuffle[batch(u - l, i)].rearrange("a h s d -> s (a h) d"),
                                     hctx[:, i % 2, :].rearrange("p (h d) -> p h d", h=H)).then_inc(shuffled, 16)
                        after_dma(sp, shuffled, b + 1)
                        sp.dma_start(Y[:, batch(u - l, i), :],
                                     shuffle[batch(u - l, i)].rearrange("a h (q r) d -> (h q) a (r d)", r=D // HD)
                                     ).then_inc(y_in, 16)

            turns(sp, 2, a_turn)

            with sp.Fori(0, T) as t:
                after(sp, cT_psum, t)
                sp.dma_start(cs[:], ctx_1024[tile(t)].rearrange("b s d -> s b d")).then_inc(ctx_in, 16)

            with sp.Fori(0, T) as t:
                after(sp, o4_ready, t + 1)
                sp.dma_start(out[tile(t)].rearrange("b s d -> s b d"), o4[:]).then_inc(stored, 16)
            after_dma(sp, stored, T)

        @block.gpsimd
        def _(pool):
            ch = Chain(pool, pool_chain)
            ch(pool.memset(ident[:], 0.0))
            ch(pool.memset(ident16[:], 0.0))
            ch(pool.memset(sel[:], 1.0))
            pool.memset(ones[:], 1.0).then_inc(consts, 1)
            pool.memset(half[:], -0.5).then_inc(consts, 1)
            ch.settle()
            for m in (ident, ident16):
                pool.affine_select(out=m[:], in_=m[:], compare_op=ALU.not_equal, fill=1.0, base=0,
                                   pattern=[[-1, P]], channel_multiplier=1).then_inc(consts, 1)
            pool.iota(eiota[:], pattern=[[0, TB], [1, E]], base=0, channel_multiplier=0,
                      allow_small_or_imprecise_dtypes=True).then_inc(consts, 1)
            ch(pool.memset(diag[:], 0.0))
            ch.settle()
            for part in range(3):
                ch(pool.affine_select(out=diag[:, part, :], in_=diag[:, part, :], compare_op=ALU.not_equal,
                                      fill=1.0, base=-E * part, pattern=[[-1, E]], channel_multiplier=1))
            ch.settle()
            ch(pool.tensor_tensor(diag[:, 0, :], diag[:, 0, :], diag[:, 1, :], ALU.add))
            ch.settle()
            ch(pool.tensor_tensor(diag[:, 0, :], diag[:, 0, :], diag[:, 2, :], ALU.add))
            ch.settle()
            pool.tensor_tensor(sel[:], bc(diag[:, 0, :], P), sel[:], ALU.mult).then_inc(consts, 1)
            pool.memset(xa[:, :, D - 1], 1.0).then_inc(consts, 1)
            pool.wait_ge(x_ms, 1)
            pool.tensor_tensor(rms1[:, 0:TB], ssq1[:, 0:TB], half[:, 0:TB], ALU.pow).then_inc(x_rms, 1)

            def stage_x(u):
                after(pool, x1_ready, u + 1)
                after(pool, x1T_psum, u)
                pool.tensor_copy(x1s[:], X[:, tile(u), :]).then_inc(x1s_ready, 1)

            def prepare_cross_attention():
                after(pool, hctx_ready, B)
                ch(pool.memset(QK[:, :, :, :, 6 * HD:HS], 0.0))
                ch.settle()
                ch(pool.memset(QK[:, :, 0, :, 6 * HD], 1.0))
                ch(pool.memset(QK[:, :, 1, :, 6 * HD + 1:6 * HD + 4], 1.0))
                ch.settle()
                ch(pool.memset(v_frame, 0.0))
                ch.settle()
                for b in range(2):
                    last = pool.memset(diagonal(b)[:, :, :, HD], 1.0)
                    if b == 0:
                        ch(last)
                last.then_inc(frames_clear, 1)
                stage_x(0)

            def a_turn(u, parity, there):
                first = isinstance(u, int) and u == 0
                for j in range(TB):
                    k = TB * u + j
                    l, i = divmod(j - 1, TB)
                    if there(-l):
                        after(pool, qkv_ready, k)
                        after(pool, s1_ready, k - 2)
                        qk_products(pool, i, 0, HP).then_inc(qk_prod, 1)
                    if j == 0 and there(2):
                        after(pool, ms2_ready, u - 1)
                        pool.tensor_tensor(rms2[:], ms2[:], half[:, 0:TB], ALU.pow).then_inc(rms2_ready, 1)
                    if j == 0 and isinstance(u, int) and u == T + 1:
                        prepare_cross_attention()
                    if j == 3 and there(2):
                        after(pool, ve1_ready, u - 1)
                        pool.tensor_tensor(rstd1[:], ve1[:], half[:, 0:TB], ALU.pow).then_inc(rstd1_ready, 1)
                    l, i = divmod(j - 2, TB)
                    if there(-l):
                        after(pool, e1_ready, k - 1)
                        after(pool, hctx_ready, k - 3)
                        av_products(pool, i, 0, HP).then_inc(av_prod, 1)
                    if first and j == 2:
                        pool.wait_ge(x_ms, 2)
                        pool.tensor_tensor(rms1[:, TB:B], ssq1[:, TB:B], half[:, TB:B], ALU.pow).then_inc(x_rms, 1)
                        pool.wait_ge(w_abs_ready, 1)
                        pool.partition_all_reduce(w_top_abs[:], w_top_abs[:], P, bass.bass_isa.ReduceOp.max
                                                  ).then_inc(w_top_ready, 1)

            turns(pool, 2, a_turn)

            def invert_roots(u):
                after(pool, ve2_ready, u - 1)
                pool.tensor_tensor(rstd2[:], ve2[:], half[:, 0:TB], ALU.pow).then_inc(rstd2_ready, 1)

            def b_turn(u, parity, there):
                if there(0) and not (isinstance(u, int) and u == 0):
                    stage_x(u)
                for j in range(TB):
                    k = TB * u + j - 1
                    if j == 3 and there(2) and not (isinstance(u, int) and u == T + 1):
                        invert_roots(u)
                    l, i = divmod(j - 1, TB)
                    if there(-l):
                        after(pool, split_ready, k)
                        after(pool, high_ready, k + 1)
                        for side in range(2):
                            ch(pool.tensor_tensor(heads(qk_rest[:, side]), heads(qk_f[:, i % 2, side]),
                                                  slots(i, side, 4, 5)[:, :, 0, :], ALU.subtract))
                        ch.settle()
                        pool.tensor_tensor(QK[:, i, 1, :, 6 * HD], ones[:, 0:H],
                                           mask_neg[:, batch(u + l, i)].broadcast_to((P, H)), ALU.mult)
                        for side, (first, end, by) in enumerate(((1, 4, 2), (0, 2, 1))):
                            for s in range(first, end, by):
                                ch(pool.tensor_scalar(slots(i, side, s, s + 1)[:, :, 0, :],
                                                      heads(qk_rest[:, side]), 1.0, None, ALU.mult))
                        ch.settle()
                        for side, low in enumerate((5, 2)):
                            last = pool.tensor_tensor(slots(i, side, low, low + 1)[:, :, 0, :], heads(qk_rest[:, side]),
                                                      slots(i, side, 1, 2)[:, :, 0, :], ALU.subtract)
                            if side == 0:
                                ch(last)
                        last.then_inc(split_ready, 1)

            turns(pool, 2, b_turn, ch, 2 * TB * 7)

            def c_turn(u, parity, there):
                for n in range(NC):
                    if n % FC == 2:
                        split_tile, e = prepared(n // FC)
                        if there(split_tile):
                            i = E * (u - split_tile) + e
                            after(pool, xe_ready, i + 1)
                            after(pool, h_psum, FC * (i - 3))
                            pool.tensor_tensor(spare_pool[:], half[:, 0:1], half[:, 0:1], ALU.mult)
                            ch(pool.tensor_scalar(x_hi[:, e % 4, :], xe[:, e % 2, :], 1.0, None, ALU.mult))
                            ch.settle()
                            pool.tensor_tensor(x_lo[:, e % 4, :], xe[:, e % 2, :], x_hi[:, e % 4, :],
                                               ALU.subtract).then_inc(xsplit_ready, 1)
                    if n == 8 and there(2):
                        after(pool, ve3_ready, u - 1)
                        pool.tensor_tensor(rstd3[:], ve3[:], half[:, 0:TB], ALU.pow).then_inc(rstd3_ready, 1)
                    if n == 16 and there(2):
                        after(pool, ve4_ready, u - 1)
                        pool.tensor_tensor(rstd4[:], ve4[:], half[:, 0:TB], ALU.pow).then_inc(rstd4_ready, 1)
                if isinstance(u, int) and u == 0:
                    invert_roots(T + 1)

            turns(pool, 2, c_turn, ch, 2 * E)

        @block.tensor
        def _(pe):
            pe.wait_ge(consts, 7)
            pe.wait_ge(w_sums_ready, 1)
            pe.matmul(PS[:, 0, 0:4], ones[:], w_abs[:], start=True, stop=True).then_inc(first_psum, 1)
            pe.transpose(PS[:, 1, 0:B], mask_f[:], ident[0:B, 0:B]).then_inc(first_psum, 1)
            pe.wait_ge(w_int_ready, 1)
            for n in range(4):
                last = pe.transpose(PS[:, 2, n * 64:n * 64 + 64].bitcast(BF16), w_int[:, n, :], ident16[:])
            last.then_inc(first_psum, 1)
            pe.wait_ge(w_intT_ready, 1)

            def expert(g, banks):
                for n in range(4):
                    pe.transpose(PS[:, banks[0], n * P:(n + 1) * P], W1_raw[:, 4 * g + n, :], ident[:])
                    last = pe.transpose(PS[:, banks[1], n * P:(n + 1) * P],
                                        W2_raw[:, g, n * P:(n + 1) * P], ident[:])
                last.then_inc(wT_psum, 1)

            def a_turn(u, parity, there):
                for j in range(TB):
                    k = TB * u + j
                    for n, (g, banks) in enumerate(experts_at(u, j)):
                        if n == 0 and g == 0:
                            pe.wait_ge(small_ready, 1)
                        elif n == 0:
                            pe.wait_ge(w_split, g)
                        expert(g, banks)
                    if j == 2 and there(2):
                        after(pe, yq_ready, u - 1)
                        after(pe, yqT_ready, u - 2)
                        for i in range(TB):
                            last = pe.transpose(PS[:, 3, i * 64:i * 64 + 64].bitcast(BF16), yq[:, i, :], ident16[:])
                        last.then_inc(yqT_psum, 1)
                    l, i = divmod(j - 3, TB)
                    if there(-l):
                        after(pe, av_prod, k - 2)
                        after(pe, av_share, k - 2)
                        after(pe, hctx_ready, k - 3)
                        for t in range(H):
                            last = pe.matmul(PS[:, 6, 0:D], ident[:], prod2[:, i % 2, D * t:D * (t + 1)],
                                             start=(t == 0), stop=(t == H - 1))
                        last.then_inc(hctx_psum, 1)
                    if j == 0 and there(0):
                        after(pe, xq_ready, u + 1)
                        after(pe, xqT_ready, u)
                        for i in range(TB):
                            last = pe.transpose(PS[:, 0, i * 64:i * 64 + 64].bitcast(BF16), xq[:, i, :], ident16[:])
                        last.then_inc(xqT_psum, 1)
                    if j == 2 and there(2):
                        after(pe, yqT_ready, u - 1)
                        after(pe, z1_ready, u - 2)
                        for i in range(TB):
                            last = pe.matmul(PS[:, 4, i * D:(i + 1) * D], yqT[:, i, :], w_intT[:, 3, :],
                                             start=True, stop=True)
                        last.then_inc(wo_psum, 1)
                    l, i = divmod(j - 1, TB)
                    if there(-l):
                        after(pe, qk_prod, k)
                        after(pe, s1_ready, k - 1)
                        for d in range(HD):
                            last = pe.matmul(PS[:, 7, 0:D], ident[:], prod1[:, i % 2, H * H * d:H * H * d + D],
                                             start=(d == 0), stop=(d == HD - 1))
                        last.then_inc(s_psum, 1)
                    if there(0):
                        if j == 0:
                            after(pe, xqT_ready, u + 1)
                        after(pe, qkv_ready, k - 1)
                        pe.matmul(PS[:, 1 + j % 2, 0:3 * D], xqT[:, j, :],
                                  w_intT[:, 0:3, :].rearrange("p a d -> p (a d)"),
                                  start=True, stop=True).then_inc(qkv_psum, 1)
                    if isinstance(u, int) and u == 0:
                        if j == 0:
                            pe.wait_ge(w1_in, 16 * 4)
                            pe.transpose(PS[:, 3, 0:E * FC], b1_rows[:], ident[0:E * FC, 0:E * FC]).then_inc(b1_psum, 1)
                        if j == 2:
                            pe.wait_ge(w_ready, 1)
                            pe.transpose(PS[:, 3, 64:64 + E], Wr_raw[:], ident[0:E, 0:E])
                            pe.wait_ge(xw_in, 16 * 8)
                            for n in range(3):
                                last = pe.transpose(PS[:, 3, (n + 1) * D:(n + 2) * D], W_raw[:, n, :], ident[:])
                            last.then_inc(small_psum, 1)
                            pe.wait_ge(ffn_in, 16 * 4)

            turns(pe, 2, a_turn)

            after(pe, z1_ready, T)
            after(pe, qkv_ready, B)

            def b_turn(u, parity, there):
                def spread(bank, j, side, ready):
                    for g in range(HG):
                        last = pe.transpose(PS[:, bank, g * 64:(g + 1) * 64].bitcast(BF16),
                                            QK[:, j, side, HR * g:HR * g + HR, :].rearrange("p h r -> p (h r)"),
                                            ident16[:])
                    last.then_inc(ready, 1)

                def half_scores(a, left, right, used, ready):
                    for g in range(HG // 2):
                        for r in range(HR):
                            rows = slice(HS * r, HS * r + used)
                            last = pe.matmul(PS[:, 2 * a + r, g * P:(g + 1) * P], left[rows, HG // 2 * a + g, :],
                                             right[rows, HG // 2 * a + g, :], start=True, stop=True)
                    last.then_inc(ready, 1)

                for j in range(TB):
                    k = TB * u + j - 1
                    l, i = divmod(j - 3, TB)
                    if there(-l):
                        after(pe, qT_ready, k - 1)
                        after(pe, kT_ready, k - 1)
                        for a in range(2):
                            after(pe, p_ready, 2 * (k - 5) + a + 1)
                            after(pe, max_done, 2 * (k - 3) + a + 1)
                            half_scores(a, QT[:, i % 2], KT[:, i], 6 * HD + 1, score_psum)
                    l, i = divmod(j - 1, TB)
                    if there(-l):
                        if i == 0:
                            after(pe, x1T_ready, u + 1)
                            after(pe, cT_ready, u + 1)
                        after(pe, qkv_copied, k)
                        pe.matmul(PS[:, 6, 0:D], x1T[:, i, :], W_T[:, 0, :], start=True, stop=True)
                        pe.matmul(PS[:, 6, D:3 * D], cT[:, i, :], W_T[:, 1:3, :].rearrange("p a d -> p (a d)"),
                                  start=True, stop=True).then_inc(proj_psum, 1)
                    if there(-((j - 7) // TB)):
                        after(pe, outT_ready, k - 5)
                        for a in range(2):
                            last = pe.transpose(PS[:, 7, a * HO:(a + 1) * HO], outT[:, a * P:(a + 1) * P],
                                                ident[0:HO, 0:HO])
                        last.then_inc(out_psum, 1)
                    l, i = divmod(j - 4, TB)
                    if there(-l):
                        after(pe, m_ready, k - 2)
                        after(pe, qT_ready, k - 1 if there(-((j - 3) // TB)) else B)
                        after(pe, qmT_ready, k - 3)
                        spread(4, i, 0, qmT_psum)
                    l, i = divmod(j - 2, TB)
                    if there(-l):
                        after(pe, split_ready, k)
                        after(pe, kT_ready, k - 1)
                        spread(5, i, 1, kT_psum)

                    def half_outputs(a):
                        l, i = divmod(j - 6, TB)
                        if there(-l):
                            after(pe, p_ready, 2 * (k - 5) + a + 1)
                            after(pe, att_ready, k - 5)
                            after(pe, v_ready, k - 4)
                            for n in range(8):
                                last = pe.matmul(PS[0:HO, 7, a * P:(a + 1) * P], v_frame[:, i % 2, a, HO * n:HO * (n + 1)],
                                                 PT[:, i % 2, 8 * a + n, :], start=(n == 0), stop=(n == 7))
                            if a == 1:
                                last.then_inc(pv_psum, 1)

                    def half_shifted(a):
                        l, i = divmod(j - 5, TB)
                        if there(-l):
                            after(pe, qmT_ready, k - 3)
                            after(pe, max_done, 2 * (k - 2) + a + 1 if there(-((j - 3) // TB)) else 2 * B)
                            after(pe, p_ready, 2 * (k - 5) + a + 1)
                            half_scores(a, KT[:, i], QmT[:, i % 2], 6 * HD + 4, scoreT_psum)

                    half_shifted(0)
                    half_outputs(0)
                    l, i = divmod(j - 2, TB)
                    if there(-l):
                        after(pe, qmT_ready, k - 2)
                        spread(4, i, 0, qT_psum)
                    half_shifted(1)
                    half_outputs(1)
                    if j == 0 and there(0):
                        after(pe, x1s_ready, u + 1)
                        after(pe, qT_ready, TB * u - 1)
                        for i in range(TB):
                            last = pe.transpose(PS[:, 4, i * P:(i + 1) * P], x1s[:, i, :], ident[:])
                        last.then_inc(x1T_psum, 1)
                        after_dma(pe, ctx_in, u + 1)
                        after(pe, kT_ready, TB * u - 1)
                        for i in range(TB):
                            last = pe.transpose(PS[:, 5, i * P:(i + 1) * P], cs[:, i, :], ident[:])
                        last.then_inc(cT_psum, 1)

            turns(pe, 2, b_turn)

            after(pe, att_ready, B)

            def c_turn(u, parity, there):
                def down(n, lag):
                    i = NC * (u - lag) + n
                    after(pe, h_lo_ready, i + 1)
                    o = PS[:, 4 + (parity - lag) % 2, :]
                    pe.matmul(o, W2_hi[:, n, :], h_hi[:, n % 4, :], start=False, stop=False)
                    pe.matmul(o, W2_hi[:, n, :], h_lo[:, n % 4, :], start=False, stop=False)
                    pe.matmul(o, W2_lo[:, n, :], h_hi[:, n % 4, :], start=False,
                              stop=(n == NC - 1)).then_inc(down_done, 1)

                for n in range(NC):
                    if n == 0 and there(1):
                        after(pe, oT_ready, u - 2)
                        for a in range(3):
                            pe.matmul(PS[:, 4 + (parity - 1) % 2, :], b2_parts[:, a, :], rwT[:, (parity - 1) % 2, :],
                                      start=(a == 0), stop=False)
                    if there(1):
                        i = NC * (u - 1) + n
                        e = n // FC
                        if n % FC == 0:
                            after(pe, xsplit_ready, E * (u - 1) + e + 1)
                        after(pe, h_lo_ready, i - 3)
                        pe.matmul(PS[:, n % 4, :], W1_hi[:, n, :], x_hi[:, e % 4, :], start=True, stop=False)
                        pe.matmul(PS[:, n % 4, :], W1_hi[:, n, :], x_lo[:, e % 4, :], start=False, stop=False)
                        pe.matmul(PS[:, n % 4, :], W1_lo[:, n, :], x_hi[:, e % 4, :], start=False,
                                  stop=True).then_inc(h_psum, 1)
                    if n < LATE:
                        if there(2):
                            down(NC - LATE + n, 2)
                    elif there(1):
                        down(n - LATE, 1)
                    if n % FC == 1:
                        lag, e = prepared(n // FC)
                        if there(lag):
                            i = E * (u - lag) + e
                            if lag == 0 and e == 0:
                                after(pe, rwT_ready, u + 1)
                            after(pe, xe_ready, i)
                            pe.matmul(PS[:, 6, :], sel[:, e, :], rwT[:, (parity - lag) % 2, :],
                                      start=True, stop=True).then_inc(rwb_psum, 1)
                    if n == 5 and there(2):
                        after(pe, oT_ready, u - 1)
                        after(pe, rwT_ready, u if there(1) else T)
                        for i in range(TB):
                            last = pe.transpose(PS[:, 7, i * D:(i + 1) * D], oT[:, i * P:(i + 1) * P], ident[:])
                        last.then_inc(y3_psum, 1)
                    if n == 9 and there(0):
                        after(pe, xa_ready, u + 1)
                        after(pe, z3_ready, u - 1)
                        after(pe, rwT_ready, u)
                        for i in range(TB):
                            last = pe.transpose(PS[:, 7, i * P:(i + 1) * P], xa[:, i, :], ident[:])
                        last.then_inc(xaT_psum, 1)
                    if n == 12 and there(0):
                        after(pe, xaT_ready, u + 1)
                        for i in range(TB):
                            last = pe.matmul(PS[:, 7, i * E:(i + 1) * E], xaT[:, parity, i * P:(i + 1) * P], Wr_T[:],
                                             start=True, stop=True)
                        last.then_inc(lg_psum, 1)
                    if n == 22 and there(0):
                        after(pe, rw_ready, u + 1)
                        for i in range(TB):
                            last = pe.transpose(PS[0:3 * E, 7, i * 64:(i + 1) * 64].bitcast(BF16),
                                                rw16[:, i, :, :].rearrange("p a e -> p (a e)"), ident16[:])
                        last.then_inc(rwT_psum, 1)

            turns(pe, 2, c_turn)

        @block.scalar
        def _(act):
            def x_squares(first, end):
                for b in range(first, end):
                    last = act.activation(Y[:, b, :], X[:, b, :], ACT.Square, accum_out=ssq1[:, b:b + 1])
                last.then_inc(x_sq, 1)

            act.wait_ge(x0_in, 16)
            x_squares(0, TB)
            act.wait_ge(first_psum, 3)
            wT = PS[:, 2, 0:256].bitcast(BF16).rearrange("p (a c) -> p a c", a=4)
            act.copy(w_intT[:, 0:2, :].rearrange("p a (d h) -> p a h d", d=HD),
                     wT[:, 0:2, :].rearrange("p a (h d) -> p a h d", h=H))
            act.copy(w_intT[:, 2:4, :], wT[:, 2:4, :]).then_inc(w_intT_ready, 1)
            act.wait_ge(x_scaled, 1)

            def scale_rows(dst, src, scale):
                for i in range(TB):
                    last = act.activation(dst(i), src(i), ACT.Copy, scale=scale(i))
                return last

            def high_weights(g, banks):
                act.wait_ge(wT_psum, g + 1)
                for n, hi in enumerate((W1_hi, W2_hi)):
                    last = act.activation(hi[:, FC * g:FC * g + FC, :].rearrange("p a d -> p (a d)"),
                                          PS[:, banks[n], :], ACT.Copy, scale=w_scale[:, n:n + 1])
                last.then_inc(w_high, 1)

            def a_turn(u, parity, there):
                for j in range(TB):
                    k = TB * u + j
                    l, i = divmod(j - 2, TB)
                    if there(-l):
                        after(act, s1_ready, k - 1)
                        after(act, av_prod, k - 3)
                        act.activation(E1[:, i % 2, :], S1d[:, i % 2, :], ACT.Exp,
                                       scale=c_qk[:, batch(u + l, i)]).then_inc(e1_ready, 1)
                    if isinstance(u, int) and u == 0 and j == 3:
                        act.wait_ge(w_scaled, 1)
                    for g, banks in experts_at(u, j):
                        high_weights(g, banks)
                    if j == 0 and there(0):
                        after(act, xqT_psum, u + 1)
                        after(act, qkv_psum, TB * u)
                        act.copy(xqT[:].rearrange("p a d -> p (a d)"), PS[:, 0, 0:256].bitcast(BF16)).then_inc(xqT_ready, 1)
                    if j == 2 and there(2):
                        after(act, yqT_psum, u - 1)
                        after(act, wo_psum, u - 2)
                        act.copy(yqT[:].rearrange("p a d -> p (a d)"), PS[:, 3, 0:256].bitcast(BF16)).then_inc(yqT_ready, 1)
                    if j == 3 and there(1):
                        after_dma(act, y_in, TB * u)
                        after(act, ms2_ready, u - 1)
                        for i in range(TB):
                            last = act.activation(ysq[:, i, :], Y[:, batch(u - 1, i), :], ACT.Square,
                                                  accum_out=ssq2[:, i:i + 1])
                        last.then_inc(ysq_ready, 1)
                    if j == 3 and there(2):
                        after(act, ve1_ready, u - 1)
                        for i in range(TB):
                            last = act.activation(z1c[:, i, :], z1[:, i, :], ACT.Identity, bias=minus_mean1[:, i:i + 1])
                        last.then_inc(z1_centered, 1)
                        after(act, z1_centered, u - 1)
                        after(act, rstd1_ready, u - 1)
                    if j == 0 and there(2):
                        after(act, rms2_ready, u - 1)
                    if there(0):
                        after(act, qkv_psum, k + 1)
                        after(act, av_prod, k - 3)
                        after(act, s1_ready, k - 2)
                        act.copy(qkv[:, j, :], PS[:, 1 + j % 2, 0:3 * D]).then_inc(qkv_ready, 1)
                    if j == 0 and there(2):
                        scale_rows(lambda i: yn[:, i, :], lambda i: Y[:, batch(u - 2, i), :],
                                   lambda i: rms2[:, i:i + 1]).then_inc(y_normal, 1)
                        after(act, y_normal, u - 1)
                        after(act, s2_ready, u - 1)
                        scale_rows(lambda i: yq_f[:, i, :], lambda i: yn[:, i, :],
                                   lambda i: s2[:, i:i + 1]).then_inc(yq_f_ready, 1)
                    if j == 3 and there(2):
                        scale_rows(lambda i: X[:, batch(u - 2, i), :], lambda i: z1c[:, i, :],
                                   lambda i: rstd1[:, i:i + 1]).then_inc(x1_ready, 1)
                    if isinstance(u, int) and u == 0 and j == 1:
                        act.wait_ge(x_in, 16)
                        x_squares(TB, B)
                    if isinstance(u, int) and u == 0 and j == 2:
                        act.wait_ge(small_psum, 1)
                        act.copy(Wr_T[:], PS[:, 3, 64:64 + E])
                        act.copy(W_T[:].rearrange("p a d -> p (a d)"), PS[:, 3, D:4 * D]).then_inc(small_ready, 1)

            turns(act, 2, a_turn)
            after(act, frames_clear, 1)

            def b_turn(u, parity, there):
                for j in range(TB):
                    k = TB * u + j - 1
                    if there(-((j - 7) // TB)):
                        after(act, pv_psum, k - 5)
                        act.copy(outT, PS[0:HO, 7, 0:2 * P]).then_inc(outT_ready, 1)
                    l, i = divmod(j - 1, TB)
                    if there(-l):
                        after(act, qkv_copied, k + 1)
                        after(act, qmT_psum, k - 3)
                        act.copy(slots(i, 0, 0, 5, 2), heads(qk_f[:, i % 2, 0]).unsqueeze(2).broadcast_to((P, H, 3, HD)))
                        act.copy(slots(i, 1, 3, 6), heads(qk_f[:, i % 2, 1]).unsqueeze(2).broadcast_to((P, H, 3, HD))
                                 ).then_inc(high_ready, 1)
                    l, i = divmod(j - 4, TB)
                    if there(-l):
                        after(act, qmT_psum, k - 2)
                        act.copy(QmT[:, i % 2].rearrange("p a d -> p (a d)"), PS[:, 4, :].bitcast(BF16)
                                 ).then_inc(qmT_ready, 1)

                    def half_exp(a):
                        l, i = divmod(j - 5, TB)
                        if there(-l):
                            after(act, scoreT_psum, 2 * (k - 4) + a + 1)
                            act.activation(half_heads(PT[:, i % 2], a), banks(a).rearrange("p r (g q) -> p r g q", q=P),
                                           ACT.Exp, scale=HD ** -0.5).then_inc(p_ready, 1)

                    half_exp(0)
                    l, i = divmod(j - 2, TB)
                    if there(-l):
                        after(act, qT_psum, k)
                        after(act, score_psum, 2 * (k - 2))
                        act.copy(QT[:, i % 2].rearrange("p a d -> p (a d)"), PS[:, 4, :].bitcast(BF16)
                                 ).then_inc(qT_ready, 1)
                    half_exp(1)
                    l, i = divmod(j - 5, TB)
                    if there(-l):
                        after(act, qkv_copied, k - 3)
                        act.copy(diagonal(i % 2)[:, :, :, 0:HD],
                                 Va[:, (TB * parity + j - 5) % 8].rearrange("p (a n d) -> p a n d", a=2, n=8)
                                 ).then_inc(v_ready, 1)
                    if j == 0 and there(0):
                        after(act, x1T_psum, u + 1)
                        after(act, proj_psum, TB * u)
                        act.copy(x1T[:].rearrange("p a d -> p (a d)"), PS[:, 4, :]).then_inc(x1T_ready, 1)
                        after(act, cT_psum, u + 1)
                        act.copy(cT[:].rearrange("p a d -> p (a d)"), PS[:, 5, :]).then_inc(cT_ready, 1)

            turns(act, 2, b_turn)

            def c_turn(u, parity, there):
                for n in range(NC):
                    if there(1):
                        i = NC * (u - 1) + n
                        after(act, h_psum, i + 1)
                        after(act, down_done, i - 3)
                        act.activation(h_hi[:, n % 4, :], PS[:, n % 4, :], ACT.Relu).then_inc(h_hi_ready, 1)
                    if n == 2 and there(2):
                        after(act, down_done, NC * (u - 1))
                        after(act, y3_psum, u - 2)
                        act.activation(oT, PS[:, 4 + parity, :], ACT.Copy, scale=o_scale[:]).then_inc(oT_ready, 1)
                    if n == 10 and there(0):
                        after(act, xaT_psum, u + 1)
                        after(act, xe_ready, E * (u - 1))
                        act.activation(xaT[:, parity, :], PS[:, 7, :], ACT.Copy, scale=X_SCALE).then_inc(xaT_ready, 1)
                    if n == 17 and there(0):
                        after(act, gap_ready, u + 1)
                        act.activation(eg[:], gap[:], ACT.Exp, scale=1 / X_SCALE).then_inc(eg_ready, 1)
                    if n == 23 and there(0):
                        after(act, rwT_psum, u + 1)
                        act.copy(rwT[:, parity, :], PS[0:3 * E, 7, 0:256].bitcast(BF16)).then_inc(rwT_ready, 1)

            turns(act, 2, c_turn)

        @block.vector
        def _(dve):
            ch = Chain(dve, dve_chain)
            step, settle = ch, ch.settle

            def settle_apart():
                settle()
                dve.memset(spare[:], 0.0)

            dve.wait_ge(w_in, 16 * 5)
            step(dve.tensor_copy(mask_f[:], mask8[:]))
            settle()
            dve.tensor_reduce(w_abs[:], w_raw[:], AX.X, ALU.add, apply_absolute_value=True).then_inc(w_sums_ready, 1)
            dve.wait_ge(x0_in, 16)
            step(dve.tensor_reduce(amax1[:, 0:TB], X[:, 0:TB, :], AX.X, ALU.max, apply_absolute_value=True))
            dve.wait_ge(x_sq, 1)
            dve.tensor_scalar(ssq1[:, 0:TB], ssq1[:, 0:TB], 1.0 / D, 1e-6, ALU.mult, ALU.add).then_inc(x_ms, 1)
            dve.wait_ge(first_psum, 2)
            step(dve.tensor_scalar(w_mean[:], PS[:, 0, 0:4], 1.0 / (D * D), 1e-5, ALU.mult, ALU.max))
            step(dve.tensor_scalar(mask_neg[:], PS[:, 1, 0:B], NEG, None, ALU.mult))
            settle()
            step(dve.reciprocal(w_inv[:], w_mean[:]))
            settle()
            step(dve.tensor_tensor(w_t[:], w_raw[:], bc(w_inv[:], D), ALU.mult))
            settle()
            step(dve.tensor_scalar(w_t[:], w_t[:], ROUND, -ROUND, ALU.add, ALU.add))
            settle()
            dve.tensor_scalar(w_int[:], w_t[:], 1.0, -1.0, ALU.min, ALU.max).then_inc(w_int_ready, 1)
            step(dve.tensor_tensor(w_qk[:], w_mean[:, 0:1], w_mean[:, 1:2], ALU.mult))

            def x_scales(first, end):
                b = slice(first, end)
                step(dve.tensor_tensor(clip1[:, b], amax1[:, b], rms1[:, b], ALU.mult))
                settle()
                step(dve.tensor_scalar(clip1[:, b], clip1[:, b], 1e-5, None, ALU.max))
                settle()
                step(dve.reciprocal(rec1[:, b], clip1[:, b]))
                step(dve.tensor_scalar(inv1[:, b], clip1[:, b], 1.0 / 127, None, ALU.mult))
                settle()
                step(dve.tensor_scalar(s1[:, b], rec1[:, b], 127.0, None, ALU.mult))
                step(dve.tensor_tensor(inv1sq[:, b], inv1[:, b], inv1[:, b], ALU.mult))
                step(dve.tensor_scalar(c_v[:, b], inv1[:, b], w_mean[:, 2:3], None, ALU.mult))
                settle()
                dve.tensor_scalar(c_qk[:, b], inv1sq[:, b], w_qk[:], HD ** -0.5, ALU.mult, ALU.mult).then_inc(x_scaled, 1)

            dve.wait_ge(x_rms, 1)
            x_scales(0, TB)

            def center_weights():
                dve.wait_ge(w1_in, 16 * 4)
                step(dve.tensor_tensor(W1_raw[:, :, 0:D - 1], W1_raw[:, :, 0:D - 1],
                                       W1_raw[:, :, D - 1:D].broadcast_to((P, E * FC, D - 1)), ALU.subtract))
                step(dve.tensor_scalar(Wr_raw[:, 0:D - 1], Wr_raw[:, 0:D - 1], Wr_raw[:, D - 1:D], None, ALU.subtract))
                settle()
                step(dve.tensor_copy(Wr_raw[:, D - 1:D], br_col[:]))
                dve.wait_ge(b1_psum, 1)
                dve.tensor_copy(W1_raw[:, :, D - 1], PS[:, 3, 0:E * FC]).then_inc(w_ready, 1)

            def largest_weights():
                dve.wait_ge(w_ready, 1)
                dve.wait_ge(ffn_in, 16 * 4)
                step(dve.tensor_reduce(w_top_abs[:, 0:1], W1_raw[:].rearrange("p a d -> p (a d)"), AX.X, ALU.max,
                                       apply_absolute_value=True))
                step(dve.tensor_reduce(w_top_abs[:, 1:2], W2_raw[:].rearrange("p a d -> p (a d)"), AX.X, ALU.max,
                                       apply_absolute_value=True))
                settle()
                dve.tensor_scalar(w_top_abs[:], w_top_abs[:], 1e-12, None, ALU.max).then_inc(w_abs_ready, 1)

            def weight_scales():
                dve.wait_ge(w_top_ready, 1)
                scale_bits, top_bits = w_scale[:].bitcast(I32), w_top_abs[:].bitcast(I32)
                step(dve.tensor_scalar(top_bits, top_bits, 0xFF << 23, None, ALU.bitwise_and))
                settle()
                for n, target in enumerate((4, 9)):
                    step(dve.tensor_scalar(scale_bits[:, n:n + 1], top_bits[:, n:n + 1], -1.0,
                                           float((254 + target) << 23), ALU.mult, ALU.add))
                settle()
                dve.tensor_scalar(b2_scale[:], w_scale[:, 0:1], w_scale[:, 1:2], X_SCALE, ALU.mult, ALU.mult
                                  ).then_inc(w_scaled, 1)
                dve.wait_ge(w_scaled, 1)
                step(dve.reciprocal(o_scale[:], b2_scale[:]))
                step(dve.tensor_scalar(b2_rep[:], b2_rep[:], b2_scale[0:3 * E, :], None, ALU.mult))
                settle()
                step(dve.tensor_copy(b2_parts[:, 0, :], b2_rep[:]))
                settle()
                step(dve.tensor_tensor(b2_rest[:, 0, :], b2_rep[:], b2_parts[:, 0, :], ALU.subtract))
                settle()
                step(dve.tensor_copy(b2_parts[:, 1, :], b2_rest[:, 0, :]))
                settle()
                step(dve.tensor_tensor(b2_rest[:, 1, :], b2_rest[:, 0, :], b2_parts[:, 1, :], ALU.subtract))
                settle()
                step(dve.tensor_copy(b2_parts[:, 2, :], b2_rest[:, 1, :]))

            def low_weights(g, banks):
                dve.wait_ge(w_high, g + 1)
                for n, (hi, lo) in enumerate(((W1_hi, W1_lo), (W2_hi, W2_lo))):
                    last = dve.scalar_tensor_tensor(lo[:, FC * g:FC * g + FC, :].rearrange("p a d -> p (a d)"),
                                                    PS[:, banks[n], :], w_scale[:, n:n + 1],
                                                    hi[:, FC * g:FC * g + FC, :].rearrange("p a d -> p (a d)"),
                                                    ALU.mult, ALU.subtract)
                    if n == 0:
                        step(last)
                last.then_inc(w_split, 1)

            def norm_stats(z, bn, mv, ve, ready, minus_mean=None):
                for i in range(TB):
                    step(dve.bn_stats(bn[:, i, :], z[:, i, :]))
                settle_apart()
                for i in range(TB):
                    step(dve.bn_aggr(mv[:, i, :], bn[:, i, :]))
                settle()
                if minus_mean is not None:
                    step(dve.tensor_scalar(minus_mean[:], mv[:, :, 0], -1.0, None, ALU.mult))
                dve.tensor_scalar(ve[:], mv[:, :, 1], 1e-5, None, ALU.add).then_inc(ready, 1)

            def norm_apply(o, z, mv, rstd):
                for i in range(TB):
                    last = dve.tensor_scalar(o(i), z[:, i, :], mv[:, i, 0:1], rstd[:, i:i + 1], ALU.subtract, ALU.mult)
                    if i < TB - 1:
                        step(last)
                return last

            def a_turn(u, parity, there):
                first = isinstance(u, int) and u == 0
                for j in range(TB):
                    k = TB * u + j
                    l2, i2 = divmod(j - 2, TB)
                    if there(-l2):
                        after(dve, e1_ready, k - 3)
                        after(dve, qk_prod, k - 1)
                        own = S1[:].rearrange("p (h t) -> p h t", t=H)
                        summed = PS[:, 7, 0:D].rearrange("p (h t) -> p h t", t=H)
                        less = S1d[:, i2 % 2, :].rearrange("p (h t) -> p h t", h=H)
                        step(dve.tensor_reduce(S1[:], prod1[:, i2 % 2, :].rearrange("p (d a) -> p a d", d=HD)[:, D:2 * D, :],
                                               AX.X, ALU.add))
                        settle()
                        step(dve.tensor_reduce(S1m[:, H // 2:H], own, AX.X, ALU.max))
                        after(dve, s_psum, k - 1)
                        step(dve.tensor_reduce(S1m[:, 0:H // 2], summed, AX.X, ALU.max))
                        settle()
                        step(dve.tensor_tensor(less[:, H // 2:H], own, bc(S1m[:, H // 2:H], H), ALU.subtract))
                        dve.tensor_tensor(less[:, 0:H // 2], summed, bc(S1m[:, 0:H // 2], H), ALU.subtract
                                          ).then_inc(s1_ready, 1)
                    if j == 0 and there(0):
                        after(dve, xqT_psum, u)
                        for i in range(TB):
                            step(dve.tensor_scalar(xq_f[:, i, :], X[:, batch(u, i), :], rms1[:, batch(u, i)],
                                                   s1[:, batch(u, i)], ALU.mult, ALU.mult))
                        settle()
                        dve.tensor_scalar(xq[:], xq_f[:], ROUND, -ROUND, ALU.add, ALU.add).then_inc(xq_ready, 1)
                    l1, i1 = divmod(j - 1, TB)
                    if there(-l1):
                        after(dve, qkv_ready, k)
                        step(qk_products(dve, i1, HP, H))
                    if there(-l2):
                        after(dve, e1_ready, k - 1)
                        av_products(dve, i2, HP, H).then_inc(av_share, 1)
                        step(dve.tensor_reduce(E1sum[:, i2 % 2, :], E1[:, i2 % 2, :].rearrange("p (h t) -> p h t", h=H),
                                               AX.X, ALU.add))
                        settle()
                        step(dve.reciprocal(E1inv[:, i2, :], E1sum[:, i2 % 2, :]))
                    l3, i3 = divmod(j - 3, TB)
                    if there(-l3):
                        after(dve, hctx_psum, k - 2)
                        after_dma(dve, shuffled, k - 4)
                        dve.scalar_tensor_tensor(hctx[:, i3 % 2, :].rearrange("p (h d) -> p h d", h=H),
                                                 PS[:, 6, 0:D].rearrange("p (h d) -> p h d", h=H),
                                                 c_v[:, batch(u + l3, i3)], bc(E1inv[:, i3, :], HD),
                                                 ALU.mult, ALU.mult).then_inc(hctx_ready, 1)
                    if first and j == 1:
                        center_weights()
                        largest_weights()
                    if first and j == 2:
                        dve.wait_ge(x_in, 16)
                        step(dve.tensor_reduce(amax1[:, TB:B], X[:, TB:B, :], AX.X, ALU.max, apply_absolute_value=True))
                        dve.wait_ge(x_sq, 2)
                        dve.tensor_scalar(ssq1[:, TB:B], ssq1[:, TB:B], 1.0 / D, 1e-6, ALU.mult, ALU.add).then_inc(x_ms, 1)
                    if first and j == 3:
                        dve.wait_ge(x_rms, 2)
                        x_scales(TB, B)
                        weight_scales()
                    for g, banks in experts_at(u, j):
                        low_weights(g, banks)
                    if j == 3 and there(1):
                        after_dma(dve, y_in, TB * u)
                        step(dve.tensor_reduce(amax2[:], Y[:, tile(u - 1), :], AX.X, ALU.max, apply_absolute_value=True))
                        after(dve, ysq_ready, u)
                        dve.tensor_scalar(ms2[:], ssq2[:], 1.0 / D, 1e-6, ALU.mult, ALU.add).then_inc(ms2_ready, 1)
                    if j == 0 and there(2):
                        after(dve, rms2_ready, u - 1)
                        step(dve.tensor_tensor(clip2[:], amax2[:], rms2[:], ALU.mult))
                        settle()
                        step(dve.tensor_scalar(clip2[:], clip2[:], 1e-5, None, ALU.max))
                        settle()
                        step(dve.reciprocal(rec2[:], clip2[:]))
                        step(dve.tensor_scalar(f2[:], clip2[:], 1.0 / 127, w_mean[:, 3:4], ALU.mult, ALU.mult))
                        settle()
                        dve.tensor_scalar(s2[:], rec2[:], 127.0, None, ALU.mult).then_inc(s2_ready, 1)
                    if j == 1 and there(2):
                        after(dve, yq_f_ready, u - 1)
                        after(dve, yqT_psum, u - 2)
                        dve.tensor_scalar(yq[:], yq_f[:], ROUND, -ROUND, ALU.add, ALU.add).then_inc(yq_ready, 1)
                    if j == 2 and there(2):
                        after(dve, wo_psum, u - 1)
                        after(dve, x1_ready, u - 2)
                        for i in range(TB):
                            last = dve.scalar_tensor_tensor(z1[:, i, :], PS[:, 4, i * D:(i + 1) * D], f2[:, i:i + 1],
                                                            X[:, batch(u - 2, i), :], ALU.mult, ALU.add)
                            if i < TB - 1:
                                step(last)
                        last.then_inc(z1_ready, 1)
                        after(dve, z1_ready, u - 1)
                        norm_stats(z1, bn1, mv1, ve1, ve1_ready, minus_mean1)

            turns(dve, 2, a_turn, ch, A_STEPS)

            def second_stats(u):
                after(dve, att_ready, TB * (u - 1))
                after(dve, x1_ready, u - 1)
                step(dve.tensor_tensor(z2[:], att2[:], X[:, tile(u - 2), :], ALU.add))
                settle()
                norm_stats(z2, bn2, mv2, ve2, ve2_ready)

            def second_norm(u):
                after(dve, rstd2_ready, u - 1)
                norm_apply(lambda i: X[:, batch(u - 2, i), :], z2, mv2, rstd2).then_inc(x2_ready, 1)

            def b_turn(u, parity, there):
                for j in range(TB):
                    k = TB * u + j - 1

                    def half_max(a):
                        if there(-((j - 3) // TB)):
                            after(dve, score_psum, 2 * (k - 2) + a + 1)
                            dve.tensor_reduce(half_heads(m2[:], a), banks(a).rearrange("p r (g t) -> p r g t", t=P),
                                              AX.X, ALU.max).then_inc(max_done, 1)

                    half_max(0)
                    l, i = divmod(j - 1, TB)
                    if there(-l):
                        after(dve, proj_psum, k + 1)
                        after(dve, v_ready, k - 7)
                        after(dve, split_ready, k - 1)
                        p = PS[:, 6, 0:3 * D].rearrange("p (a d) -> p a d", a=3)
                        step(dve.tensor_tensor(Va[:, (TB * parity + j - 1) % 8], p[:, 2], b_qkv[:, 2], ALU.add))
                        dve.tensor_tensor(qk_f[:, i % 2], p[:, 0:2], b_qkv[:, 0:2], ALU.add).then_inc(qkv_copied, 1)
                    l, i = divmod(j - 7, TB)
                    if there(-l):
                        after(dve, out_psum, k - 5)
                        o = PS[:, 7, 0:H * (HD + 1)].rearrange("p (h d) -> p h d", h=H)
                        step(dve.tensor_scalar(sum2[:], o[:, :, HD], 1e-30, None, ALU.max))
                        settle()
                        step(dve.reciprocal(rsum2[:], sum2[:]))
                        settle()
                        dve.tensor_tensor(att2[:, i, :].rearrange("p (h d) -> p h d", h=H), o[:, :, 0:HD],
                                          bc(rsum2[:], HD), ALU.mult).then_inc(att_ready, 1)
                    half_max(1)
                    l, i = divmod(j - 2, TB)
                    if there(-l):
                        after(dve, kT_psum, k)
                        after(dve, scoreT_psum, 2 * (k - 4))
                        dve.tensor_copy(KT[:, i].rearrange("p a d -> p (a d)"), PS[:, 5, :].bitcast(BF16)
                                        ).then_inc(kT_ready, 1)
                    l, i = divmod(j - 3, TB)
                    if there(-l):
                        after(dve, max_done, 2 * (k - 1))
                        parts3 = QK[:, i, 0, :, 6 * HD + 1:6 * HD + 4]
                        step(dve.tensor_scalar(m_neg[:], m2[:], -1.0, -0.1 * NEG, ALU.mult, ALU.min))
                        settle()
                        step(dve.tensor_copy(parts3[:, :, 0], m_neg[:]))
                        settle()
                        step(dve.tensor_tensor(m_rest[:, 0], m_neg[:], parts3[:, :, 0], ALU.subtract))
                        settle()
                        step(dve.tensor_copy(parts3[:, :, 1], m_rest[:, 0]))
                        settle()
                        dve.tensor_tensor(parts3[:, :, 2], m_rest[:, 0], parts3[:, :, 1], ALU.subtract
                                          ).then_inc(m_ready, 1)
                    if there(2) and not (isinstance(u, int) and u == T + 1):
                        if j == 2:
                            second_stats(u)
                        if j == 3:
                            second_norm(u)

            turns(dve, 2, b_turn, ch, B_STEPS)

            after(dve, x2_ready, T - 1)
            gb = gam[:].unsqueeze(1).broadcast_to((P, TB, D))
            be = bet[:].unsqueeze(1).broadcast_to((P, TB, D))

            def c_turn(u, parity, there):
                for n in range(NC):
                    if there(1):
                        after(dve, h_hi_ready, NC * (u - 1) + n + 1)
                        dve.scalar_tensor_tensor(h_lo[:, n % 4, :], PS[:, n % 4, :], 0.0, h_hi[:, n % 4, :],
                                                 ALU.max, ALU.subtract).then_inc(h_lo_ready, 1)
                    if n % FC == 1:
                        lag, e = prepared(n // FC)
                        if there(lag):
                            i = E * (u - lag) + e
                            after(dve, rwb_psum, i + 1)
                            after(dve, xsplit_ready, i - 1)
                            dve.tensor_tensor(xe[:, e % 2, :], xaT[:, (parity - lag) % 2, :], PS[:, 6, :],
                                              ALU.mult).then_inc(xe_ready, 1)
                    if n == 0 and there(0):
                        after(dve, xaT_psum, u)
                        dve.tensor_copy(xa[:, :, 0:D - 1], X[:, tile(u), 0:D - 1]).then_inc(xa_ready, 1)
                    if n == 14 and there(0):
                        after(dve, lg_psum, u + 1)
                        step(dve.tensor_copy(lg[:].rearrange("p a e -> p (a e)"), PS[:, 7, 0:TB * E]))
                        settle_apart()
                        for i in range(TB):
                            step(dve.max(top[:, i, :], lg[:, i, :]))
                        settle()
                        dve.tensor_tensor(gap[:], top[:, :, 1], top[:, :, 0], ALU.subtract).then_inc(gap_ready, 1)
                    if n == 15 and there(0):
                        for i in range(TB):
                            step(dve.max_index(topi[:, i, :], top[:, i, :], lg[:, i, :]))
                        settle()
                        step(dve.tensor_copy(topf[:], topi[:]))
                        settle()
                        for a in range(2):
                            step(dve.tensor_tensor(oh[:, a], eiota[:], topf[:, :, a:a + 1].broadcast_to((P, TB, E)),
                                                   ALU.is_equal))
                    if n == 18 and there(0):
                        after(dve, eg_ready, u + 1)
                        step(dve.tensor_scalar(eg1[:], eg[:], 1.0, None, ALU.add))
                        settle()
                        step(dve.reciprocal(w_top[:, 0, :], eg1[:]))
                        settle()
                        step(dve.tensor_tensor(w_top[:, 1, :], eg[:], w_top[:, 0, :], ALU.mult))
                        step(dve.tensor_tensor(oh[:, 0], oh[:, 0], bc(w_top[:, 0, :], E), ALU.mult))
                        settle()
                        step(dve.tensor_tensor(oh[:, 1], oh[:, 1], bc(w_top[:, 1, :], E), ALU.mult))
                        settle()
                        step(dve.tensor_tensor(rw[:], oh[:, 0], oh[:, 1], ALU.add))
                        settle()
                    if n == 19 and there(0):
                        step(dve.tensor_copy(rw16[:, :, 0, :], rw[:]))
                        settle()
                        step(dve.tensor_tensor(rw_rest[:, 0], rw[:], rw16[:, :, 0, :], ALU.subtract))
                        settle()
                        step(dve.tensor_copy(rw16[:, :, 1, :], rw_rest[:, 0]))
                        settle()
                        step(dve.tensor_tensor(rw_rest[:, 1], rw_rest[:, 0], rw16[:, :, 1, :], ALU.subtract))
                        settle()
                        dve.tensor_copy(rw16[:, :, 2, :], rw_rest[:, 1]).then_inc(rw_ready, 1)
                    if n == 6 and there(2):
                        after(dve, y3_psum, u - 1)
                        dve.tensor_tensor(z3[:], PS[:, 7, :].rearrange("p (a d) -> p a d", a=TB), X[:, tile(u - 2), :],
                                          ALU.add).then_inc(z3_ready, 1)
                        after(dve, z3_ready, u - 1)
                        norm_stats(z3, bn3, mv3, ve3, ve3_ready)
                    if n == 10 and there(2):
                        after(dve, rstd3_ready, u - 1)
                        step(norm_apply(lambda i: n3[:, i, :], z3, mv3, rstd3))
                        settle()
                    if n == 11 and there(2):
                        step(dve.tensor_tensor(g3[:], n3[:], gb, ALU.mult))
                        settle()
                    if n == 12 and there(2):
                        step(dve.tensor_tensor(n3[:], g3[:], be, ALU.add))
                        settle()
                    if n == 13 and there(2):
                        step(dve.tensor_tensor(z4[:], n3[:], X[:, tile(u - 2), :], ALU.add))
                        settle()
                        norm_stats(z4, bn4, mv4, ve4, ve4_ready)
                    if n == 17 and there(2):
                        after(dve, rstd4_ready, u - 1)
                        after_dma(dve, stored, u - 2)
                        norm_apply(lambda i: o4[:, i, :], z4, mv4, rstd4).then_inc(o4_ready, 1)

                if isinstance(u, int) and u == 0:
                    second_stats(T + 1)
                    second_norm(T + 1)

            turns(dve, 2, c_turn, ch, C_STEPS)


_INS = ["x", "ctx_1024", "mask_BxS2_bf0", "L0_attn_wq", "L0_attn_wk", "L0_attn_wv", "L0_attn_wo",
        "L0_xattn_Wq", "L0_xattn_bq", "L0_xattn_Wk", "L0_xattn_bk", "L0_xattn_Wv", "L0_xattn_bv",
        "L0_ffn_Wr", "L0_ffn_br", "L0_ffn_W1", "L0_ffn_b1", "L0_ffn_W2", "L0_ffn_b2", "L0_ffn_gamma", "L0_ffn_beta"]


def kernel(**inputs):
    import numpy as _np
    import concourse.bacc as _bacc
    from concourse import mybir as _mybir
    from concourse.bass_utils import run_bass_kernel_spmd as _run

    nc = _bacc.Bacc("TRN2", target_bir_lowering=False, num_devices=1)
    arrays, args = {}, []
    for name in _INS:
        a = _np.ascontiguousarray(inputs[name])
        arrays[f"in_{name}_dram"] = a
        args.append(nc.dram_tensor(f"in_{name}_dram", a.shape, _mybir.dt.from_np(a.dtype), kind="ExternalInput").ap())
    args.append(nc.dram_tensor("out_dram", inputs["x"].shape, _mybir.dt.float32, kind="ExternalOutput").ap())
    decoder_layer(nc, *args)
    r = _run(nc, [arrays], core_ids=[0])
    return r.results[0]["out_dram"]
```
